# Optimizing a Trainium2 kernel written in Bass

```python
import numpy as np
import jax
import jax.numpy as jnp

def _softmax(x, axis=-1):
    return jax.nn.softmax(x, axis=axis)

def _gelu(x):
    return jax.nn.gelu(x, approximate=True)

def _silu(x):
    return jax.nn.silu(x)

def _sigmoid(x):
    return jax.nn.sigmoid(x)

def _layernorm(x, axis=-1, eps=1e-05):
    m = jnp.mean(x, axis=axis, keepdims=True)
    v = jnp.var(x, axis=axis, keepdims=True)
    return (x - m) / jnp.sqrt(v + eps)

def _scatter_add(tgt, idx, src, axis=0):
    return tgt.at[idx].add(src)

def _segment_sum(src, seg, n):
    return jax.ops.segment_sum(src, seg, n)
kernel_name = 'mk_vit_tower_d2_tok_img768_r4_74bfb1'

def setup_inputs(seed: int=0):
    np.random.seed(seed)
    _w = jnp.asarray

    def _rec_inputs():
        import jax
        import jax.numpy as jnp
        _rk = jax.random.key(seed)
        x = -0.000356955 + 1 * jax.random.normal(jax.random.fold_in(_rk, 1), (64, 3, 224, 224), jnp.float32)
        return x
    x = _rec_inputs()

    def _L0_tok_setup():
        import jax, jax.numpy as jnp
        import numpy as np
        C, H, W_IMG = (3, 224, 224)
        NP = 14
        PS = H // NP
        D_IN = C * PS * PS
        D = 192
        SEQ = NP * NP + 1
        B = 128

        def _sinusoidal_pos_embed(seq_len, d):
            i = np.arange(seq_len, dtype=np.float64)[:, None]
            j = np.arange(d, dtype=np.float64)[None, :]
            angle = i / np.power(10000.0, (j - j % 2) / d)
            pe = np.where(j % 2 == 0, np.sin(angle), np.cos(angle))
            return jnp.asarray(pe, dtype=jnp.float32)
        key = jax.random.key(seed)
        kx, kw, kc = jax.random.split(key, 3)
        x = jax.random.normal(kx, (B, C, H, W_IMG), dtype=jnp.float32)
        W = jax.random.normal(kw, (D, D_IN), dtype=jnp.float32) * 0.02
        b = jnp.zeros((D,), dtype=jnp.float32)
        class_token = jax.random.uniform(kc, (1, D), dtype=jnp.float32)
        pos_embed = _sinusoidal_pos_embed(SEQ, D)
        return {'x': x, 'W': W, 'b': b, 'class_token': class_token, 'pos_embed': pos_embed}
    _L0_tok_all = _L0_tok_setup()
    _L0_tok_in = {k: v for k, v in _L0_tok_all.items() if k in ('W', 'b', 'class_token', 'pos_embed')}
    del _L0_tok_all

    def _L0_attn_setup():
        import jax, jax.numpy as jnp
        import numpy as np
        B, S, D, OUT = (8, 512, 192, 192)
        key = jax.random.key(seed)
        kx, kw = jax.random.split(key)
        x = jax.random.normal(kx, (B, S, D), dtype=jnp.float32)
        W = jax.random.normal(kw, (3, D, OUT), dtype=jnp.float32) * (2.0 / (D + OUT)) ** 0.5
        return {'x': x, 'W': W}
    _L0_attn_all = _L0_attn_setup()
    _L0_attn_in = {k: v for k, v in _L0_attn_all.items() if k in ('W',)}
    del _L0_attn_all

    def _L0_ffn_setup():
        import jax, jax.numpy as jnp
        import numpy as np
        B, T, H, F, E = (128, 32, 192, 768, 3)
        key = jax.random.key(seed)
        ks = jax.random.split(key, 4)
        s = 0.02
        return {'x': jax.random.normal(ks[0], (B, T, H), jnp.float32), 'Wg': jax.random.normal(ks[1], (E, H), jnp.float32) * s, 'W1': jax.random.normal(ks[2], (E, H, F), jnp.float32) * s, 'b1': jnp.zeros((E, F), jnp.float32), 'W2': jax.random.normal(ks[3], (E, F, H), jnp.float32) * s, 'b2': jnp.zeros((E, H), jnp.float32)}
    _L0_ffn_all = _L0_ffn_setup()
    _L0_ffn_in = {k: v for k, v in _L0_ffn_all.items() if k in ('Wg', 'W1', 'b1', 'W2', 'b2')}
    del _L0_ffn_all

    def _L1_attn_setup():
        import jax, jax.numpy as jnp
        import numpy as np
        DIM = 192
        NUM_HEADS = 12
        HEAD_DIM = DIM // NUM_HEADS
        SCALE = HEAD_DIM ** (-0.5)
        key = jax.random.key(seed)
        k_x, k_qkv, k_proj = jax.random.split(key, 3)
        B, N, C = (16, 256, DIM)
        x = jax.random.normal(k_x, (B, N, C), dtype=jnp.float32)
        w_qkv = jax.random.truncated_normal(k_qkv, -2.0, 2.0, (3 * C, C), dtype=jnp.float32) * 0.02
        w_proj = jax.random.truncated_normal(k_proj, -2.0, 2.0, (C, C), dtype=jnp.float32) * 0.02
        b_proj = jnp.zeros((C,), dtype=jnp.float32)
        return {'x': x, 'w_qkv': w_qkv, 'w_proj': w_proj, 'b_proj': b_proj}
    _L1_attn_all = _L1_attn_setup()
    _L1_attn_in = {k: v for k, v in _L1_attn_all.items() if k in ('w_qkv', 'w_proj', 'b_proj')}
    del _L1_attn_all

    def _L1_ffn_setup():
        import jax, jax.numpy as jnp
        import numpy as np
        ATOM = {'vm': 0, 'im': 1, 'cm': 2, 'sc': 3, 'cc': 4}
        TASK_PAIRS = [('vm', 'sc'), ('vm', 'cc'), ('im', 'sc'), ('im', 'cc'), ('cm', 'sc'), ('cm', 'cc')]
        SRC_IDX = np.array([[ATOM[l], ATOM[r]] for l, r in TASK_PAIRS], dtype=np.int32)
        DST_IDX = np.array([[ATOM[r], ATOM[l]] for l, r in TASK_PAIRS], dtype=np.int32)
        NCLS = 6
        NATOMS = 5

        def _l2norm(x, eps=1e-12):
            return x / jnp.clip(jnp.linalg.norm(x, axis=-1, keepdims=True), eps)
        key = jax.random.key(seed)
        ks = jax.random.split(key, 12)
        B, NPATCH, D, H = (64, 197, 192, 768)
        std = 0.02
        x = jax.random.normal(ks[0], (B, NCLS + NPATCH, D), dtype=jnp.float32)
        fc1_w = jax.random.normal(ks[1], (H, D), dtype=jnp.float32) * std
        fc1_b = jnp.zeros((H,), jnp.float32)
        fc2_w = jax.random.normal(ks[2], (D, H), dtype=jnp.float32) * std
        fc2_b = jnp.zeros((D,), jnp.float32)
        gate_pair = jax.random.normal(ks[3], (NCLS, 2, D), dtype=jnp.float32) * std
        atom_in_w = jax.random.normal(ks[4], (NATOMS, H, D), dtype=jnp.float32) * std
        atom_in_b = jax.random.normal(ks[5], (NATOMS, H), dtype=jnp.float32) * std
        atom_out_w = jax.random.normal(ks[6], (NATOMS, D, H), dtype=jnp.float32) * std
        atom_out_b = jax.random.normal(ks[7], (NATOMS, D), dtype=jnp.float32) * std
        balance_bias = jnp.zeros((NCLS, 2), jnp.float32)
        return {'x': x, 'fc1_w': fc1_w, 'fc1_b': fc1_b, 'fc2_w': fc2_w, 'fc2_b': fc2_b, 'gate_pair': gate_pair, 'atom_in_w': atom_in_w, 'atom_in_b': atom_in_b, 'atom_out_w': atom_out_w, 'atom_out_b': atom_out_b, 'balance_bias': balance_bias}
    _L1_ffn_all = _L1_ffn_setup()
    _L1_ffn_in = {k: v for k, v in _L1_ffn_all.items() if k in ('fc1_w', 'fc1_b', 'fc2_w', 'fc2_b', 'gate_pair', 'atom_in_w', 'atom_in_b', 'atom_out_w', 'atom_out_b', 'balance_bias')}
    del _L1_ffn_all
    return {'x': x, 'L0_tok_W': _L0_tok_in['W'], 'L0_tok_b': _L0_tok_in['b'], 'L0_tok_class_token': _L0_tok_in['class_token'], 'L0_tok_pos_embed': _L0_tok_in['pos_embed'], 'L0_attn_W': _L0_attn_in['W'], 'L0_ffn_Wg': _L0_ffn_in['Wg'], 'L0_ffn_W1': _L0_ffn_in['W1'], 'L0_ffn_b1': _L0_ffn_in['b1'], 'L0_ffn_W2': _L0_ffn_in['W2'], 'L0_ffn_b2': _L0_ffn_in['b2'], 'L1_attn_w_qkv': _L1_attn_in['w_qkv'], 'L1_attn_w_proj': _L1_attn_in['w_proj'], 'L1_attn_b_proj': _L1_attn_in['b_proj'], 'L1_ffn_fc1_w': _L1_ffn_in['fc1_w'], 'L1_ffn_fc1_b': _L1_ffn_in['fc1_b'], 'L1_ffn_fc2_w': _L1_ffn_in['fc2_w'], 'L1_ffn_fc2_b': _L1_ffn_in['fc2_b'], 'L1_ffn_gate_pair': _L1_ffn_in['gate_pair'], 'L1_ffn_atom_in_w': _L1_ffn_in['atom_in_w'], 'L1_ffn_atom_in_b': _L1_ffn_in['atom_in_b'], 'L1_ffn_atom_out_w': _L1_ffn_in['atom_out_w'], 'L1_ffn_atom_out_b': _L1_ffn_in['atom_out_b'], 'L1_ffn_balance_bias': _L1_ffn_in['balance_bias']}

def reference(x, L0_tok_W, L0_tok_b, L0_tok_class_token, L0_tok_pos_embed, L0_attn_W, L0_ffn_Wg, L0_ffn_W1, L0_ffn_b1, L0_ffn_W2, L0_ffn_b2, L1_attn_w_qkv, L1_attn_w_proj, L1_attn_b_proj, L1_ffn_fc1_w, L1_ffn_fc1_b, L1_ffn_fc2_w, L1_ffn_fc2_b, L1_ffn_gate_pair, L1_ffn_atom_in_w, L1_ffn_atom_in_b, L1_ffn_atom_out_w, L1_ffn_atom_out_b, L1_ffn_balance_bias):
    import jax
    import jax.numpy as jnp

    def _L0_tok_ref(x, W, b, class_token, pos_embed):
        import jax, jax.numpy as jnp
        import numpy as np
        C, H, W_IMG = (3, 224, 224)
        NP = 14
        PS = H // NP
        D_IN = C * PS * PS
        D = 192
        SEQ = NP * NP + 1
        B = 128

        def _sinusoidal_pos_embed(seq_len, d):
            i = np.arange(seq_len, dtype=np.float64)[:, None]
            j = np.arange(d, dtype=np.float64)[None, :]
            angle = i / np.power(10000.0, (j - j % 2) / d)
            pe = np.where(j % 2 == 0, np.sin(angle), np.cos(angle))
            return jnp.asarray(pe, dtype=jnp.float32)
        n = x.shape[0]
        p = x.reshape(n, C, NP, PS, NP, PS)
        p = p.transpose(0, 2, 4, 1, 3, 5).reshape(n, NP * NP, D_IN)
        tokens = jnp.einsum('npd,hd->nph', p, W) + b
        cls = jnp.broadcast_to(class_token[None], (n, 1, D))
        tokens = jnp.concatenate([cls, tokens], axis=1)
        return tokens + pos_embed[None]

    def _L0_attn_ref(x, W):
        import jax, jax.numpy as jnp
        import numpy as np
        B, S, D, OUT = (8, 512, 192, 192)
        q = jnp.einsum('bsd,do->bso', x, W[0])
        k = jnp.einsum('bsd,do->bso', x, W[1])
        v = jnp.einsum('bsd,do->bso', x, W[2])
        scale = 1.0 / W.shape[-1] ** 0.5
        e = jnp.einsum('bqo,bko->bqk', q, k) * scale
        a = jax.nn.softmax(e, axis=-1)
        o = jnp.einsum('bqk,bko->bqo', a, v)
        return o

    def _L0_ffn_ref(x, Wg, W1, b1, W2, b2):
        import jax, jax.numpy as jnp
        import numpy as np
        B, T, H, F, E = (128, 32, 192, 768, 3)
        scores = jax.nn.softmax(jnp.mean(x, axis=1) @ Wg.T, axis=-1)
        _, idx = jax.lax.top_k(scores, 1)
        sel = idx[:, 0]
        h = jax.nn.gelu(jnp.einsum('bth,ehf->betf', x, W1) + b1[None, :, None, :], approximate=False)
        y = jnp.einsum('betf,efh->beth', h, W2) + b2[None, :, None, :]
        w = scores * jax.nn.one_hot(sel, E, dtype=scores.dtype)
        out = jnp.einsum('beth,be->bth', y, w)
        return out

    def _L1_attn_ref(x, w_qkv, w_proj, b_proj):
        import jax, jax.numpy as jnp
        import numpy as np
        DIM = 192
        NUM_HEADS = 12
        HEAD_DIM = DIM // NUM_HEADS
        SCALE = HEAD_DIM ** (-0.5)
        B, N, C = x.shape
        H, D = (NUM_HEADS, HEAD_DIM)
        qkv = jnp.einsum('bnc,ec->bne', x, w_qkv)
        qkv = qkv.reshape(B, N, 3, H, D).transpose(2, 0, 3, 1, 4)
        q, k, v = (qkv[0], qkv[1], qkv[2])
        attn = jnp.einsum('bhid,bhjd->bhij', q, k) * SCALE
        attn = jax.nn.softmax(attn, axis=-1)
        out = jnp.einsum('bhij,bhjd->bhid', attn, v)
        out = out.transpose(0, 2, 1, 3).reshape(B, N, C)
        out = jnp.einsum('bnc,oc->bno', out, w_proj) + b_proj
        return out

    def _L1_ffn_ref(x, fc1_w, fc1_b, fc2_w, fc2_b, gate_pair, atom_in_w, atom_in_b, atom_out_w, atom_out_b, balance_bias):
        import jax, jax.numpy as jnp
        import numpy as np
        ATOM = {'vm': 0, 'im': 1, 'cm': 2, 'sc': 3, 'cc': 4}
        TASK_PAIRS = [('vm', 'sc'), ('vm', 'cc'), ('im', 'sc'), ('im', 'cc'), ('cm', 'sc'), ('cm', 'cc')]
        SRC_IDX = np.array([[ATOM[l], ATOM[r]] for l, r in TASK_PAIRS], dtype=np.int32)
        DST_IDX = np.array([[ATOM[r], ATOM[l]] for l, r in TASK_PAIRS], dtype=np.int32)
        NCLS = 6
        NATOMS = 5

        def _l2norm(x, eps=1e-12):
            return x / jnp.clip(jnp.linalg.norm(x, axis=-1, keepdims=True), eps)
        src = jnp.asarray(SRC_IDX)
        dst = jnp.asarray(DST_IDX)
        D = x.shape[-1]
        H = atom_in_w.shape[1]
        cls_tokens = x[:, :NCLS]
        patch_tokens = x[:, NCLS:]
        patch_out = jax.nn.gelu(patch_tokens @ fc1_w.T + fc1_b, approximate=False) @ fc2_w.T + fc2_b
        gate_in = _l2norm(cls_tokens.astype(jnp.float32))
        gate_w = _l2norm(gate_pair.astype(jnp.float32))
        gate_logits = jnp.einsum('bnd,nrd->bnr', gate_in, gate_w) + balance_bias[None]
        route_probs = jax.nn.softmax(gate_logits, axis=-1)
        chosen_route = jnp.argmax(route_probs, axis=-1)
        hid_all = jax.nn.gelu(jnp.einsum('bnd,ahd->bnah', cls_tokens, atom_in_w) + atom_in_b[None, None], approximate=False)
        sh_pair = hid_all[:, jnp.arange(NCLS)[:, None], src, :]
        route_out_w = atom_out_w[dst.reshape(-1)].reshape(NCLS, 2, D, H)
        route_candidates = jnp.einsum('bnrh,nrdh->bnrd', sh_pair, route_out_w) + atom_out_b[dst][None]
        chosen_w = jnp.take_along_axis(route_probs, chosen_route[..., None], axis=-1)
        chosen_cand = jnp.take_along_axis(route_candidates, chosen_route[:, :, None, None], axis=2)[:, :, 0]
        cls_out = chosen_cand * chosen_w.astype(chosen_cand.dtype)
        return jnp.concatenate([cls_out, patch_out], axis=1)
    h = _L0_tok_ref(x, L0_tok_W, L0_tok_b, L0_tok_class_token, L0_tok_pos_embed)
    h = h + _L0_attn_ref(_layernorm(h, axis=-1), L0_attn_W)
    h = h + _L0_ffn_ref(_layernorm(h, axis=-1), L0_ffn_Wg, L0_ffn_W1, L0_ffn_b1, L0_ffn_W2, L0_ffn_b2)
    h = h + _L1_attn_ref(_layernorm(h, axis=-1), L1_attn_w_qkv, L1_attn_w_proj, L1_attn_b_proj)
    h = h + _L1_ffn_ref(_layernorm(h, axis=-1), L1_ffn_fc1_w, L1_ffn_fc1_b, L1_ffn_fc2_w, L1_ffn_fc2_b, L1_ffn_gate_pair, L1_ffn_atom_in_w, L1_ffn_atom_in_b, L1_ffn_atom_out_w, L1_ffn_atom_out_b, L1_ffn_balance_bias)
    return h

_drawn_inputs = setup_inputs


def setup_inputs(seed=0):
    import zlib

    import numpy as np

    out = dict(_drawn_inputs(seed))
    spreads = {'L0_tok_b': (0.0, 0.1),
     'L0_ffn_b1': (0.0, 0.587),
     'L0_ffn_b2': (0.0, 0.1),
     'L1_attn_b_proj': (0.0, 0.1),
     'L1_ffn_fc1_b': (0.0, 0.292),
     'L1_ffn_fc2_b': (0.0, 0.1),
     'L1_ffn_balance_bias': (0.0, 0.8)}
    factors = {'L0_tok_class_token': 2.806,
     'L1_ffn_gate_pair': 8.0,
     'L1_ffn_atom_in_w': 7.854,
     'L1_ffn_atom_in_b': 8.0,
     'L1_ffn_atom_out_w': 7.621,
     'L1_ffn_atom_out_b': 31.693}
    for name, (base, spread) in spreads.items():
        noise = np.random.default_rng([zlib.crc32(name.encode()), seed]).standard_normal(out[name].shape)
        drawn = base * np.exp(spread * noise) if base else spread * noise
        out[name] = jnp.asarray(drawn.astype(out[name].dtype))
    for name, factor in factors.items():
        out[name] = (out[name] * factor).astype(out[name].dtype)
    return out
```

```python
from contextlib import ExitStack

import concourse.bass as bass
from concourse import mybir

F32 = mybir.dt.float32
I32 = mybir.dt.int32
ALU = mybir.AluOpType
ACT = mybir.ActivationFunctionType
AX = mybir.AxisListType.X

IMAGES, CHANNELS, SIDE = 64, 3, 224
GRID = 14
PS = SIDE // GRID
D = 192
F = 768
SEQ = GRID * GRID + 1
R = 99
T = 2
SP_ = R * T
KC = 96
NK = D // KC
HC = F // 128
TOKK = CHANNELS * PS * PS // 128
HEADS, HD = 12, 16
GROUPS = HEADS // 4
EXPERTS = 3
NCLS, ATOMS = 6, 5
EPS = 1e-5
PAIRS = IMAGES // 2
XROWS = 2 * CHANNELS * GRID
PX = [(0, 5), (5, 10), (10, 14)]

STAGES = (["tok", "ln1", "q0", "s0", "p0", "o0", "ln2", "route", "hid0", "out0", "ln3", "qkv"]
          + [("head", s) for s in range(HEADS + 3)] + ["proj", "ln4", "hid1", "out1"])


def merged_order(lag):
    n = len(STAGES)
    order = [("x", 0, 0)]
    for k in range(n):
        order.append((STAGES[k], 0, 0))
        j = (k - lag) % n
        order.append((STAGES[j], 1, 0 if k >= lag else 1))
    return order


LAG = 15
ORDER = merged_order(LAG)


def vit_kernel(nc, x, tok_w, tok_b, cls_tok, pos, attn_w, wg, w1, b1, w2, b2, w_qkv, w_proj, b_proj,
               fc1_w, fc1_b, fc2_w, fc2_b, gate_pair, atom_in_w, atom_in_b, atom_out_w, atom_out_b,
               balance, out, scratch):
    with ExitStack() as ctx:
        def sb(name, shape, dt=F32, stack=ctx):
            return stack.enter_context(nc.sbuf_tensor(name, shape, dt))

        def sem(name):
            return ctx.enter_context(nc.semaphore(name))

        def both(name):
            return [sem(f"{name}_{p}") for p in range(2)]

        ident = sb("ident", [128, 128])
        ones = sb("ones", [1, 128])
        not_cls = sb("not_cls", [R, 1])
        minus_half = sb("minus_half", [128, T])
        eps = sb("eps", [128, T])
        pos_b = sb("pos_b", [R, T, D])
        tok_wT = sb("tok_wT", [128, TOKK, D])
        qk_fold = sb("qk_fold", [KC, NK, D])
        attn_wv = sb("attn_wv", [KC, NK, D])
        wgT = sb("wgT", [KC, NK, EXPERTS])
        qk_wT = sb("qk_wT", [KC, NK, 2 * HEADS * 32])
        v_wT = sb("v_wT", [KC, NK, D])
        proj_wT = sb("proj_wT", [128, GROUPS, D])
        proj_brow = sb("proj_brow", [1, D])
        fc1_wT = sb("fc1_wT", [KC, NK, HC, 128])
        fc1_bc = sb("fc1_bc", [128, HC])
        fc2_wT = sb("fc2_wT", [128, HC, D])
        fc2_brow = sb("fc2_brow", [1, D])
        atom_brow = sb("atom_brow", [1, ATOMS, D])
        atom_bc = sb("atom_bc", [128, ATOMS, HC])

        with ExitStack() as early:
            tok_n = sb("tok_n", [KC, NK, F], stack=early)
            attn_n = sb("attn_n", [KC, 2, NK, D], stack=early)
            qkT = sb("qkT", [KC, 2, NK, D], stack=early)
            qkv_n = sb("qkv_n", [KC, 6, D], stack=early)
            proj_n = sb("proj_n", [KC, NK, HEADS, 32], stack=early)
            fc1_n = sb("fc1_n", [128, HC, D], stack=early)
            fc2_n = sb("fc2_n", [KC, NK, F], stack=early)
            wg_n = sb("wg_n", [EXPERTS, D], stack=early)
            row_add = sb("row_add", [R, T, D], stack=early)
        atom_in_n = [sb(f"atom_in_n{a}", [128, HC, D]) for a in range(ATOMS)]
        atom_out_n = [sb(f"atom_out_n{a}", [KC, NK, F]) for a in range(ATOMS)]

        with ExitStack() as loop:
            def two(name, shape, dt=F32):
                return [sb(f"{name}{p}", shape, dt, loop) for p in range(2)]

            xin = sb("xin", [XROWS, PS, SIDE], stack=loop)
            xg = sb("xg", [XROWS, GRID, PS * PS], stack=loop)
            xT = sb("xT", [128, 2 * XROWS * GRID + 4], stack=loop)
            hx = two("hx", [R, 2, T, D])
            stats = two("stats", [R, T, 6])
            moments = two("moments", [R, T, 2])
            var_eps = two("var_eps", [R, T])
            rstd = two("rstd", [R, T])
            xnT = two("xnT", [KC, NK, SP_])
            gT = two("gT", [KC, NK, SP_])
            vals = two("vals", [R, T, D + 16])
            nmax0 = two("nmax0", [R, T])
            sum0 = two("sum0", [R, T])
            inv0 = two("inv0", [R, T])
            turned = two("turned", [R, 2, T, SP_])
            xsum = two("xsum", [KC, NK])
            logit = two("logit", [R, EXPERTS])
            nlmax = two("nlmax", [R, 1])
            lexp = two("lexp", [R, EXPERTS])
            lsum = two("lsum", [R, 1])
            linv = two("linv", [R, 1])
            ltop = two("ltop", [R, 1])
            weight = two("weight", [R, 1])
            below = two("below", [R, 2])
            expert = two("expert", [1, 1], I32)
            w1_sb = two("w1_sb", [KC, NK, F])
            w2_sb = two("w2_sb", [128, HC, D])
            b1_sb = two("b1_sb", [128, HC])
            b2_sb = two("b2_sb", [1, D])
            hidT = two("hidT", [128, HC, SP_])
            qkh = two("qkh", [128, 2 * GROUPS, SP_])
            nmax1 = two("nmax1", [R, HEADS, T])
            sum1 = two("sum1", [R, HEADS, T])
            inv1 = two("inv1", [R, HEADS, T])
            probs1 = two("probs1", [R, 3, T, SP_])
            probs0 = [probs1[p][:, 0, :, :] for p in range(2)]
            headT = two("headT", [128, GROUPS, SP_])
            y = two("y", [R, T, D])
        cls = sb("cls", [IMAGES, NCLS, 2, D])
        clsT = sb("clsT", [KC, NK, NCLS, IMAGES])
        gate = sb("gate", [IMAGES, 2 * NCLS, D])
        gbias = sb("gbias", [IMAGES, 2 * NCLS])
        prod = sb("prod", [IMAGES, 2 * NCLS, D])
        sumsq = sb("sumsq", [IMAGES, 3 * NCLS])
        norms = sb("norms", [IMAGES, 3 * NCLS])
        dots = sb("dots", [IMAGES, NCLS, 2])
        small = sb("small", [IMAGES, 8, 2 * NCLS])
        coef = sb("coef", [IMAGES, NCLS, 2])
        atom_inT = [sb(f"atom_inT{a}", [KC, NK, HC, 128]) for a in range(2)]
        atom_outT = [sb(f"atom_outT{a}", [128, HC, D]) for a in range(ATOMS)]
        atom_hid = [sb(f"atom_hid{a}", [128, HC, 2 if a < 3 else 3, IMAGES]) for a in range(ATOMS)]
        half = sb("half", [IMAGES, 3 * NCLS])

        bank = [[ctx.enter_context(nc.psum_tensor(f"bank{p}{k}", [128, 512], F32)) for k in range(4)]
                for p in range(2)]
        all_banks = bank[0] + bank[1]

        ld_tok, ld_attn, ld_late, ld_cls = sem("ld_tok"), sem("ld_attn"), sem("ld_late"), sem("ld_cls")
        ld_atoms = sem("ld_atoms")
        consts, zeros = sem("consts"), sem("zeros")
        w_turned, w_placed = sem("w_turned"), sem("w_placed")
        x_loaded, x_regrouped, x_turned = sem("x_loaded"), sem("x_regrouped"), sem("x_turned")
        x_placed_v, x_placed_a = sem("x_placed_v"), sem("x_placed_a")
        tok_done, h_ready = both("tok_done"), both("h_ready")
        stats_ready, moments_ready = both("stats_ready"), both("moments_ready")
        eps_added, rstd_ready = both("eps_added"), both("rstd_ready")
        xn_ready, xn_turned, xnT_ready = both("xn_ready"), both("xn_turned"), both("xnT_ready")
        g_done, g_ready, v_done, v_ready = both("g_done"), both("g_ready"), both("v_done"), both("v_ready")
        s0_done, nmax0_ready, p0_ready = both("s0_done"), both("nmax0_ready"), both("p0_ready")
        p0_turned, p0T_ready, inv0_ready, o0_done = (both("p0_turned"), both("p0T_ready"),
                                                     both("inv0_ready"), both("o0_done"))
        xsum_ready, logit_done, logit_ready = both("xsum_ready"), both("logit_done"), both("logit_ready")
        nlmax_ready, lexp_ready, below_ready = both("nlmax_ready"), both("lexp_ready"), both("below_ready")
        expert_ready, experts_loaded = both("expert_ready"), both("experts_loaded")
        lparts_ready, weight_ready = both("lparts_ready"), both("weight_ready")
        hid_done, hid_ready, y_done = both("hid_done"), both("hid_ready"), both("y_done")
        qk_done, qk_ready = both("qk_done"), both("qk_ready")
        s1_done, nmax1_ready, p1_ready = both("s1_done"), both("nmax1_ready"), both("p1_ready")
        inv1_ready, p1_normed = both("inv1_ready"), both("p1_normed")
        p1_turned, p1T_ready = both("p1_turned"), both("p1T_ready")
        heads_done, heads_ready, proj_done = both("heads_done"), both("heads_ready"), both("proj_done")
        out_ready = both("out_ready")
        cls_stored, stored = both("cls_stored"), both("stored")
        c_turned, c_placed, a_hid, a_gelu = sem("c_turned"), sem("c_placed"), sem("a_hid"), sem("a_gelu")
        cand_done, cls_step, cls_pool, cls_exp = (sem("cand_done"), sem("cls_step"), sem("cls_pool"),
                                                  sem("cls_exp"))
        cls_out_stored, cls_ready, combined = sem("cls_out_stored"), sem("cls_ready"), sem("combined")

        x_rows = x.rearrange("b c (y i) w -> (b c y) i w", i=PS)
        tok_v = tok_w.rearrange("(k p) d -> p k d", k=NK)

        def folded(src, width):
            jobs = []
            for c in range(0, HC, 2):
                jobs.append([src[:, k, cc::width] if width > 1 else src[:, k, cc * 128:(cc + 1) * 128]
                             for cc in (c, c + 1) for k in range(NK)])
            return jobs

        turns = []
        for c, ins in zip(range(0, TOKK, 2), folded(tok_n, 1)):
            turns.append((ins, tok_wT[:, c:c + 2, :].rearrange("p a d -> p (a d)"), None))
        for w in range(2):
            for k in range(NK):
                turns.append(([attn_n[:, w, j, k * KC:(k + 1) * KC] for j in range(NK)], qkT[:, w, k, :], None))
        ATTN_TURNS = len(turns)
        turns.append(([wg_n[:, k * KC:(k + 1) * KC] for k in range(NK)],
                      wgT[:, :, :].rearrange("p k e -> p (k e)"), None))
        for e in range(4):
            for k in range(NK):
                dst = qk_wT[:, k, e * 6 * 32:(e + 1) * 6 * 32].rearrange("p (h d) -> p h d", d=32)[:, :, 0:HD]
                turns.append(([qkv_n[:, e, k * KC:(k + 1) * KC]], dst, HD ** -0.5 if e < 2 else None))
        for k in range(NK):
            turns.append(([qkv_n[:, e, k * KC:(k + 1) * KC] for e in (4, 5)], v_wT[:, k, :], None))
        for g in range(GROUPS):
            turns.append(([proj_n[:, k, 4 * g:4 * g + 4, :].rearrange("p h d -> p (h d)") for k in range(NK)],
                          proj_wT[:, g, :], None))
        for k in range(NK):
            for c in range(0, HC, 3):
                turns.append(([fc1_n[:, c + j, k * KC:(k + 1) * KC] for j in range(3)],
                              fc1_wT[:, k, c:c + 3, :].rearrange("p c f -> p (c f)"), None))
        for c, ins in zip(range(0, HC, 2), folded(fc2_n, HC)):
            turns.append((ins, fc2_wT[:, c:c + 2, :].rearrange("p a d -> p (a d)"), None))

        def route(c, r):
            left, right = c // 2, 3 + c % 2
            return (left, c % 2, right) if r == 0 else (right, c // 2, left)

        def clsT_v(k, a):
            if a < 3:
                return clsT[:, k, 2 * a:2 * a + 2, :]
            return clsT[:, k, a - 3::2, :]

        cls_turns = [([cls[:, c, 1, k * KC:(k + 1) * KC] for c in range(NCLS)],
                      clsT[:, k, :, :].rearrange("p n b -> p (n b)")) for k in range(NK)]
        atom_turns = []
        for a in range(ATOMS):
            jobs = []
            for k in range(NK):
                for c in range(0, HC, 3):
                    jobs.append(([atom_in_n[a][:, c + j, k * KC:(k + 1) * KC] for j in range(3)],
                                 atom_inT[a % 2][:, k, c:c + 3, :].rearrange("p c f -> p (c f)")))
            for c, ins in zip(range(0, HC, 2), folded(atom_out_n[a], HC)):
                jobs.append((ins, atom_outT[a][:, c:c + 2, :].rearrange("p a d -> p (a d)")))
            atom_turns.append(jobs)
        SUMS_STEP, SHIFT_STEP = 4, 13

        def x_tile(u):
            hh, q = divmod(u, 3)
            lo, hi = PX[q]
            dst = xT[:, hh * XROWS * GRID:(hh + 1) * XROWS * GRID].rearrange("p (r x) -> p x r", x=GRID)
            return dst[:, lo:hi, :], bank[0][u % 3][:, 0:(hi - lo) * XROWS].rearrange("p (x r) -> p x r", r=XROWS)

        def width(aps):
            return sum(a.shape[0] for a in aps)

        def run_stages(eng, stages, peel_last=False):
            for name, p, behind in ORDER:
                if not behind:
                    stages(name, p, 0)
            with eng.Fori(1, PAIRS - peel_last) as i:
                for name, p, behind in ORDER:
                    stages(name, p, i - behind if behind else i)
            if peel_last:
                for name, p, behind in ORDER:
                    stages(name, p, PAIRS - 1 - behind)
            for name, p, behind in ORDER:
                if behind:
                    stages(name, p, PAIRS - 1)

        block = ctx.enter_context(nc.Block())

        @block.sync
        def _(sp):
            sp.dma_start(tok_n[:], tok_v).then_inc(ld_tok, 16)
            sp.dma_start(xin[:], x_rows[0:XROWS]).then_inc(x_loaded, 16)
            sp.dma_start(attn_n[:], attn_w[0:2].rearrange("w (k p) o -> p w k o", k=NK)).then_inc(ld_attn, 16)
            sp.dma_start(attn_wv[:], attn_w[2].rearrange("(k p) o -> p k o", k=NK)).then_inc(ld_attn, 16)
            sp.wait_ge(zeros, 1)
            sp.dma_start(pos_b[0:R - 1, 0, :], pos[1:R, :]).then_inc(ld_tok, 16)
            sp.dma_start(pos_b[0:R - 1, 1, :], pos[R:SEQ, :]).then_inc(ld_tok, 16)
            sp.dma_start(pos_b[R - 1:R, 0, :], pos[0:1, :]).then_inc(ld_tok, 16)
            sp.dma_start(row_add[0:R - 1, 0, :], tok_b.unsqueeze(0).broadcast_to([R - 1, D])).then_inc(ld_tok, 16)
            sp.dma_start(row_add[0:R - 1, 1, :], tok_b.unsqueeze(0).broadcast_to([R - 1, D])).then_inc(ld_tok, 16)
            sp.dma_start(row_add[R - 1:R, 0, :], cls_tok).then_inc(ld_tok, 16)
            sp.dma_start(wg_n[:], wg).then_inc(ld_late, 16)
            sp.dma_start(qkv_n[:], w_qkv.rearrange("(e p) c -> p e c", e=6)).then_inc(ld_late, 16)
            for k in range(NK):
                sp.dma_start(proj_n[:, k, :, 0:HD],
                             w_proj[k * KC:(k + 1) * KC, :].rearrange("p (h d) -> p h d", d=HD)).then_inc(ld_late, 16)
            sp.dma_start(proj_brow[:], b_proj.unsqueeze(0)).then_inc(ld_late, 16)
            sp.dma_start(fc1_n[:], fc1_w.rearrange("(p c) d -> p c d", c=HC)).then_inc(ld_late, 16)
            sp.dma_start(fc1_bc[:], fc1_b.rearrange("(p c) -> p c", c=HC)).then_inc(ld_late, 16)
            sp.dma_start(fc2_n[:], fc2_w.rearrange("(k p) f -> p k f", k=NK)).then_inc(ld_late, 16)
            sp.dma_start(fc2_brow[:], fc2_b.unsqueeze(0)).then_inc(ld_late, 16)
            sp.dma_start(atom_brow[:], atom_out_b.unsqueeze(0)).then_inc(ld_atoms, 16)
            sp.dma_start(atom_bc[:], atom_in_b.rearrange("a (p c) -> p a c", c=HC)).then_inc(ld_atoms, 16)
            sp.wait_ge(w_placed, len(turns) + NK + 1)
            for a in range(ATOMS):
                sp.dma_start(atom_in_n[a][:], atom_in_w[a].rearrange("(p c) d -> p c d", c=HC)).then_inc(ld_atoms, 16)
                sp.dma_start(atom_out_n[a][:], atom_out_w[a].rearrange("(k p) f -> p k f", k=NK)).then_inc(ld_atoms, 16)

            def stages(name, p, it):
                if name == "x" and not (isinstance(it, int) and it == PAIRS - 1):
                    sp.wait_ge(x_regrouped, 3 * it + 3)
                    sp.dma_start(xin[:], x_rows[bass.ds((it + 1) * XROWS, XROWS)]).then_inc(x_loaded, 16)
                if name == "route":
                    sp.wait_ge(expert_ready[p], it + 1)
                    sp.nop(nofuse=True)
                    e = sp.value_load(expert[p][0:1, 0:1], min_val=0, max_val=EXPERTS - 1)
                    sp.dma_start(w1_sb[p][:], w1[bass.ds(e, 1)].rearrange("o (k p) f -> (o p) k f", k=NK)
                                 ).then_inc(experts_loaded[p], 16)
                    sp.dma_start(w2_sb[p][:], w2[bass.ds(e, 1)].rearrange("o (p c) d -> (o p) c d", c=HC)
                                 ).then_inc(experts_loaded[p], 16)
                    sp.dma_start(b1_sb[p][:], b1[bass.ds(e, 1)].rearrange("o (p c) -> (o p) c", c=HC)
                                 ).then_inc(experts_loaded[p], 16)
                    sp.dma_start(b2_sb[p][:], b2[bass.ds(e, 1)]).then_inc(experts_loaded[p], 16)
                if name == "ln4":
                    sp.wait_ge(xn_ready[p], 4 * it + 4)
                    img = 2 * it + p
                    sp.dma_start(scratch[bass.ds(img, 1), 1:NCLS].rearrange("o n k d -> (o n) k d"),
                                 hx[p][0:NCLS - 1, :, 0, :]).then_inc(cls_stored[p], 16)
                    sp.dma_start(scratch[bass.ds(img, 1), 0:1].rearrange("o n k d -> (o n) k d"),
                                 hx[p][R - 1:R, :, 0, :]).then_inc(cls_stored[p], 16)
                if name == "out1":
                    sp.wait_ge(out_ready[p], it + 1)
                    img = 2 * it + p
                    sp.dma_start(out[bass.ds(img, 1), NCLS:R].rearrange("o s d -> (o s) d"),
                                 y[p][NCLS - 1:R - 1, 0, :]).then_inc(stored[p], 16)
                    sp.dma_start(out[bass.ds(img, 1), R:SEQ].rearrange("o s d -> (o s) d"),
                                 y[p][0:R - 1, 1, :]).then_inc(stored[p], 16)

            run_stages(sp, stages, peel_last=True)
            for p in range(2):
                sp.wait_ge(cls_stored[p], 32 * PAIRS + 32)
                sp.wait_ge(stored[p], 32 * PAIRS + 32)
            sp.wait_ge(cls_ready, 1)
            sp.dma_start(cls[:], scratch).then_inc(ld_cls, 16)
            sp.dma_start(gate[:], gate_pair.rearrange("n r d -> (n r) d").unsqueeze(0)
                         .broadcast_to([IMAGES, 2 * NCLS, D])).then_inc(ld_cls, 16)
            sp.dma_start(gbias[:], balance.rearrange("n r -> (n r)").unsqueeze(0)
                         .broadcast_to([IMAGES, 2 * NCLS])).then_inc(ld_cls, 16)
            sp.wait_ge(cls_ready, 2)
            sp.dma_start(out[:, 0:NCLS, :], cls[:, :, 0, :]).then_inc(cls_out_stored, 16)
            sp.wait_ge(cls_out_stored, 16)

        @block.gpsimd
        def _(pool):
            g = nc.gpsimd
            g.memset(ident[:], 0.0).then_inc(consts, 1)
            pool.wait_ge(consts, 1)
            g.affine_select(out=ident[:], in_=ident[:], compare_op=ALU.not_equal, fill=1.0, base=0,
                            pattern=[[-1, 128]], channel_multiplier=1).then_inc(consts, 1)
            g.memset(eps[:], EPS)
            g.memset(minus_half[:], -0.5).then_inc(consts, 1)
            pool.wait_ge(consts, 2)
            g.tensor_scalar(not_cls[:], ident[0:R, R - 1:R], -1.0, 1.0, ALU.mult, ALU.add).then_inc(consts, 1)
            pool.wait_ge(consts, 4)

            def regroup(it):
                pool.wait_ge(x_loaded, 16 * it + 16)
                if not isinstance(it, int) or it:
                    pool.wait_ge(x_turned, 6 * it)
                pool.nop(nofuse=True)
                for lo, hi in PX:
                    dst = xg[:, lo:hi, :].rearrange("p x (i j) -> p i x j", j=PS)
                    src = xin[:, :, lo * PS:hi * PS].rearrange("p i (x j) -> p i x j", j=PS)
                    g.tensor_copy(dst, src).then_inc(x_regrouped, 1)

            regroup(0)

            def stages(name, p, it):
                if name == "tok" and p == 1 and not (isinstance(it, int) and it == PAIRS - 1):
                    regroup(it + 1)
                if name in ("ln1", "ln2", "ln3", "ln4"):
                    n = 4 * it + int(name[2])
                    pool.wait_ge(moments_ready[p], n)
                    g.tensor_tensor(var_eps[p][:], moments[p][:, :, 1], eps[0:R, 0:T], ALU.add).then_inc(eps_added[p], 1)
                    pool.wait_ge(eps_added[p], n)
                    g.tensor_tensor(rstd[p][:], var_eps[p][:], minus_half[0:R, 0:T], ALU.pow).then_inc(rstd_ready[p], 1)
                if name[0] == "head" and 1 <= name[1] <= HEADS:
                    s = name[1] - 1
                    pool.wait_ge(inv1_ready[p], HEADS * it + s + 1)
                    w = probs1[p][:, s % 3, :, :]
                    g.tensor_tensor(w, w, inv1[p][:, s, :].unsqueeze(2).broadcast_to([R, T, SP_]),
                                    ALU.mult).then_inc(p1_normed[p], 1)

            run_stages(pool, stages, peel_last=True)
            pool.wait_ge(cls_step, 4)
            g.tensor_tensor(norms[:], sumsq[:], half[:], ALU.pow).then_inc(cls_pool, 1)

        @block.tensor
        def _(pe):
            t_ = nc.tensor

            def turn(ins, dst, sem_):
                at = 0
                for a in ins:
                    n, m = a.shape[0], a.shape[1]
                    last = t_.transpose(dst[0:m, at:at + n], a, ident[0:n, 0:n])
                    at += n
                last.then_inc(sem_, 1)

            pe.wait_ge(consts, 4)
            pe.wait_ge(ld_tok, 16 * 7)
            for j, (ins, dst, f) in enumerate(turns):
                if j == TOKK // 2:
                    pe.wait_ge(ld_attn, 32)
                if j == ATTN_TURNS:
                    pe.wait_ge(ld_late, 16 * 9)
                if j >= 8:
                    pe.wait_ge(w_placed, j - 7)
                turn(ins, all_banks[j % 8], w_turned)
            pe.wait_ge(w_placed, len(turns))
            for m in range(NK):
                for k in range(NK):
                    last = t_.matmul(all_banks[m][0:KC, 0:D], qkT[:, 0, k, m * KC:(m + 1) * KC], qkT[:, 1, k, :],
                                     start=(k == 0), stop=(k == NK - 1))
                last.then_inc(w_turned, 1)
            pe.wait_ge(w_placed, len(turns) + NK + 1)

            def patches(p, t):
                for k in range(TOKK):
                    c, hh = k // 2, k % 2
                    at = (hh * XROWS + (p * CHANNELS + c) * GRID) * GRID + t * (R - 1)
                    yield xT[:, at:at + R], tok_wT[:, k, :]

            def accumulate(dst, pairs):
                pairs = list(pairs)
                for j, (a, b) in enumerate(pairs):
                    last = t_.matmul(dst, a, b, start=(j == 0), stop=(j == len(pairs) - 1))
                return last

            def turn_tokens(p, it, n, b):
                pe.wait_ge(xn_ready[p], 4 * it + n)
                for k in range(NK):
                    for t in range(T):
                        last = t_.transpose(b[0:KC, k * SP_ + t * R:k * SP_ + (t + 1) * R],
                                            hx[p][:, 1, t, k * KC:(k + 1) * KC], ident[0:R, 0:R])
                last.then_inc(xn_turned[p], 1)

            def values(p, it, b, w):
                for t in range(T):
                    last = accumulate(b[0:R, t * D:(t + 1) * D],
                                      [(xnT[p][:, k, t * R:(t + 1) * R], w[:, k, :]) for k in range(NK)])
                last.then_inc(v_done[p], 1)

            def hidden(p, w):
                for j in range(HC // 2):
                    for c in (2 * j, 2 * j + 1):
                        last = accumulate(bank[p][j][:, (c % 2) * SP_:(c % 2 + 1) * SP_],
                                          [(w(k, c), xnT[p][:, k, :]) for k in range(NK)])
                    last.then_inc(hid_done[p], 1)

            def hid_out(p, it, n, w, brow):
                b = bank[p][3]
                for t in range(T):
                    for c in range(HC):
                        if t == 0 and c % 2 == 0:
                            pe.wait_ge(hid_ready[p], 6 * it + 3 * n + c // 2 + 1)
                        t_.matmul(b[0:R, t * D:(t + 1) * D], hidT[p][:, c, t * R:(t + 1) * R], w[:, c, :],
                                  start=(c == 0), stop=False)
                    last = t_.matmul(b[0:R, t * D:(t + 1) * D], ones[0:1, 0:R], brow[0:1, :], start=False, stop=True)
                last.then_inc(y_done[p], 1)

            def stages(name, p, it):
                b = bank[p]
                if name == "x":
                    for u in range(6):
                        hh, q = divmod(u, 3)
                        if u >= 3:
                            pe.wait_ge(x_placed_v if u % 2 else x_placed_a, 3 * it + (u - 3) // 2 + 1)
                        if hh == 0:
                            pe.wait_ge(x_regrouped, 3 * it + q + 1)
                        for j, px in enumerate(range(*PX[q])):
                            src = xg[:, px, hh * 128:(hh + 1) * 128]
                            last = t_.transpose(bank[0][u % 3][:, j * XROWS:(j + 1) * XROWS], src,
                                                ident[0:XROWS, 0:XROWS])
                        last.then_inc(x_turned, 1)
                elif name == "tok":
                    pe.wait_ge(x_placed_v, 3 * it + 3)
                    pe.wait_ge(x_placed_a, 3 * it + 3)
                    for t in range(T):
                        last = accumulate(b[0][0:R, t * D:(t + 1) * D], patches(p, t))
                    last.then_inc(tok_done[p], 1)
                elif name in ("ln1", "ln2", "ln3", "ln4"):
                    turn_tokens(p, it, int(name[2]), b[{"ln1": 1, "ln2": 3, "ln3": 0, "ln4": 1}[name]])
                elif name == "q0":
                    pe.wait_ge(xnT_ready[p], 4 * it + 1)
                    for m in range(NK):
                        last = accumulate(b[2][0:KC, m * SP_:(m + 1) * SP_],
                                          [(qk_fold[:, k, m * KC:(m + 1) * KC], xnT[p][:, k, :]) for k in range(NK)])
                    last.then_inc(g_done[p], 1)
                    values(p, it, b[3], attn_wv)
                elif name == "s0":
                    pe.wait_ge(g_ready[p], it + 1)
                    for t in range(T):
                        last = accumulate(b[0][0:R, t * SP_:(t + 1) * SP_],
                                          [(gT[p][:, k, t * R:(t + 1) * R], xnT[p][:, k, :]) for k in range(NK)])
                    last.then_inc(s0_done[p], 1)
                elif name == "p0":
                    pe.wait_ge(p0_ready[p], it + 1)
                    for kt in range(T):
                        for t in range(T):
                            last = t_.transpose(b[1][0:R, kt * SP_ + t * R:kt * SP_ + (t + 1) * R],
                                                probs0[p][:, t, kt * R:(kt + 1) * R], ident[0:R, 0:R])
                    last.then_inc(p0_turned[p], 1)
                elif name == "o0":
                    pe.wait_ge(p0T_ready[p], it + 1)
                    pe.wait_ge(v_ready[p], 2 * it + 1)
                    for t in range(T):
                        last = accumulate(b[2][0:R, t * D:(t + 1) * D],
                                          [(turned[p][:, 0, kt, t * R:(t + 1) * R], vals[p][:, kt, 0:D])
                                           for kt in range(T)])
                    last.then_inc(o0_done[p], 1)
                elif name == "route":
                    pe.wait_ge(xsum_ready[p], it + 1)
                    accumulate(b[1][0:R, 0:EXPERTS],
                               [(xsum[p][:, k:k + 1].broadcast_to([KC, R]), wgT[:, k, :]) for k in range(NK)]
                               ).then_inc(logit_done[p], 1)
                elif name == "hid0":
                    pe.wait_ge(experts_loaded[p], 64 * it + 64)
                    hidden(p, lambda k, c: w1_sb[p][:, k, c::HC])
                elif name == "out0":
                    hid_out(p, it, 0, w2_sb[p], b2_sb[p])
                elif name == "qkv":
                    pe.wait_ge(xnT_ready[p], 4 * it + 3)
                    for j in range(GROUPS):
                        for m in (2 * j, 2 * j + 1):
                            last = accumulate(b[1 + j][:, (m % 2) * SP_:(m % 2 + 1) * SP_],
                                              [(qk_wT[:, k, m * 128:(m + 1) * 128], xnT[p][:, k, :])
                                               for k in range(NK)])
                        last.then_inc(qk_done[p], 1)
                    values(p, it, b[0], v_wT)
                elif name[0] == "head":
                    s = name[1]
                    if s < HEADS:
                        if s == 0:
                            pe.wait_ge(qk_ready[p], 3 * it + 3)
                            pe.wait_ge(v_ready[p], 2 * it + 2)
                        if s >= 2:
                            pe.wait_ge(p1_ready[p], HEADS * it + s - 1)
                        r, gr = (s % 4) * 32, s // 4
                        for t in range(T):
                            last = t_.matmul(b[s % 2][0:R, t * SP_:(t + 1) * SP_],
                                             qkh[p][r:r + HD, gr, t * R:(t + 1) * R],
                                             qkh[p][r:r + HD, GROUPS + gr, :], start=True, stop=True)
                        last.then_inc(s1_done[p], 1)
                    if 2 <= s < HEADS + 2:
                        h = s - 2
                        pe.wait_ge(p1_normed[p], HEADS * it + h + 1)
                        if h:
                            pe.wait_ge(p1T_ready[p], HEADS * it + h)
                        for kt in range(T):
                            for t in range(T):
                                last = t_.transpose(b[2][0:R, kt * SP_ + t * R:kt * SP_ + (t + 1) * R],
                                                    probs1[p][:, h % 3, t, kt * R:(kt + 1) * R], ident[0:R, 0:R])
                        last.then_inc(p1_turned[p], 1)
                    if s >= 3:
                        h = s - 3
                        pe.wait_ge(p1T_ready[p], HEADS * it + h + 1)
                        if h % 4 == 0 and h:
                            pe.wait_ge(heads_ready[p], GROUPS * it + h // 4)
                        r = (h % 4) * 32
                        for kt in range(T):
                            last = t_.matmul(b[3][r:r + 32, 0:SP_], vals[p][:, kt, h * HD:h * HD + 32],
                                             turned[p][:, h % 2, kt, :], start=(kt == 0), stop=(kt == T - 1))
                        if h % 4 == 3:
                            last.then_inc(heads_done[p], 1)
                elif name == "proj":
                    pe.wait_ge(heads_ready[p], GROUPS * it + GROUPS)
                    for t in range(T):
                        last = accumulate(b[0][0:R, t * D:(t + 1) * D],
                                          [(headT[p][:, gr, t * R:(t + 1) * R], proj_wT[:, gr, :])
                                           for gr in range(GROUPS)] + [(ones[0:1, 0:R], proj_brow[0:1, :])])
                    last.then_inc(proj_done[p], 1)
                elif name == "hid1":
                    pe.wait_ge(xnT_ready[p], 4 * it + 4)
                    hidden(p, lambda k, c: fc1_wT[:, k, c, :])
                elif name == "out1":
                    hid_out(p, it, 1, fc2_wT, fc2_brow)

            run_stages(pe, stages)

            n = 0
            pe.wait_ge(ld_cls, 48)
            pe.wait_ge(ld_atoms, 16 * (2 + 2 * ATOMS))
            pe.wait_ge(cls_ready, 1)
            for ins, dst in cls_turns:
                if n >= 2:
                    pe.wait_ge(c_placed, n - 1)
                turn(ins, all_banks[n % 2], c_turned)
                n += 1
            for a in range(ATOMS):
                for ins, dst in atom_turns[a]:
                    pe.wait_ge(c_placed, n - 1)
                    turn(ins, all_banks[n % 2], c_turned)
                    n += 1
                pe.wait_ge(c_placed, n)
                w = clsT_v(0, a).shape[1] * IMAGES
                for c in range(HC):
                    u = a * HC + c
                    if u >= 2:
                        pe.wait_ge(a_gelu, u - 1)
                    dst = all_banks[2 + u % 2][:, 0:w].rearrange("p (n b) -> p n b", b=IMAGES)
                    accumulate(dst, [(atom_inT[a % 2][:, k, c, :], clsT_v(k, a)) for k in range(NK)]
                               ).then_inc(a_hid, 1)
            pe.wait_ge(a_gelu, ATOMS * HC)
            for c in range(NCLS):
                if c >= 2:
                    pe.wait_ge(combined, 2 * c - 2)
                for r in range(2):
                    src, col, dst = route(c, r)
                    last = accumulate(all_banks[4 + c % 2][0:IMAGES, r * D:(r + 1) * D],
                                      [(atom_hid[src][:, j, col, :], atom_outT[dst][:, j, :]) for j in range(HC)]
                                      + [(ones[0:1, 0:IMAGES], atom_brow[0:1, dst, :])])
                last.then_inc(cand_done, 1)

        @block.vector
        def _(dve):
            v = nc.vector
            v.memset(pos_b[:], 0.0)
            v.memset(row_add[:], 0.0)
            v.memset(proj_n[:], 0.0).then_inc(zeros, 1)
            v.memset(qk_wT[:], 0.0)
            v.memset(xT[:, 2 * XROWS * GRID:], 0.0)
            v.memset(ones[:], 1.0)
            for p in range(2):
                v.memset(probs1[p][:, :, :, SEQ:SP_], 0.0)
                last = v.memset(vals[p][:, :, D:D + 16], 0.0)
            last.then_inc(zeros, 1)
            for p in range(2):
                dve.sem_inc(cls_stored[p], 32)
                dve.sem_inc(stored[p], 32)
            dve.wait_ge(zeros, 2)
            dve.wait_ge(ld_tok, 16 * 7)
            dve.wait_ge(consts, 4)
            for j, (ins, dst, f) in enumerate(turns):
                dve.wait_ge(w_turned, j + 1)
                m, n = ins[0].shape[1], width(ins)
                src = all_banks[j % 8][0:m, 0:n]
                if len(dst.shape) == 3:
                    src = src.rearrange("p (h d) -> p h d", d=HD)
                if f is None:
                    v.tensor_copy(dst, src).then_inc(w_placed, 1)
                else:
                    v.tensor_scalar(dst, src, f, None, ALU.mult).then_inc(w_placed, 1)
            for m in range(NK):
                dve.wait_ge(w_turned, len(turns) + m + 1)
                v.tensor_scalar(qk_fold[:, m, :], all_banks[m][0:KC, 0:D], D ** -0.5, None,
                                ALU.mult).then_inc(w_placed, 1)
            v.tensor_tensor(pos_b[:], pos_b[:], row_add[:], ALU.add).then_inc(w_placed, 1)
            dve.wait_ge(w_placed, len(turns) + NK + 1)

            def layer_norm(p, it, n):
                h, xn = hx[p][:, 0, :, :], hx[p][:, 1, :, :]
                dve.wait_ge(h_ready[p], 4 * it + n)
                for t in range(T):
                    last = v.bn_stats(stats[p][:, t, :], h[:, t, :])
                last.then_inc(stats_ready[p], 1)
                dve.wait_ge(stats_ready[p], 4 * it + n)
                dve.nop(nofuse=True)
                for t in range(T):
                    last = v.bn_aggr(moments[p][:, t, :], stats[p][:, t, :])
                last.then_inc(moments_ready[p], 1)
                dve.wait_ge(rstd_ready[p], 4 * it + n)
                for t in range(T):
                    last = v.tensor_scalar(xn[:, t, :], h[:, t, :], moments[p][:, t, 0:1], rstd[p][:, t:t + 1],
                                           ALU.subtract, ALU.mult)
                last.then_inc(xn_ready[p], 1)
                b = bank[p][{1: 1, 2: 3, 3: 0, 4: 1}[n]]
                dve.wait_ge(xn_turned[p], 4 * it + n)
                v.tensor_copy(xnT[p][:].rearrange("p k s -> p (k s)"), b[0:KC, 0:NK * SP_]).then_inc(xnT_ready[p], 1)

            def stages(name, p, it):
                b = bank[p]
                h = hx[p][:, 0, :, :].rearrange("p t d -> p (t d)")
                if name == "x":
                    for u in range(0, 6, 2):
                        dve.wait_ge(x_turned, 6 * it + u + 1)
                        dst, src = x_tile(u)
                        v.tensor_copy(dst, src).then_inc(x_placed_v, 1)
                elif name == "tok":
                    dve.wait_ge(tok_done[p], it + 1)
                    if not (isinstance(it, int) and it == 0):
                        dve.wait_ge(out_ready[p], it)
                    dve.wait_ge(cls_stored[p], 32 * it + 32)
                    v.scalar_tensor_tensor(out=h, in0=b[0][0:R, 0:T * D], scalar=not_cls[:, 0:1],
                                           in1=pos_b[:].rearrange("p t d -> p (t d)"),
                                           op0=ALU.mult, op1=ALU.add).then_inc(h_ready[p], 1)
                elif name in ("ln1", "ln2", "ln3", "ln4"):
                    layer_norm(p, it, int(name[2]))
                elif name == "s0":
                    dve.wait_ge(s0_done[p], it + 1)
                    v.tensor_reduce(nmax0[p][:], b[0][0:R, 0:T * SP_].rearrange("p (t s) -> p t s", s=SP_)[:, :, 0:SEQ],
                                    AX, ALU.max, negate=True).then_inc(nmax0_ready[p], 1)
                elif name == "p0":
                    dve.wait_ge(p0_turned[p], it + 1)
                    v.tensor_copy(turned[p][:, 0, :, :].rearrange("p k s -> p (k s)"),
                                  b[1][0:R, 0:T * SP_]).then_inc(p0T_ready[p], 1)
                    v.reciprocal(inv0[p][:], sum0[p][:]).then_inc(inv0_ready[p], 1)
                elif name == "o0":
                    dve.wait_ge(o0_done[p], it + 1)
                    dve.wait_ge(inv0_ready[p], it + 1)
                    for t in range(T):
                        last = v.scalar_tensor_tensor(out=hx[p][:, 0, t, :], in0=b[2][0:R, t * D:(t + 1) * D],
                                                      scalar=inv0[p][:, t:t + 1], in1=hx[p][:, 0, t, :],
                                                      op0=ALU.mult, op1=ALU.add)
                    last.then_inc(h_ready[p], 1)
                elif name == "route":
                    dve.wait_ge(xnT_ready[p], 4 * it + 2)
                    v.tensor_reduce(xsum[p][:], xnT[p][:, :, 0:SEQ], AX, ALU.add).then_inc(xsum_ready[p], 1)
                    dve.wait_ge(logit_done[p], it + 1)
                    v.tensor_scalar(logit[p][:], b[1][0:R, 0:EXPERTS], 1.0 / SEQ, None, ALU.mult).then_inc(logit_ready[p], 1)
                    dve.wait_ge(logit_ready[p], it + 1)
                    v.tensor_reduce(nlmax[p][:], logit[p][:], AX, ALU.max, negate=True).then_inc(nlmax_ready[p], 1)
                    dve.wait_ge(nlmax_ready[p], it + 1)
                    v.tensor_scalar(below[p][:], logit[p][:, 0:2], nlmax[p][:, 0:1], 0.0, ALU.add,
                                    ALU.is_lt).then_inc(below_ready[p], 1)
                    dve.wait_ge(below_ready[p], it + 1)
                    v.scalar_tensor_tensor(out=expert[p][:], in0=below[p][0:1, 1:2], scalar=1.0,
                                           in1=below[p][0:1, 0:1], op0=ALU.add, op1=ALU.mult).then_inc(expert_ready[p], 1)
                    dve.wait_ge(lexp_ready[p], it + 1)
                    v.tensor_reduce(ltop[p][:], lexp[p][:], AX, ALU.max)
                    v.reciprocal(linv[p][:], lsum[p][:]).then_inc(lparts_ready[p], 1)
                    dve.wait_ge(lparts_ready[p], it + 1)
                    v.tensor_tensor(weight[p][:], ltop[p][:], linv[p][:], ALU.mult).then_inc(weight_ready[p], 1)
                elif name == "out0":
                    dve.wait_ge(y_done[p], 2 * it + 1)
                    dve.wait_ge(weight_ready[p], it + 1)
                    v.scalar_tensor_tensor(out=h, in0=b[3][0:R, 0:T * D], scalar=weight[p][:, 0:1], in1=h,
                                           op0=ALU.mult, op1=ALU.add).then_inc(h_ready[p], 1)
                elif name[0] == "head":
                    s = name[1]
                    if s < HEADS:
                        dve.wait_ge(s1_done[p], HEADS * it + s + 1)
                        src = b[s % 2][0:R, 0:T * SP_].rearrange("p (t s) -> p t s", s=SP_)[:, :, 0:SEQ]
                        v.tensor_reduce(nmax1[p][:, s, :], src, AX, ALU.max, negate=True).then_inc(nmax1_ready[p], 1)
                    if 1 <= s <= HEADS:
                        dve.wait_ge(p1_ready[p], HEADS * it + s)
                        v.reciprocal(inv1[p][:, s - 1, :], sum1[p][:, s - 1, :]).then_inc(inv1_ready[p], 1)
                    if 2 <= s < HEADS + 2:
                        dve.wait_ge(p1_turned[p], HEADS * it + s - 1)
                        v.tensor_copy(turned[p][:, s % 2, :, :].rearrange("p k s -> p (k s)"),
                                      b[2][0:R, 0:T * SP_]).then_inc(p1T_ready[p], 1)
                    if s >= 3 and (s - 3) % 4 == 3:
                        gr = (s - 3) // 4
                        dve.wait_ge(heads_done[p], GROUPS * it + gr + 1)
                        v.tensor_copy(headT[p][:, gr, :], b[3][:, 0:SP_]).then_inc(heads_ready[p], 1)
                elif name == "proj":
                    dve.wait_ge(proj_done[p], it + 1)
                    v.tensor_tensor(h, b[0][0:R, 0:T * D], h, ALU.add).then_inc(h_ready[p], 1)
                elif name == "out1":
                    dve.wait_ge(y_done[p], 2 * it + 2)
                    dve.wait_ge(stored[p], 32 * it + 32)
                    v.tensor_tensor(y[p][:].rearrange("p t d -> p (t d)"), b[3][0:R, 0:T * D], h,
                                    ALU.add).then_inc(out_ready[p], 1)

            run_stages(dve, stages)

            for p in range(2):
                dve.wait_ge(out_ready[p], PAIRS)
                dve.wait_ge(stored[p], 32 * PAIRS + 32)
                dve.wait_ge(cls_stored[p], 32 * PAIRS + 32)
            v.memset(half[:], 0.5).then_inc(cls_ready, 1)
            for n, (ins, dst) in enumerate(cls_turns + [job for jobs in atom_turns for job in jobs]):
                dve.wait_ge(c_turned, n + 1)
                a, job = divmod(n - len(cls_turns), len(atom_turns[0]))
                if a >= 2 and job == 0:
                    dve.wait_ge(a_hid, (a - 1) * HC)
                v.tensor_copy(dst, all_banks[n % 2][0:ins[0].shape[1], 0:width(ins)]).then_inc(c_placed, 1)

            dve.wait_ge(ld_cls, 48)
            dve.wait_ge(cls_ready, 1)
            step = [0]

            def link(ins):
                step[0] += 1
                ins.then_inc(cls_step, 1)
                dve.wait_ge(cls_step, step[0])

            xc = cls[:, :, 1, :]
            pv = prod[:].rearrange("b (n r) d -> b n r d", r=2)
            gv = gate[:].rearrange("b (n r) d -> b n r d", r=2)
            sv = small[:].rearrange("b k (n r) -> b k n r", r=2)

            def over_routes(a):
                return a.unsqueeze(2).broadcast_to([IMAGES, NCLS, 2])

            link(v.tensor_tensor(prod[:, 0:NCLS, :], xc, xc, ALU.mult))
            link(v.tensor_reduce(sumsq[:, 0:NCLS], prod[:, 0:NCLS, :], AX, ALU.add))
            link(v.tensor_tensor(prod[:], gate[:], gate[:], ALU.mult))
            link(v.tensor_reduce(sumsq[:, NCLS:], prod[:], AX, ALU.add))
            assert step[0] == SUMS_STEP
            for r in range(2):
                last = v.tensor_tensor(pv[:, :, r, :], xc, gv[:, :, r, :], ALU.mult)
            link(last)
            link(v.tensor_reduce(dots[:].rearrange("b n r -> b (n r)"), prod[:], AX, ALU.add))
            dve.wait_ge(cls_pool, 1)
            link(v.tensor_scalar(norms[:], norms[:], 1e-12, None, ALU.max))
            link(v.reciprocal(sumsq[:], norms[:]))
            link(v.tensor_tensor(dots[:], dots[:], over_routes(sumsq[:, 0:NCLS]), ALU.mult))
            link(v.tensor_tensor(dots[:], dots[:], sumsq[:, NCLS:].rearrange("b (n r) -> b n r", r=2), ALU.mult))
            link(v.tensor_tensor(dots[:], dots[:], gbias[:].rearrange("b (n r) -> b n r", r=2), ALU.add))
            link(v.tensor_reduce(small[:, 0, 0:NCLS], dots[:], AX, ALU.max))
            link(v.tensor_tensor(sv[:, 1, :, :], dots[:], over_routes(small[:, 0, 0:NCLS]), ALU.subtract))
            assert step[0] == SHIFT_STEP
            dve.wait_ge(cls_exp, 1)
            link(v.tensor_reduce(small[:, 3, 0:NCLS], sv[:, 2, :, :], AX, ALU.add))
            link(v.reciprocal(small[:, 4, 0:NCLS], small[:, 3, 0:NCLS]))
            link(v.tensor_tensor(sv[:, 5, :, :], sv[:, 2, :, :], over_routes(small[:, 4, 0:NCLS]), ALU.mult))
            link(v.tensor_tensor(small[:, 6, 0:NCLS], dots[:, :, 0], dots[:, :, 1], ALU.is_ge))
            link(v.tensor_scalar(small[:, 7, 0:NCLS], small[:, 6, 0:NCLS], -1.0, 1.0, ALU.mult, ALU.add))
            link(v.tensor_tensor(coef[:, :, 0], sv[:, 5, :, 0], small[:, 6, 0:NCLS], ALU.mult))
            link(v.tensor_tensor(coef[:, :, 1], sv[:, 5, :, 1], small[:, 7, 0:NCLS], ALU.mult))
            for c in range(NCLS):
                dve.wait_ge(cand_done, c + 1)
                for r in range(2):
                    v.scalar_tensor_tensor(out=cls[:, c, 0, :], in0=all_banks[4 + c % 2][0:IMAGES, r * D:(r + 1) * D],
                                           scalar=coef[:, c, r:r + 1], in1=cls[:, c, 0, :],
                                           op0=ALU.mult, op1=ALU.add).then_inc(combined, 1)
                    dve.wait_ge(combined, 2 * c + r + 1)
            v.memset(half[:], 0.0).then_inc(cls_ready, 1)

        @block.scalar
        def _(act):
            s_ = nc.scalar

            def softmax_weights(dst, src, nmax, total):
                for t in range(T):
                    last = s_.activation(dst[:, t, 0:SEQ], src[0:R, t * SP_:t * SP_ + SEQ], ACT.Exp,
                                         bias=nmax[:, t:t + 1], scale=1.0, accum_out=total[:, t:t + 1])
                return last

            def stages(name, p, it):
                b = bank[p]
                if name == "x":
                    for u in range(1, 6, 2):
                        act.wait_ge(x_turned, 6 * it + u + 1)
                        dst, src = x_tile(u)
                        s_.activation(dst, src, ACT.Copy).then_inc(x_placed_a, 1)
                elif name == "q0":
                    act.wait_ge(g_done[p], it + 1)
                    s_.activation(gT[p][:].rearrange("p k s -> p (k s)"), b[2][0:KC, 0:NK * SP_],
                                  ACT.Copy).then_inc(g_ready[p], 1)
                    act.wait_ge(v_done[p], 2 * it + 1)
                    s_.activation(vals[p][:, :, 0:D], b[3][0:R, 0:T * D].rearrange("p (t d) -> p t d", t=T),
                                  ACT.Copy).then_inc(v_ready[p], 1)
                elif name == "s0":
                    act.wait_ge(nmax0_ready[p], it + 1)
                    softmax_weights(probs0[p], b[0], nmax0[p], sum0[p]).then_inc(p0_ready[p], 1)
                elif name == "route":
                    act.wait_ge(nlmax_ready[p], it + 1)
                    s_.activation(lexp[p][:], logit[p][:], ACT.Exp, bias=nlmax[p][:, 0:1], scale=1.0,
                                  accum_out=lsum[p][:]).then_inc(lexp_ready[p], 1)
                elif name in ("hid0", "hid1"):
                    n = 6 * it + (3 if name == "hid1" else 0)
                    bias = fc1_bc if name == "hid1" else b1_sb[p]
                    for j in range(HC // 2):
                        act.wait_ge(hid_done[p], n + j + 1)
                        for c in (2 * j, 2 * j + 1):
                            last = s_.activation(hidT[p][:, c, :], b[j][:, (c % 2) * SP_:(c % 2 + 1) * SP_], ACT.Gelu,
                                                 bias=bias[:, c:c + 1], scale=1.0)
                        last.then_inc(hid_ready[p], 1)
                elif name == "qkv":
                    for j in range(GROUPS):
                        act.wait_ge(qk_done[p], GROUPS * it + j + 1)
                        s_.activation(qkh[p][:, 2 * j:2 * j + 2, :].rearrange("p m s -> p (m s)"),
                                      b[1 + j][:, 0:2 * SP_], ACT.Copy).then_inc(qk_ready[p], 1)
                    act.wait_ge(v_done[p], 2 * it + 2)
                    s_.activation(vals[p][:, :, 0:D], b[0][0:R, 0:T * D].rearrange("p (t d) -> p t d", t=T),
                                  ACT.Copy).then_inc(v_ready[p], 1)
                elif name[0] == "head" and name[1] < HEADS:
                    s = name[1]
                    if s >= 3:
                        act.wait_ge(p1_turned[p], HEADS * it + s - 2)
                    act.wait_ge(nmax1_ready[p], HEADS * it + s + 1)
                    softmax_weights(probs1[p][:, s % 3], b[s % 2], nmax1[p][:, s, :], sum1[p][:, s, :]
                                    ).then_inc(p1_ready[p], 1)

            run_stages(act, stages)
            for u in range(ATOMS * HC):
                a, c = divmod(u, HC)
                act.wait_ge(a_hid, u + 1)
                n = atom_hid[a].shape[2]
                s_.activation(atom_hid[a][:, c, :, :], all_banks[2 + u % 2][:, 0:n * IMAGES]
                              .rearrange("p (n b) -> p n b", b=IMAGES), ACT.Gelu,
                              bias=atom_bc[:, a, c:c + 1], scale=1.0).then_inc(a_gelu, 1)
            act.wait_ge(cls_step, SHIFT_STEP)
            s_.activation(small[:, 2, :], small[:, 1, :], ACT.Exp).then_inc(cls_exp, 1)


_INS = ["x", "L0_tok_W", "L0_tok_b", "L0_tok_class_token", "L0_tok_pos_embed", "L0_attn_W", "L0_ffn_Wg",
        "L0_ffn_W1", "L0_ffn_b1", "L0_ffn_W2", "L0_ffn_b2", "L1_attn_w_qkv", "L1_attn_w_proj",
        "L1_attn_b_proj", "L1_ffn_fc1_w", "L1_ffn_fc1_b", "L1_ffn_fc2_w", "L1_ffn_fc2_b",
        "L1_ffn_gate_pair", "L1_ffn_atom_in_w", "L1_ffn_atom_in_b", "L1_ffn_atom_out_w",
        "L1_ffn_atom_out_b", "L1_ffn_balance_bias"]


def kernel(**inputs):
    import numpy as _np
    import concourse.bacc as _bacc
    from concourse import mybir as _mybir
    from concourse.bass_utils import run_bass_kernel_spmd as _run

    nc = _bacc.Bacc("TRN2", target_bir_lowering=False, num_devices=1)
    arrays, args = {}, []
    for name in _INS:
        a = _np.ascontiguousarray(inputs[name])
        arrays[f"in_{name}_dram"] = a
        args.append(nc.dram_tensor(f"in_{name}_dram", a.shape, _mybir.dt.from_np(a.dtype), kind="ExternalInput").ap())
    out = nc.dram_tensor("out_0_dram", (IMAGES, SEQ, D), _mybir.dt.float32, kind="ExternalOutput").ap()
    scratch = nc.dram_tensor("cls_scratch", (IMAGES, NCLS, 2, D), _mybir.dt.float32, kind="Internal").ap()
    vit_kernel(nc, *args, out, scratch)
    r = _run(nc, [arrays], core_ids=[0])
    return r.results[0]["out_0_dram"]
```

```python
from contextlib import ExitStack

import concourse.bass as bass
from concourse import mybir

F32 = mybir.dt.float32
F32R = mybir.dt.float32r
I32 = mybir.dt.int32
ALU = mybir.AluOpType
ACT = mybir.ActivationFunctionType
AX = mybir.AxisListType.X

IMAGES, CHANNELS, SIDE = 64, 3, 224
GRID = 14
PS = SIDE // GRID
D = 192
F = 768
SEQ = GRID * GRID + 1
R = 99
T = 2
SP_ = R * T
KC = 96
NK = D // KC
HC = F // 128
TOKK = CHANNELS * PS * PS // 128
HEADS, HD = 12, 16
GROUPS = HEADS // 4
EXPERTS = 3
NCLS, ATOMS = 6, 5
EPS = 1e-5
PAIRS = IMAGES // 2
XROWS = 2 * CHANNELS * GRID
PX = [(0, 5), (5, 10), (10, 14)]

RING = 6


def norm_stages(n):
    return [(f"stat{n}", 0.0, 2.2), (f"norm{n}", 0.0, 0.9), (f"turn{n}", 0.4, 1.0)]


def ffn_stages(n):
    return [(f"hid{n}_0", 1.3, 0.0), (f"hid{n}_1", 1.3, 0.0), (f"hid{n}_2", 1.3, 0.9),
            (f"out{n}_0", 1.95, 0.0), (f"out{n}_1", 1.95, 1.2)]


STAGES = ([("tok0", 1.95, 0.0), ("tok1", 1.95, 1.2)] + norm_stages(1)
          + [("q0", 1.3, 0.0), ("v0", 1.3, 0.0), ("s0", 1.3, 2.4), ("p0", 0.4, 1.0), ("o0", 1.3, 1.2)]
          + norm_stages(2) + [("route", 0.1, 12.0)] + ffn_stages(0) + norm_stages(3)
          + [("qk1_0", 1.3, 0.0), ("qk1_1", 1.3, 0.0), ("qk1_2", 1.3, 0.0), ("v1", 1.3, 0.9)]
          + [(("max", j), 0.35, 1.0) for j in range(HEADS // 2)] + [("maxT", 0.1, 0.8)]
          + [(("att", s), 1.9 if s % 4 == 1 and s > 4 else 0.5, 0.3) for s in range(HEADS + 2)]
          + [("proj", 1.95, 1.2)] + norm_stages(4) + ffn_stages(1))
OFFSET = 0.7


def merged_order():
    tensor = sum(w for _, w, _ in STAGES)
    waits = sum(w for _, _, w in STAGES)
    stretch = (2 * tensor - waits) / tensor
    at, starts = 0.0, []
    for name, work, wait in STAGES:
        starts.append((name, at))
        at += work * stretch + wait
    order = [(0.0, 0, "x", 0, 0)]
    for name, t in starts:
        order.append((t, 1, name, 0, 0))
        late = t + OFFSET * at
        order.append((late % at, 2, name, 1, int(late >= at)))
    order.sort(key=lambda o: o[:2])
    return [(name, p, behind) for _, _, name, p, behind in order]


ORDER = merged_order()
TURN_BANK = {1: 1, 2: 3, 3: 0, 4: 1}


def vit_kernel(nc, x, tok_w, tok_b, cls_tok, pos, attn_w, wg, w1, b1, w2, b2, w_qkv, w_proj, b_proj,
               fc1_w, fc1_b, fc2_w, fc2_b, gate_pair, atom_in_w, atom_in_b, atom_out_w, atom_out_b,
               balance, out, scratch):
    with ExitStack() as ctx:
        def sb(name, shape, dt=F32, stack=ctx):
            return stack.enter_context(nc.sbuf_tensor(name, shape, dt))

        def sem(name):
            return ctx.enter_context(nc.semaphore(name))

        def both(name):
            return [sem(f"{name}_{p}") for p in range(2)]

        ident = sb("ident", [128, 128])
        ones = sb("ones", [1, 128])
        not_cls = sb("not_cls", [R, 1])
        ones32 = sb("ones32", [R, 32])
        group_row = sb("group_row", [128, GROUPS])
        rest_factor = sb("rest_factor", [128, 1])
        select = sb("select", [128, GROUPS, R], F32R)
        minus_half = sb("minus_half", [128, T])
        eps = sb("eps", [128, T])
        pos_b = sb("pos_b", [R, T, D])
        tok_wT = sb("tok_wT", [128, TOKK, D])
        qk_fold = sb("qk_fold", [KC, NK, D])
        attn_wv = sb("attn_wv", [KC, NK, D])
        wgT = sb("wgT", [KC, NK, EXPERTS])
        qk_wT = sb("qk_wT", [KC, NK, 2 * HEADS * 32])
        v_wT = sb("v_wT", [KC, NK, D])
        proj_wT = sb("proj_wT", [128, GROUPS, D])
        proj_brow = sb("proj_brow", [1, D])
        fc1_wT = sb("fc1_wT", [KC, NK, HC, 128])
        fc1_bc = sb("fc1_bc", [128, HC])
        fc2_wT = sb("fc2_wT", [128, HC, D])
        fc2_brow = sb("fc2_brow", [1, D])
        atom_brow = sb("atom_brow", [1, ATOMS, D])
        atom_bc = sb("atom_bc", [128, ATOMS, HC])

        with ExitStack() as early:
            tok_n = sb("tok_n", [KC, NK, F], stack=early)
            attn_n = sb("attn_n", [KC, 2, NK, D], stack=early)
            qkT = sb("qkT", [KC, 2, NK, D], stack=early)
            qkv_n = sb("qkv_n", [KC, 6, D], stack=early)
            proj_n = sb("proj_n", [KC, NK, HEADS, 32], stack=early)
            fc1_n = sb("fc1_n", [128, HC, D], stack=early)
            fc2_n = sb("fc2_n", [KC, NK, F], stack=early)
            wg_n = sb("wg_n", [EXPERTS, D], stack=early)
            row_add = sb("row_add", [R, T, D], stack=early)
        atom_in_n = [sb(f"atom_in_n{a}", [128, HC, D]) for a in range(ATOMS - 1)]
        atom_out_n = [sb(f"atom_out_n{a}", [KC, NK, F]) for a in range(ATOMS - 1)]

        with ExitStack() as loop:
            def two(name, shape, dt=F32):
                return [sb(f"{name}{p}", shape, dt, loop) for p in range(2)]

            xin = sb("xin", [XROWS, PS, SIDE], stack=loop)
            xg = sb("xg", [XROWS, GRID, PS * PS], stack=loop)
            xT = sb("xT", [128, 2 * XROWS * GRID + 4], stack=loop)
            hx = two("hx", [R, 2, T, D])
            stats = two("stats", [R, T, 6])
            moments = two("moments", [R, T, 2])
            var_eps = two("var_eps", [R, T])
            rstd = two("rstd", [R, T])
            xnT = two("xnT", [KC, NK, SP_])
            gT = two("gT", [KC, NK, SP_])
            vals = two("vals", [R, T, D + 16])
            nmax0 = two("nmax0", [R, T])
            sum0 = two("sum0", [R, T])
            inv0 = two("inv0", [R, T])
            xsum = two("xsum", [KC, NK])
            logit = two("logit", [R, EXPERTS])
            nlmax = two("nlmax", [R, 1])
            lexp = two("lexp", [R, EXPERTS])
            lsum = two("lsum", [R, 1])
            linv = two("linv", [R, 1])
            ltop = two("ltop", [R, 1])
            weight = two("weight", [R, 1])
            below = two("below", [R, 2])
            expert = two("expert", [1, 1], I32)
            w1_sb = two("w1_sb", [KC, NK, F])
            w2_sb = two("w2_sb", [128, HC, D])
            b1_sb = two("b1_sb", [128, HC])
            b2_sb = two("b2_sb", [1, D])
            with ExitStack() as hid:
                hidT = [sb(f"hidT{p}", [128, HC, SP_], stack=hid) for p in range(2)]
            hi = two("hi", [128, 2 * GROUPS, SP_], F32R)
            rest = two("rest", [128, 2 * GROUPS, SP_], F32R)
            nmax1 = two("nmax1", [R, T, 4, 32])
            nmaxT = two("nmaxT", [128, SP_], F32R)
            inv1 = two("inv1", [128, SP_])
            probs = two("probs", [R, RING, T, SP_])
            probs0 = [probs[p][:, 0, :, :] for p in range(2)]
            turned = [probs[p][:, 1, :, :] for p in range(2)]
            headT = two("headT", [128, GROUPS, SP_])
            y = two("y", [R, T, D])
        atom_in_n.append(sb(f"atom_in_n{ATOMS - 1}", [128, HC, D]))
        atom_out_n.append(sb(f"atom_out_n{ATOMS - 1}", [KC, NK, F]))
        cls = sb("cls", [IMAGES, NCLS, 2, D])
        clsT = sb("clsT", [KC, NK, NCLS, IMAGES])
        gate = sb("gate", [IMAGES, 2 * NCLS, D])
        gbias = sb("gbias", [IMAGES, 2 * NCLS])
        prod = sb("prod", [IMAGES, 2 * NCLS, D])
        sumsq = sb("sumsq", [IMAGES, 3 * NCLS])
        norms = sb("norms", [IMAGES, 3 * NCLS])
        dots = sb("dots", [IMAGES, NCLS, 2])
        small = sb("small", [IMAGES, 8, 2 * NCLS])
        coef = sb("coef", [IMAGES, NCLS, 2])
        atom_inT = [sb(f"atom_inT{a}", [KC, NK, HC, 128]) for a in range(2)]
        atom_outT = [sb(f"atom_outT{a}", [128, HC, D]) for a in range(ATOMS)]
        atom_hid = [sb(f"atom_hid{a}", [128, HC, 2 if a < 3 else 3, IMAGES]) for a in range(ATOMS)]
        half = sb("half", [IMAGES, 3 * NCLS])

        banks = [ctx.enter_context(nc.psum_tensor(f"banks{p}", [128, 4, 512], F32)) for p in range(2)]
        bank = [[banks[p][:, k, :] for k in range(4)] for p in range(2)]
        all_banks = bank[0] + bank[1]

        ld_tok, ld_attn, ld_late, ld_cls = sem("ld_tok"), sem("ld_attn"), sem("ld_late"), sem("ld_cls")
        ld_atoms = sem("ld_atoms")
        consts, zeros = sem("consts"), sem("zeros")
        w_turned, w_placed = sem("w_turned"), sem("w_placed")
        x_loaded, x_regrouped, x_turned = sem("x_loaded"), sem("x_regrouped"), sem("x_turned")
        x_placed_v, x_placed_a = sem("x_placed_v"), sem("x_placed_a")
        tok_done, h_ready = both("tok_done"), both("h_ready")
        stats_ready, moments_ready = both("stats_ready"), both("moments_ready")
        eps_added, rstd_ready = both("eps_added"), both("rstd_ready")
        xn_ready, xn_turned, xnT_ready = both("xn_ready"), both("xn_turned"), both("xnT_ready")
        g_done, g_ready, v_done, v_ready = both("g_done"), both("g_ready"), both("v_done"), both("v_ready")
        s0_done, nmax0_ready, p0_ready = both("s0_done"), both("nmax0_ready"), both("p0_ready")
        p0_turned, p0T_ready, inv0_ready, o0_done = (both("p0_turned"), both("p0T_ready"),
                                                     both("inv0_ready"), both("o0_done"))
        xsum_ready, logit_done, logit_ready = both("xsum_ready"), both("logit_done"), both("logit_ready")
        nlmax_ready, lexp_ready, below_ready = both("nlmax_ready"), both("lexp_ready"), both("below_ready")
        expert_ready, experts_loaded = both("expert_ready"), both("experts_loaded")
        lparts_ready, weight_ready = both("lparts_ready"), both("weight_ready")
        hid_done, hid_ready, y_done = both("hid_done"), both("hid_ready"), both("y_done")
        qk_done, hi_ready, rest_ready = both("qk_done"), both("hi_ready"), both("rest_ready")
        s1_done, nmax1_ready = both("s1_done"), both("nmax1_ready")
        nmax_turned, nmaxT_ready = both("nmax_turned"), both("nmaxT_ready")
        st_done, p1_ready, inv1_ready = both("st_done"), both("p1_ready"), both("inv1_ready")
        heads_done, heads_ready, proj_done = both("heads_done"), both("heads_ready"), both("proj_done")
        out_ready = both("out_ready")
        cls_stored, stored = both("cls_stored"), both("stored")
        c_turned, c_placed, a_hid, a_gelu = sem("c_turned"), sem("c_placed"), sem("a_hid"), sem("a_gelu")
        cand_done, cls_step, cls_pool, cls_exp = (sem("cand_done"), sem("cls_step"), sem("cls_pool"),
                                                  sem("cls_exp"))
        cls_out_stored, cls_ready, combined = sem("cls_out_stored"), sem("cls_ready"), sem("combined")

        x_rows = x.rearrange("b c (y i) w -> (b c y) i w", i=PS)
        tok_v = tok_w.rearrange("(k p) d -> p k d", k=NK)

        def folded(src, width):
            jobs = []
            for c in range(0, HC, 2):
                jobs.append([src[:, k, cc::width] if width > 1 else src[:, k, cc * 128:(cc + 1) * 128]
                             for cc in (c, c + 1) for k in range(NK)])
            return jobs

        turns = []
        for c, ins in zip(range(0, TOKK, 2), folded(tok_n, 1)):
            turns.append((ins, tok_wT[:, c:c + 2, :].rearrange("p a d -> p (a d)"), None))
        for w in range(2):
            for k in range(NK):
                turns.append(([attn_n[:, w, j, k * KC:(k + 1) * KC] for j in range(NK)], qkT[:, w, k, :], None))
        ATTN_TURNS = len(turns)
        turns.append(([wg_n[:, k * KC:(k + 1) * KC] for k in range(NK)],
                      wgT[:, :, :].rearrange("p k e -> p (k e)"), None))
        for e in range(4):
            for k in range(NK):
                dst = qk_wT[:, k, e * 6 * 32:(e + 1) * 6 * 32].rearrange("p (h r d) -> p h r d", d=HD, r=2)
                turns.append(([qkv_n[:, e, k * KC:(k + 1) * KC]], dst, HD ** -0.5 if e < 2 else None))
        for k in range(NK):
            turns.append(([qkv_n[:, e, k * KC:(k + 1) * KC] for e in (4, 5)], v_wT[:, k, :], None))
        for g in range(GROUPS):
            turns.append(([proj_n[:, k, 4 * g:4 * g + 4, :].rearrange("p h d -> p (h d)") for k in range(NK)],
                          proj_wT[:, g, :], None))
        for k in range(NK):
            for c in range(0, HC, 3):
                turns.append(([fc1_n[:, c + j, k * KC:(k + 1) * KC] for j in range(3)],
                              fc1_wT[:, k, c:c + 3, :].rearrange("p c f -> p (c f)"), None))
        for c, ins in zip(range(0, HC, 2), folded(fc2_n, HC)):
            turns.append((ins, fc2_wT[:, c:c + 2, :].rearrange("p a d -> p (a d)"), None))

        def route(c, r):
            left, right = c // 2, 3 + c % 2
            return (left, c % 2, right) if r == 0 else (right, c // 2, left)

        def clsT_v(k, a):
            if a < 3:
                return clsT[:, k, 2 * a:2 * a + 2, :]
            return clsT[:, k, a - 3::2, :]

        cls_turns = [([cls[:, c, 1, k * KC:(k + 1) * KC] for c in range(NCLS)],
                      clsT[:, k, :, :].rearrange("p n b -> p (n b)")) for k in range(NK)]
        atom_turns = []
        for a in range(ATOMS):
            jobs = []
            for k in range(NK):
                for c in range(0, HC, 3):
                    jobs.append(([atom_in_n[a][:, c + j, k * KC:(k + 1) * KC] for j in range(3)],
                                 atom_inT[a % 2][:, k, c:c + 3, :].rearrange("p c f -> p (c f)")))
            for c, ins in zip(range(0, HC, 2), folded(atom_out_n[a], HC)):
                jobs.append((ins, atom_outT[a][:, c:c + 2, :].rearrange("p a d -> p (a d)")))
            atom_turns.append(jobs)
        SUMS_STEP, SHIFT_STEP = 4, 13

        def x_tile(u):
            hh, q = divmod(u, 3)
            lo, hi = PX[q]
            dst = xT[:, hh * XROWS * GRID:(hh + 1) * XROWS * GRID].rearrange("p (r x) -> p x r", x=GRID)
            return dst[:, lo:hi, :], bank[0][u % 3][:, 0:(hi - lo) * XROWS].rearrange("p (x r) -> p x r", r=XROWS)

        def width(aps):
            return sum(a.shape[0] for a in aps)

        def run_stages(eng, stages, peel_last=False):
            for name, p, behind in ORDER:
                if not behind:
                    stages(name, p, 0)
            with eng.Fori(1, PAIRS - peel_last) as i:
                for name, p, behind in ORDER:
                    stages(name, p, i - behind if behind else i)
            if peel_last:
                for name, p, behind in ORDER:
                    stages(name, p, PAIRS - 1 - behind)
            for name, p, behind in ORDER:
                if behind:
                    stages(name, p, PAIRS - 1)

        block = ctx.enter_context(nc.Block())

        @block.sync
        def _(sp):
            sp.dma_start(tok_n[:], tok_v).then_inc(ld_tok, 16)
            sp.dma_start(xin[:], x_rows[0:XROWS]).then_inc(x_loaded, 16)
            sp.dma_start(attn_n[:], attn_w[0:2].rearrange("w (k p) o -> p w k o", k=NK)).then_inc(ld_attn, 16)
            sp.dma_start(attn_wv[:], attn_w[2].rearrange("(k p) o -> p k o", k=NK)).then_inc(ld_attn, 16)
            sp.wait_ge(zeros, 1)
            sp.dma_start(pos_b[0:R - 1, 0, :], pos[1:R, :]).then_inc(ld_tok, 16)
            sp.dma_start(pos_b[0:R - 1, 1, :], pos[R:SEQ, :]).then_inc(ld_tok, 16)
            sp.dma_start(pos_b[R - 1:R, 0, :], pos[0:1, :]).then_inc(ld_tok, 16)
            sp.dma_start(row_add[0:R - 1, 0, :], tok_b.unsqueeze(0).broadcast_to([R - 1, D])).then_inc(ld_tok, 16)
            sp.dma_start(row_add[0:R - 1, 1, :], tok_b.unsqueeze(0).broadcast_to([R - 1, D])).then_inc(ld_tok, 16)
            sp.dma_start(row_add[R - 1:R, 0, :], cls_tok).then_inc(ld_tok, 16)
            sp.dma_start(wg_n[:], wg).then_inc(ld_late, 16)
            sp.dma_start(qkv_n[:], w_qkv.rearrange("(e p) c -> p e c", e=6)).then_inc(ld_late, 16)
            for k in range(NK):
                sp.dma_start(proj_n[:, k, :, 0:HD],
                             w_proj[k * KC:(k + 1) * KC, :].rearrange("p (h d) -> p h d", d=HD)).then_inc(ld_late, 16)
            sp.dma_start(proj_brow[:], b_proj.unsqueeze(0)).then_inc(ld_late, 16)
            sp.dma_start(fc1_n[:], fc1_w.rearrange("(p c) d -> p c d", c=HC)).then_inc(ld_late, 16)
            sp.dma_start(fc1_bc[:], fc1_b.rearrange("(p c) -> p c", c=HC)).then_inc(ld_late, 16)
            sp.dma_start(fc2_n[:], fc2_w.rearrange("(k p) f -> p k f", k=NK)).then_inc(ld_late, 16)
            sp.dma_start(fc2_brow[:], fc2_b.unsqueeze(0)).then_inc(ld_late, 16)
            sp.dma_start(atom_brow[:], atom_out_b.unsqueeze(0)).then_inc(ld_atoms, 16)
            sp.dma_start(atom_bc[:], atom_in_b.rearrange("a (p c) -> p a c", c=HC)).then_inc(ld_atoms, 16)
            sp.wait_ge(w_placed, len(turns) + NK + 1)
            for a in range(ATOMS - 1):
                sp.dma_start(atom_in_n[a][:], atom_in_w[a].rearrange("(p c) d -> p c d", c=HC)).then_inc(ld_atoms, 16)
                sp.dma_start(atom_out_n[a][:], atom_out_w[a].rearrange("(k p) f -> p k f", k=NK)).then_inc(ld_atoms, 16)

            def stages(name, p, it):
                if name == "x" and not (isinstance(it, int) and it == PAIRS - 1):
                    sp.wait_ge(x_regrouped, 3 * it + 3)
                    sp.dma_start(xin[:], x_rows[bass.ds((it + 1) * XROWS, XROWS)]).then_inc(x_loaded, 16)
                if name == "route":
                    sp.wait_ge(expert_ready[p], it + 1)
                    sp.nop(nofuse=True)
                    e = sp.value_load(expert[p][0:1, 0:1], min_val=0, max_val=EXPERTS - 1)
                    sp.dma_start(w1_sb[p][:], w1[bass.ds(e, 1)].rearrange("o (k p) f -> (o p) k f", k=NK)
                                 ).then_inc(experts_loaded[p], 16)
                    sp.dma_start(w2_sb[p][:], w2[bass.ds(e, 1)].rearrange("o (p c) d -> (o p) c d", c=HC)
                                 ).then_inc(experts_loaded[p], 16)
                    sp.dma_start(b1_sb[p][:], b1[bass.ds(e, 1)].rearrange("o (p c) -> (o p) c", c=HC)
                                 ).then_inc(experts_loaded[p], 16)
                    sp.dma_start(b2_sb[p][:], b2[bass.ds(e, 1)]).then_inc(experts_loaded[p], 16)
                if name == "norm4":
                    sp.wait_ge(xn_ready[p], 4 * it + 4)
                    img = 2 * it + p
                    sp.dma_start(scratch[bass.ds(img, 1), 1:NCLS].rearrange("o n k d -> (o n) k d"),
                                 hx[p][0:NCLS - 1, :, 0, :]).then_inc(cls_stored[p], 16)
                    sp.dma_start(scratch[bass.ds(img, 1), 0:1].rearrange("o n k d -> (o n) k d"),
                                 hx[p][R - 1:R, :, 0, :]).then_inc(cls_stored[p], 16)
                if name == "out1_1":
                    sp.wait_ge(out_ready[p], it + 1)
                    img = 2 * it + p
                    sp.dma_start(out[bass.ds(img, 1), NCLS:R].rearrange("o s d -> (o s) d"),
                                 y[p][NCLS - 1:R - 1, 0, :]).then_inc(stored[p], 16)
                    sp.dma_start(out[bass.ds(img, 1), R:SEQ].rearrange("o s d -> (o s) d"),
                                 y[p][0:R - 1, 1, :]).then_inc(stored[p], 16)

            run_stages(sp, stages, peel_last=True)
            for p in range(2):
                sp.wait_ge(cls_stored[p], 32 * PAIRS + 32)
                sp.wait_ge(stored[p], 32 * PAIRS + 32)
            sp.wait_ge(cls_ready, 1)
            a = ATOMS - 1
            sp.dma_start(atom_in_n[a][:], atom_in_w[a].rearrange("(p c) d -> p c d", c=HC)).then_inc(ld_atoms, 16)
            sp.dma_start(atom_out_n[a][:], atom_out_w[a].rearrange("(k p) f -> p k f", k=NK)).then_inc(ld_atoms, 16)
            sp.dma_start(cls[:], scratch).then_inc(ld_cls, 16)
            sp.dma_start(gate[:], gate_pair.rearrange("n r d -> (n r) d").unsqueeze(0)
                         .broadcast_to([IMAGES, 2 * NCLS, D])).then_inc(ld_cls, 16)
            sp.dma_start(gbias[:], balance.rearrange("n r -> (n r)").unsqueeze(0)
                         .broadcast_to([IMAGES, 2 * NCLS])).then_inc(ld_cls, 16)
            sp.wait_ge(cls_ready, 2)
            sp.dma_start(out[:, 0:NCLS, :], cls[:, :, 0, :]).then_inc(cls_out_stored, 16)
            sp.wait_ge(cls_out_stored, 16)

        @block.gpsimd
        def _(pool):
            g = nc.gpsimd
            g.memset(ident[:], 0.0).then_inc(consts, 1)
            pool.wait_ge(consts, 1)
            g.affine_select(out=ident[:], in_=ident[:], compare_op=ALU.not_equal, fill=1.0, base=0,
                            pattern=[[-1, 128]], channel_multiplier=1).then_inc(consts, 1)
            g.memset(eps[:], EPS)
            g.memset(minus_half[:], -0.5).then_inc(consts, 1)
            pool.wait_ge(consts, 2)
            g.tensor_scalar(not_cls[:], ident[0:R, R - 1:R], -1.0, 1.0, ALU.mult, ALU.add).then_inc(consts, 1)
            pool.wait_ge(consts, 4)

            def regroup(it):
                pool.wait_ge(x_loaded, 16 * it + 16)
                if not isinstance(it, int) or it:
                    pool.wait_ge(x_turned, 6 * it)
                pool.nop(nofuse=True)
                for lo, hi in PX:
                    dst = xg[:, lo:hi, :].rearrange("p x (i j) -> p i x j", j=PS)
                    src = xin[:, :, lo * PS:hi * PS].rearrange("p i (x j) -> p i x j", j=PS)
                    g.tensor_copy(dst, src).then_inc(x_regrouped, 1)

            regroup(0)

            def stages(name, p, it):
                if name == "tok0" and p == 1 and not (isinstance(it, int) and it == PAIRS - 1):
                    regroup(it + 1)
                if name[:4] == "stat":
                    n = 4 * it + int(name[4])
                    pool.wait_ge(moments_ready[p], n)
                    g.tensor_tensor(var_eps[p][:], moments[p][:, :, 1], eps[0:R, 0:T], ALU.add).then_inc(eps_added[p], 1)
                    pool.wait_ge(eps_added[p], n)
                    g.tensor_tensor(rstd[p][:], var_eps[p][:], minus_half[0:R, 0:T], ALU.pow).then_inc(rstd_ready[p], 1)

            run_stages(pool, stages, peel_last=True)
            pool.wait_ge(cls_step, 4)
            g.tensor_tensor(norms[:], sumsq[:], half[:], ALU.pow).then_inc(cls_pool, 1)

        @block.tensor
        def _(pe):
            t_ = nc.tensor

            def turn(ins, dst, sem_):
                at = 0
                for a in ins:
                    n, m = a.shape[0], a.shape[1]
                    last = t_.transpose(dst[0:m, at:at + n], a, ident[0:n, 0:n])
                    at += n
                last.then_inc(sem_, 1)

            pe.wait_ge(consts, 4)
            pe.wait_ge(ld_tok, 16 * 7)
            for j, (ins, dst, f) in enumerate(turns):
                if j == TOKK // 2:
                    pe.wait_ge(ld_attn, 32)
                if j == ATTN_TURNS:
                    pe.wait_ge(ld_late, 16 * 9)
                if j >= 8:
                    pe.wait_ge(w_placed, j - 7)
                turn(ins, all_banks[j % 8], w_turned)
            pe.wait_ge(w_placed, len(turns))
            for m in range(NK):
                for k in range(NK):
                    last = t_.matmul(all_banks[m][0:KC, 0:D], qkT[:, 0, k, m * KC:(m + 1) * KC], qkT[:, 1, k, :],
                                     start=(k == 0), stop=(k == NK - 1))
                last.then_inc(w_turned, 1)
            pe.wait_ge(w_placed, len(turns) + NK + 1)

            def patches(p, t):
                for k in range(TOKK):
                    c, hh = k // 2, k % 2
                    at = (hh * XROWS + (p * CHANNELS + c) * GRID) * GRID + t * (R - 1)
                    yield xT[:, at:at + R], tok_wT[:, k, :]

            def accumulate(dst, pairs):
                pairs = list(pairs)
                for j, (a, b) in enumerate(pairs):
                    last = t_.matmul(dst, a, b, start=(j == 0), stop=(j == len(pairs) - 1))
                return last

            def turn_tokens(p, it, n, b):
                pe.wait_ge(xn_ready[p], 4 * it + n)
                for k in range(NK):
                    for t in range(T):
                        last = t_.transpose(b[0:KC, k * SP_ + t * R:k * SP_ + (t + 1) * R],
                                            hx[p][:, 1, t, k * KC:(k + 1) * KC], ident[0:R, 0:R])
                last.then_inc(xn_turned[p], 1)

            def values(p, it, b, w):
                for t in range(T):
                    last = accumulate(b[0:R, t * D:(t + 1) * D],
                                      [(xnT[p][:, k, t * R:(t + 1) * R], w[:, k, :]) for k in range(NK)])
                last.then_inc(v_done[p], 1)

            def hidden(p, j, w):
                for c in (2 * j, 2 * j + 1):
                    last = accumulate(bank[p][j][:, (c % 2) * SP_:(c % 2 + 1) * SP_],
                                      [(w(k, c), xnT[p][:, k, :]) for k in range(NK)])
                last.then_inc(hid_done[p], 1)

            def hid_out(p, it, n, t, w, brow):
                b = bank[p][3]
                for c in range(HC):
                    if t == 0 and c % 2 == 0:
                        pe.wait_ge(hid_ready[p], 6 * it + 3 * n + c // 2 + 1)
                    t_.matmul(b[0:R, t * D:(t + 1) * D], hidT[p][:, c, t * R:(t + 1) * R], w[:, c, :],
                              start=(c == 0), stop=False)
                last = t_.matmul(b[0:R, t * D:(t + 1) * D], ones[0:1, 0:R], brow[0:1, :], start=False, stop=True)
                if t == T - 1:
                    last.then_inc(y_done[p], 1)

            def stages(name, p, it):
                b = bank[p]
                if name == "x":
                    for u in range(6):
                        hh, q = divmod(u, 3)
                        if u >= 3:
                            pe.wait_ge(x_placed_v if u % 2 else x_placed_a, 3 * it + (u - 3) // 2 + 1)
                        if hh == 0:
                            pe.wait_ge(x_regrouped, 3 * it + q + 1)
                        for j, px in enumerate(range(*PX[q])):
                            src = xg[:, px, hh * 128:(hh + 1) * 128]
                            last = t_.transpose(bank[0][u % 3][:, j * XROWS:(j + 1) * XROWS], src,
                                                ident[0:XROWS, 0:XROWS])
                        last.then_inc(x_turned, 1)
                elif name in ("tok0", "tok1"):
                    if name == "tok0":
                        pe.wait_ge(x_placed_v, 3 * it + 3)
                        pe.wait_ge(x_placed_a, 3 * it + 3)
                    t = int(name[3])
                    last = accumulate(b[0][0:R, t * D:(t + 1) * D], patches(p, t))
                    if t == T - 1:
                        last.then_inc(tok_done[p], 1)
                elif name[:4] == "turn":
                    n = int(name[4])
                    turn_tokens(p, it, n, b[TURN_BANK[n]])
                elif name == "q0":
                    pe.wait_ge(xnT_ready[p], 4 * it + 1)
                    for m in range(NK):
                        last = accumulate(b[2][0:KC, m * SP_:(m + 1) * SP_],
                                          [(qk_fold[:, k, m * KC:(m + 1) * KC], xnT[p][:, k, :]) for k in range(NK)])
                    last.then_inc(g_done[p], 1)
                elif name == "v0":
                    values(p, it, b[3], attn_wv)
                elif name == "s0":
                    pe.wait_ge(g_ready[p], it + 1)
                    for t in range(T):
                        last = accumulate(b[0][0:R, t * SP_:(t + 1) * SP_],
                                          [(gT[p][:, k, t * R:(t + 1) * R], xnT[p][:, k, :]) for k in range(NK)])
                    last.then_inc(s0_done[p], 1)
                elif name == "p0":
                    pe.wait_ge(p0_ready[p], it + 1)
                    for kt in range(T):
                        for t in range(T):
                            last = t_.transpose(b[1][0:R, kt * SP_ + t * R:kt * SP_ + (t + 1) * R],
                                                probs0[p][:, t, kt * R:(kt + 1) * R], ident[0:R, 0:R])
                    last.then_inc(p0_turned[p], 1)
                elif name == "o0":
                    pe.wait_ge(p0T_ready[p], it + 1)
                    pe.wait_ge(v_ready[p], 2 * it + 1)
                    for t in range(T):
                        last = accumulate(b[2][0:R, t * D:(t + 1) * D],
                                          [(turned[p][:, kt, t * R:(t + 1) * R], vals[p][:, kt, 0:D])
                                           for kt in range(T)])
                    last.then_inc(o0_done[p], 1)
                elif name == "route":
                    pe.wait_ge(xsum_ready[p], it + 1)
                    accumulate(b[1][0:R, 0:EXPERTS],
                               [(xsum[p][:, k:k + 1].broadcast_to([KC, R]), wgT[:, k, :]) for k in range(NK)]
                               ).then_inc(logit_done[p], 1)
                elif name[:4] == "hid0":
                    if name == "hid0_0":
                        pe.wait_ge(experts_loaded[p], 64 * it + 64)
                    hidden(p, int(name[5]), lambda k, c: w1_sb[p][:, k, c::HC])
                elif name[:4] == "out0":
                    hid_out(p, it, 0, int(name[5]), w2_sb[p], b2_sb[p])
                elif name[:3] == "qk1":
                    pe.wait_ge(xnT_ready[p], 4 * it + 3)
                    j = int(name[4])
                    for m in (2 * j, 2 * j + 1):
                        last = accumulate(b[1 + j][:, (m % 2) * SP_:(m % 2 + 1) * SP_],
                                          [(qk_wT[:, k, m * 128:(m + 1) * 128], xnT[p][:, k, :])
                                           for k in range(NK)])
                    last.then_inc(qk_done[p], 1)
                elif name == "v1":
                    values(p, it, b[0], v_wT)
                elif name[0] == "max":
                    j = name[1]
                    if j == 0:
                        pe.wait_ge(hi_ready[p], GROUPS * it + GROUPS)
                        pe.wait_ge(rest_ready[p], GROUPS * it + GROUPS)
                        pe.wait_ge(v_ready[p], 2 * it + 2)
                    if j >= 2:
                        pe.wait_ge(nmax1_ready[p], 6 * it + j - 1)
                    for h in (2 * j, 2 * j + 1):
                        r, gr = (h % 4) * 32, h // 4
                        for t in range(T):
                            last = t_.matmul(b[h % 4][0:R, t * SP_:(t + 1) * SP_],
                                             rest[p][r:r + 32, gr, t * R:(t + 1) * R],
                                             hi[p][r:r + 32, GROUPS + gr, :], start=True, stop=True)
                    last.then_inc(s1_done[p], 1)
                elif name == "maxT":
                    pe.wait_ge(nmax1_ready[p], 6 * it + 6)
                    for t in range(T):
                        last = t_.transpose(b[0][:, t * R:(t + 1) * R], nmax1[p][:, t, :, :].rearrange("p s g -> p (s g)"),
                                            ident[0:R, 0:R])
                    last.then_inc(nmax_turned[p], 1)
                elif name[0] == "att":
                    s = name[1]
                    if s < HEADS:
                        if s == 0:
                            pe.wait_ge(nmaxT_ready[p], it + 1)
                        if s >= 2:
                            pe.wait_ge(p1_ready[p], HEADS * it + s - 1)
                        r, gr = (s % 4) * 32, s // 4
                        for kt in range(T):
                            last = accumulate(b[s % 2][0:R, kt * SP_:(kt + 1) * SP_],
                                              [(w[p][r:r + 32, GROUPS + gr, kt * R:(kt + 1) * R],
                                                rest[p][r:r + 32, gr, :]) for w in (hi, rest)]
                                              + [(select[r:r + 32, gr, :], nmaxT[p][r:r + 32, :])])
                        last.then_inc(st_done[p], 1)
                    if s % 4 == 1 and s > 4:
                        gr = s // 4 - 1
                        pe.wait_ge(p1_ready[p], HEADS * it + 4 * gr + 4)
                        if gr:
                            pe.wait_ge(heads_ready[p], GROUPS * it + gr)
                        for kt in range(T):
                            rows = R if kt == 0 else R - 1
                            for dst in (b[2], b[3]):
                                for h in range(4 * gr, 4 * gr + 4):
                                    r = (h % 4) * 32
                                    w = vals[p][0:rows, kt, h * HD:h * HD + 32] if dst is b[2] else ones32[0:rows, :]
                                    last = t_.matmul(dst[r:r + 32, 0:SP_], w, probs[p][0:rows, h % RING, kt, :],
                                                     start=(kt == 0), stop=(kt == T - 1))
                        last.then_inc(heads_done[p], 1)
                elif name == "proj":
                    pe.wait_ge(heads_ready[p], GROUPS * it + GROUPS)
                    for t in range(T):
                        last = accumulate(b[0][0:R, t * D:(t + 1) * D],
                                          [(headT[p][:, gr, t * R:(t + 1) * R], proj_wT[:, gr, :])
                                           for gr in range(GROUPS)] + [(ones[0:1, 0:R], proj_brow[0:1, :])])
                    last.then_inc(proj_done[p], 1)
                elif name[:4] == "hid1":
                    pe.wait_ge(xnT_ready[p], 4 * it + 4)
                    hidden(p, int(name[5]), lambda k, c: fc1_wT[:, k, c, :])
                elif name[:4] == "out1":
                    hid_out(p, it, 1, int(name[5]), fc2_wT, fc2_brow)

            run_stages(pe, stages)

            n = 0
            pe.wait_ge(ld_cls, 48)
            pe.wait_ge(ld_atoms, 16 * (2 + 2 * ATOMS))
            pe.wait_ge(cls_ready, 1)
            for ins, dst in cls_turns:
                if n >= 2:
                    pe.wait_ge(c_placed, n - 1)
                turn(ins, all_banks[n % 2], c_turned)
                n += 1
            for a in range(ATOMS):
                for ins, dst in atom_turns[a]:
                    pe.wait_ge(c_placed, n - 1)
                    turn(ins, all_banks[n % 2], c_turned)
                    n += 1
                pe.wait_ge(c_placed, n)
                w = clsT_v(0, a).shape[1] * IMAGES
                for c in range(HC):
                    u = a * HC + c
                    if u >= 2:
                        pe.wait_ge(a_gelu, u - 1)
                    dst = all_banks[2 + u % 2][:, 0:w].rearrange("p (n b) -> p n b", b=IMAGES)
                    accumulate(dst, [(atom_inT[a % 2][:, k, c, :], clsT_v(k, a)) for k in range(NK)]
                               ).then_inc(a_hid, 1)
            pe.wait_ge(a_gelu, ATOMS * HC)
            for c in range(NCLS):
                if c >= 2:
                    pe.wait_ge(combined, 2 * c - 2)
                for r in range(2):
                    src, col, dst = route(c, r)
                    last = accumulate(all_banks[4 + c % 2][0:IMAGES, r * D:(r + 1) * D],
                                      [(atom_hid[src][:, j, col, :], atom_outT[dst][:, j, :]) for j in range(HC)]
                                      + [(ones[0:1, 0:IMAGES], atom_brow[0:1, dst, :])])
                last.then_inc(cand_done, 1)

        @block.vector
        def _(dve):
            v = nc.vector
            v.memset(pos_b[:], 0.0)
            v.memset(row_add[:], 0.0)
            v.memset(proj_n[:], 0.0).then_inc(zeros, 1)
            v.memset(qk_wT[:], 0.0)
            v.memset(xT[:, 2 * XROWS * GRID:], 0.0)
            v.memset(ones[:], 1.0)
            v.memset(ones32[:], 1.0)
            for p in range(2):
                v.memset(probs[p][:, 0, :, SEQ:SP_], 0.0)
                last = v.memset(vals[p][:, :, D:D + 16], 0.0)
            last.then_inc(zeros, 1)
            for p in range(2):
                dve.sem_inc(cls_stored[p], 32)
                dve.sem_inc(stored[p], 32)
            dve.wait_ge(zeros, 2)
            dve.wait_ge(ld_tok, 16 * 7)
            dve.wait_ge(consts, 4)
            for gr in range(GROUPS):
                v.tensor_reduce(group_row[:, gr:gr + 1], ident[:, gr::32], AX, ALU.add)
            v.memset(nmax1[0][:], 0.0)
            v.memset(nmax1[1][:], 0.0).then_inc(zeros, 1)
            dve.wait_ge(zeros, 3)
            v.tensor_copy(select[:], group_row[:].unsqueeze(2).broadcast_to([128, GROUPS, R]))
            v.tensor_reduce(rest_factor[:], ident[:].rearrange("p (h r d) -> p h r d", d=HD, r=2)[:, :, 1, :],
                            mybir.AxisListType.XY, ALU.add, negate=True)
            for j, (ins, dst, f) in enumerate(turns):
                dve.wait_ge(w_turned, j + 1)
                m, n = ins[0].shape[1], width(ins)
                src = all_banks[j % 8][0:m, 0:n]
                if len(dst.shape) == 4:
                    src = src.rearrange("p (h d) -> p h d", d=HD).unsqueeze(2).broadcast_to([m, n // HD, 2, HD])
                if f is None:
                    v.tensor_copy(dst, src).then_inc(w_placed, 1)
                else:
                    v.tensor_scalar(dst, src, f, None, ALU.mult).then_inc(w_placed, 1)
            for m in range(NK):
                dve.wait_ge(w_turned, len(turns) + m + 1)
                v.tensor_scalar(qk_fold[:, m, :], all_banks[m][0:KC, 0:D], D ** -0.5, None,
                                ALU.mult).then_inc(w_placed, 1)
            v.tensor_tensor(pos_b[:], pos_b[:], row_add[:], ALU.add).then_inc(w_placed, 1)
            dve.wait_ge(w_placed, len(turns) + NK + 1)

            def token_moments(p, it, n):
                h = hx[p][:, 0, :, :]
                dve.wait_ge(h_ready[p], 4 * it + n)
                for t in range(T):
                    last = v.bn_stats(stats[p][:, t, :], h[:, t, :])
                last.then_inc(stats_ready[p], 1)
                dve.wait_ge(stats_ready[p], 4 * it + n)
                dve.nop(nofuse=True)
                for t in range(T):
                    last = v.bn_aggr(moments[p][:, t, :], stats[p][:, t, :])
                last.then_inc(moments_ready[p], 1)

            def apply_norm(p, it, n):
                h, xn = hx[p][:, 0, :, :], hx[p][:, 1, :, :]
                dve.wait_ge(rstd_ready[p], 4 * it + n)
                for t in range(T):
                    last = v.tensor_scalar(xn[:, t, :], h[:, t, :], moments[p][:, t, 0:1], rstd[p][:, t:t + 1],
                                           ALU.subtract, ALU.mult)
                last.then_inc(xn_ready[p], 1)

            def stages(name, p, it):
                b = bank[p]
                h = hx[p][:, 0, :, :].rearrange("p t d -> p (t d)")
                if name == "x":
                    for u in range(0, 6, 2):
                        dve.wait_ge(x_turned, 6 * it + u + 1)
                        dst, src = x_tile(u)
                        v.tensor_copy(dst, src).then_inc(x_placed_v, 1)
                elif name == "tok1":
                    dve.wait_ge(tok_done[p], it + 1)
                    if not (isinstance(it, int) and it == 0):
                        dve.wait_ge(out_ready[p], it)
                    dve.wait_ge(cls_stored[p], 32 * it + 32)
                    v.scalar_tensor_tensor(out=h, in0=b[0][0:R, 0:T * D], scalar=not_cls[:, 0:1],
                                           in1=pos_b[:].rearrange("p t d -> p (t d)"),
                                           op0=ALU.mult, op1=ALU.add).then_inc(h_ready[p], 1)
                elif name[:4] == "stat":
                    token_moments(p, it, int(name[4]))
                elif name[:4] == "norm":
                    apply_norm(p, it, int(name[4]))
                elif name[:4] == "turn":
                    n = int(name[4])
                    dve.wait_ge(xn_turned[p], 4 * it + n)
                    v.tensor_copy(xnT[p][:].rearrange("p k s -> p (k s)"),
                                  b[TURN_BANK[n]][0:KC, 0:NK * SP_]).then_inc(xnT_ready[p], 1)
                elif name == "s0":
                    dve.wait_ge(s0_done[p], it + 1)
                    v.tensor_reduce(nmax0[p][:], b[0][0:R, 0:T * SP_].rearrange("p (t s) -> p t s", s=SP_)[:, :, 0:SEQ],
                                    AX, ALU.max, negate=True).then_inc(nmax0_ready[p], 1)
                elif name == "p0":
                    dve.wait_ge(p0_turned[p], it + 1)
                    v.tensor_copy(turned[p].rearrange("p k s -> p (k s)"),
                                  b[1][0:R, 0:T * SP_]).then_inc(p0T_ready[p], 1)
                    v.reciprocal(inv0[p][:], sum0[p][:]).then_inc(inv0_ready[p], 1)
                elif name == "o0":
                    dve.wait_ge(o0_done[p], it + 1)
                    dve.wait_ge(inv0_ready[p], it + 1)
                    for t in range(T):
                        last = v.scalar_tensor_tensor(out=hx[p][:, 0, t, :], in0=b[2][0:R, t * D:(t + 1) * D],
                                                      scalar=inv0[p][:, t:t + 1], in1=hx[p][:, 0, t, :],
                                                      op0=ALU.mult, op1=ALU.add)
                    last.then_inc(h_ready[p], 1)
                elif name == "route":
                    dve.wait_ge(xnT_ready[p], 4 * it + 2)
                    v.tensor_reduce(xsum[p][:], xnT[p][:, :, 0:SEQ], AX, ALU.add).then_inc(xsum_ready[p], 1)
                    dve.wait_ge(logit_done[p], it + 1)
                    v.tensor_scalar(logit[p][:], b[1][0:R, 0:EXPERTS], 1.0 / SEQ, None, ALU.mult).then_inc(logit_ready[p], 1)
                    dve.wait_ge(logit_ready[p], it + 1)
                    v.tensor_reduce(nlmax[p][:], logit[p][:], AX, ALU.max, negate=True).then_inc(nlmax_ready[p], 1)
                    dve.wait_ge(nlmax_ready[p], it + 1)
                    v.tensor_scalar(below[p][:], logit[p][:, 0:2], nlmax[p][:, 0:1], 0.0, ALU.add,
                                    ALU.is_lt).then_inc(below_ready[p], 1)
                    dve.wait_ge(below_ready[p], it + 1)
                    v.scalar_tensor_tensor(out=expert[p][:], in0=below[p][0:1, 1:2], scalar=1.0,
                                           in1=below[p][0:1, 0:1], op0=ALU.add, op1=ALU.mult).then_inc(expert_ready[p], 1)
                    dve.wait_ge(lexp_ready[p], it + 1)
                    v.tensor_reduce(ltop[p][:], lexp[p][:], AX, ALU.max)
                    v.reciprocal(linv[p][:], lsum[p][:]).then_inc(lparts_ready[p], 1)
                    dve.wait_ge(lparts_ready[p], it + 1)
                    v.tensor_tensor(weight[p][:], ltop[p][:], linv[p][:], ALU.mult).then_inc(weight_ready[p], 1)
                elif name == "out0_1":
                    dve.wait_ge(y_done[p], 2 * it + 1)
                    dve.wait_ge(weight_ready[p], it + 1)
                    v.scalar_tensor_tensor(out=h, in0=b[3][0:R, 0:T * D], scalar=weight[p][:, 0:1], in1=h,
                                           op0=ALU.mult, op1=ALU.add).then_inc(h_ready[p], 1)
                elif name[:3] == "qk1":
                    j = int(name[4])
                    dve.wait_ge(hi_ready[p], GROUPS * it + j + 1)
                    for lo, end, f in {0: [(0, 2, rest_factor[:, 0:1])],
                                       1: [(2, 3, rest_factor[:, 0:1]), (3, 4, -1.0)],
                                       2: [(4, 6, -1.0)]}[j]:
                        last = v.scalar_tensor_tensor(
                            out=rest[p][:, lo:end, :].rearrange("p m s -> p (m s)"),
                            in0=hi[p][:, lo:end, :].bitcast(F32).rearrange("p m s -> p (m s)"), scalar=f,
                            in1=b[1 + j][:, (lo - 2 * j) * SP_:(end - 2 * j) * SP_], op0=ALU.mult, op1=ALU.add)
                    last.then_inc(rest_ready[p], 1)
                elif name[0] == "max":
                    j = name[1]
                    dve.wait_ge(s1_done[p], 6 * it + j + 1)
                    k = 2 * (j % 2)
                    src = banks[p][0:R, k:k + 2, 0:T * SP_].rearrange("p h (t s) -> p h t s", s=SP_)[:, :, :, 0:SEQ]
                    v.tensor_reduce(nmax1[p][:, :, k:k + 2, j // 2].rearrange("p t h -> p h t"), src, AX, ALU.max,
                                    negate=True).then_inc(nmax1_ready[p], 1)
                elif name == "maxT":
                    dve.wait_ge(nmax_turned[p], it + 1)
                    v.tensor_copy(nmaxT[p][:], b[0][:, 0:SP_]).then_inc(nmaxT_ready[p], 1)
                elif name[0] == "att" and name[1] % 4 == 1 and name[1] > 4:
                    gr = name[1] // 4 - 1
                    dve.wait_ge(heads_done[p], GROUPS * it + gr + 1)
                    v.reciprocal(inv1[p][:], b[3][:, 0:SP_]).then_inc(inv1_ready[p], 1)
                    dve.wait_ge(inv1_ready[p], GROUPS * it + gr + 1)
                    v.tensor_tensor(headT[p][:, gr, :], b[2][:, 0:SP_], inv1[p][:], ALU.mult).then_inc(heads_ready[p], 1)
                elif name == "proj":
                    dve.wait_ge(proj_done[p], it + 1)
                    v.tensor_tensor(h, b[0][0:R, 0:T * D], h, ALU.add).then_inc(h_ready[p], 1)
                elif name == "out1_1":
                    dve.wait_ge(y_done[p], 2 * it + 2)
                    dve.wait_ge(stored[p], 32 * it + 32)
                    v.tensor_tensor(y[p][:].rearrange("p t d -> p (t d)"), b[3][0:R, 0:T * D], h,
                                    ALU.add).then_inc(out_ready[p], 1)

            run_stages(dve, stages)

            for p in range(2):
                dve.wait_ge(out_ready[p], PAIRS)
                dve.wait_ge(stored[p], 32 * PAIRS + 32)
                dve.wait_ge(cls_stored[p], 32 * PAIRS + 32)
            v.memset(half[:], 0.5).then_inc(cls_ready, 1)
            for n, (ins, dst) in enumerate(cls_turns + [job for jobs in atom_turns for job in jobs]):
                dve.wait_ge(c_turned, n + 1)
                a, job = divmod(n - len(cls_turns), len(atom_turns[0]))
                if a >= 2 and job == 0:
                    dve.wait_ge(a_hid, (a - 1) * HC)
                v.tensor_copy(dst, all_banks[n % 2][0:ins[0].shape[1], 0:width(ins)]).then_inc(c_placed, 1)

            dve.wait_ge(ld_cls, 48)
            dve.wait_ge(cls_ready, 1)
            step = [0]

            def link(ins):
                step[0] += 1
                ins.then_inc(cls_step, 1)
                dve.wait_ge(cls_step, step[0])

            xc = cls[:, :, 1, :]
            pv = prod[:].rearrange("b (n r) d -> b n r d", r=2)
            gv = gate[:].rearrange("b (n r) d -> b n r d", r=2)
            sv = small[:].rearrange("b k (n r) -> b k n r", r=2)

            def over_routes(a):
                return a.unsqueeze(2).broadcast_to([IMAGES, NCLS, 2])

            link(v.tensor_tensor(prod[:, 0:NCLS, :], xc, xc, ALU.mult))
            link(v.tensor_reduce(sumsq[:, 0:NCLS], prod[:, 0:NCLS, :], AX, ALU.add))
            link(v.tensor_tensor(prod[:], gate[:], gate[:], ALU.mult))
            link(v.tensor_reduce(sumsq[:, NCLS:], prod[:], AX, ALU.add))
            assert step[0] == SUMS_STEP
            for r in range(2):
                last = v.tensor_tensor(pv[:, :, r, :], xc, gv[:, :, r, :], ALU.mult)
            link(last)
            link(v.tensor_reduce(dots[:].rearrange("b n r -> b (n r)"), prod[:], AX, ALU.add))
            dve.wait_ge(cls_pool, 1)
            link(v.tensor_scalar(norms[:], norms[:], 1e-12, None, ALU.max))
            link(v.reciprocal(sumsq[:], norms[:]))
            link(v.tensor_tensor(dots[:], dots[:], over_routes(sumsq[:, 0:NCLS]), ALU.mult))
            link(v.tensor_tensor(dots[:], dots[:], sumsq[:, NCLS:].rearrange("b (n r) -> b n r", r=2), ALU.mult))
            link(v.tensor_tensor(dots[:], dots[:], gbias[:].rearrange("b (n r) -> b n r", r=2), ALU.add))
            link(v.tensor_reduce(small[:, 0, 0:NCLS], dots[:], AX, ALU.max))
            link(v.tensor_tensor(sv[:, 1, :, :], dots[:], over_routes(small[:, 0, 0:NCLS]), ALU.subtract))
            assert step[0] == SHIFT_STEP
            dve.wait_ge(cls_exp, 1)
            link(v.tensor_reduce(small[:, 3, 0:NCLS], sv[:, 2, :, :], AX, ALU.add))
            link(v.reciprocal(small[:, 4, 0:NCLS], small[:, 3, 0:NCLS]))
            link(v.tensor_tensor(sv[:, 5, :, :], sv[:, 2, :, :], over_routes(small[:, 4, 0:NCLS]), ALU.mult))
            link(v.tensor_tensor(small[:, 6, 0:NCLS], dots[:, :, 0], dots[:, :, 1], ALU.is_ge))
            link(v.tensor_scalar(small[:, 7, 0:NCLS], small[:, 6, 0:NCLS], -1.0, 1.0, ALU.mult, ALU.add))
            link(v.tensor_tensor(coef[:, :, 0], sv[:, 5, :, 0], small[:, 6, 0:NCLS], ALU.mult))
            link(v.tensor_tensor(coef[:, :, 1], sv[:, 5, :, 1], small[:, 7, 0:NCLS], ALU.mult))
            for c in range(NCLS):
                dve.wait_ge(cand_done, c + 1)
                for r in range(2):
                    v.scalar_tensor_tensor(out=cls[:, c, 0, :], in0=all_banks[4 + c % 2][0:IMAGES, r * D:(r + 1) * D],
                                           scalar=coef[:, c, r:r + 1], in1=cls[:, c, 0, :],
                                           op0=ALU.mult, op1=ALU.add).then_inc(combined, 1)
                    dve.wait_ge(combined, 2 * c + r + 1)
            v.memset(half[:], 0.0).then_inc(cls_ready, 1)

        @block.scalar
        def _(act):
            s_ = nc.scalar

            def softmax_weights(dst, src, nmax, total):
                for t in range(T):
                    last = s_.activation(dst[:, t, 0:SEQ], src[0:R, t * SP_:t * SP_ + SEQ], ACT.Exp,
                                         bias=nmax[:, t:t + 1], scale=1.0, accum_out=total[:, t:t + 1])
                return last

            def stages(name, p, it):
                b = bank[p]
                if name == "x":
                    for u in range(1, 6, 2):
                        act.wait_ge(x_turned, 6 * it + u + 1)
                        dst, src = x_tile(u)
                        s_.activation(dst, src, ACT.Copy).then_inc(x_placed_a, 1)
                elif name == "q0":
                    act.wait_ge(g_done[p], it + 1)
                    s_.activation(gT[p][:].rearrange("p k s -> p (k s)"), b[2][0:KC, 0:NK * SP_],
                                  ACT.Copy).then_inc(g_ready[p], 1)
                elif name == "v0":
                    act.wait_ge(v_done[p], 2 * it + 1)
                    s_.activation(vals[p][:, :, 0:D], b[3][0:R, 0:T * D].rearrange("p (t d) -> p t d", t=T),
                                  ACT.Copy).then_inc(v_ready[p], 1)
                elif name == "s0":
                    act.wait_ge(nmax0_ready[p], it + 1)
                    softmax_weights(probs0[p], b[0], nmax0[p], sum0[p]).then_inc(p0_ready[p], 1)
                elif name == "route":
                    act.wait_ge(nlmax_ready[p], it + 1)
                    s_.activation(lexp[p][:], logit[p][:], ACT.Exp, bias=nlmax[p][:, 0:1], scale=1.0,
                                  accum_out=lsum[p][:]).then_inc(lexp_ready[p], 1)
                elif name[:3] == "hid":
                    layer, j = int(name[3]), int(name[5])
                    bias = fc1_bc if layer else b1_sb[p]
                    act.wait_ge(hid_done[p], 6 * it + 3 * layer + j + 1)
                    for c in (2 * j, 2 * j + 1):
                        last = s_.activation(hidT[p][:, c, :], b[j][:, (c % 2) * SP_:(c % 2 + 1) * SP_], ACT.Gelu,
                                             bias=bias[:, c:c + 1], scale=1.0)
                    last.then_inc(hid_ready[p], 1)
                elif name[:3] == "qk1":
                    j = int(name[4])
                    act.wait_ge(qk_done[p], GROUPS * it + j + 1)
                    s_.activation(hi[p][:, 2 * j:2 * j + 2, :].rearrange("p m s -> p (m s)"),
                                  b[1 + j][:, 0:2 * SP_], ACT.Copy).then_inc(hi_ready[p], 1)
                elif name == "v1":
                    act.wait_ge(v_done[p], 2 * it + 2)
                    s_.activation(vals[p][:, :, 0:D], b[0][0:R, 0:T * D].rearrange("p (t d) -> p t d", t=T),
                                  ACT.Copy).then_inc(v_ready[p], 1)
                elif name[0] == "att" and name[1] < HEADS:
                    s = name[1]
                    if s >= RING:
                        act.wait_ge(heads_done[p], GROUPS * it + (s - RING) // 4 + 1)
                    act.wait_ge(st_done[p], HEADS * it + s + 1)
                    s_.activation(probs[p][:, s % RING, :, :].rearrange("p k s -> p (k s)"),
                                  b[s % 2][0:R, 0:T * SP_], ACT.Exp).then_inc(p1_ready[p], 1)

            run_stages(act, stages)
            for u in range(ATOMS * HC):
                a, c = divmod(u, HC)
                act.wait_ge(a_hid, u + 1)
                n = atom_hid[a].shape[2]
                s_.activation(atom_hid[a][:, c, :, :], all_banks[2 + u % 2][:, 0:n * IMAGES]
                              .rearrange("p (n b) -> p n b", b=IMAGES), ACT.Gelu,
                              bias=atom_bc[:, a, c:c + 1], scale=1.0).then_inc(a_gelu, 1)
            act.wait_ge(cls_step, SHIFT_STEP)
            s_.activation(small[:, 2, :], small[:, 1, :], ACT.Exp).then_inc(cls_exp, 1)


_INS = ["x", "L0_tok_W", "L0_tok_b", "L0_tok_class_token", "L0_tok_pos_embed", "L0_attn_W", "L0_ffn_Wg",
        "L0_ffn_W1", "L0_ffn_b1", "L0_ffn_W2", "L0_ffn_b2", "L1_attn_w_qkv", "L1_attn_w_proj",
        "L1_attn_b_proj", "L1_ffn_fc1_w", "L1_ffn_fc1_b", "L1_ffn_fc2_w", "L1_ffn_fc2_b",
        "L1_ffn_gate_pair", "L1_ffn_atom_in_w", "L1_ffn_atom_in_b", "L1_ffn_atom_out_w",
        "L1_ffn_atom_out_b", "L1_ffn_balance_bias"]


def kernel(**inputs):
    import numpy as _np
    import concourse.bacc as _bacc
    from concourse import mybir as _mybir
    from concourse.bass_utils import run_bass_kernel_spmd as _run

    nc = _bacc.Bacc("TRN2", target_bir_lowering=False, num_devices=1)
    arrays, args = {}, []
    for name in _INS:
        a = _np.ascontiguousarray(inputs[name])
        arrays[f"in_{name}_dram"] = a
        args.append(nc.dram_tensor(f"in_{name}_dram", a.shape, _mybir.dt.from_np(a.dtype), kind="ExternalInput").ap())
    out = nc.dram_tensor("out_0_dram", (IMAGES, SEQ, D), _mybir.dt.float32, kind="ExternalOutput").ap()
    scratch = nc.dram_tensor("cls_scratch", (IMAGES, NCLS, 2, D), _mybir.dt.float32, kind="Internal").ap()
    vit_kernel(nc, *args, out, scratch)
    r = _run(nc, [arrays], core_ids=[0])
    return r.results[0]["out_0_dram"]
```

```python
from contextlib import ExitStack

import concourse.bass as bass
from concourse import mybir

F32 = mybir.dt.float32
F32R = mybir.dt.float32r
I32 = mybir.dt.int32
ALU = mybir.AluOpType
ACT = mybir.ActivationFunctionType
AX = mybir.AxisListType.X

IMAGES, CHANNELS, SIDE = 64, 3, 224
GRID = 14
PS = SIDE // GRID
D = 192
F = 768
SEQ = GRID * GRID + 1
R = 99
T = 2
SP_ = R * T
KC = 96
NK = D // KC
DD = 256
HC = F // 128
TOKK = CHANNELS * PS * PS // 128
HEADS, HD = 12, 16
GROUPS = HEADS // 4
EXPERTS = 3
NCLS, ATOMS = 6, 5
EPS = 1e-5
PAIRS = IMAGES // 2
XROWS = 2 * CHANNELS * GRID
PX = [(0, 5), (5, 10), (10, 14)]

RING = 6
REGROUPED = 2
REGROUPS = GRID // REGROUPED



def norm_stages(n):
    return [f"stat{n}", f"norm{n}", f"turn{n}"]


def ffn_stages(n):
    return [f"hid{n}_0", f"hid{n}_1", f"hid{n}_2", f"out{n}_0", f"out{n}_1"]


AHEAD = ["x", "tok0", "tok1"] + norm_stages(1)
STAGES = (["q0", "v0", "s0", "p0", "o0"] + norm_stages(2)
          + ["route", "x", "tok0", "tok1", "stat1", "split", "norm1", "hid0_0", "hid0_1", "turn1",
             "hid0_2", "out0_0", "out0_1"] + norm_stages(3) + ["qk1_0", "qk1_1", "qk1_2", "v1"]
          + [("max", j) for j in range(HEADS // 2)] + ["maxT"] + [("att", s) for s in range(HEADS + 2)]
          + ["proj"] + norm_stages(4) + ffn_stages(1))

B_FIRST = 38
MERGE = ("abababbbabbaaabbbbaababbababbbbaabbbbaaabaabrrabbraarbbbbaabbbraaaabbaabarababab"
         "aaabaababaaabaaaaababrbaabbabbabbaabababbab")


def merged_order():
    order = []
    first, second, parts = 0, B_FIRST, 0
    for which in MERGE:
        if which == "a":
            name, p, behind = STAGES[first], 0, 0
            first += 1
        elif which == "b":
            name, p, behind = STAGES[second % len(STAGES)], 1, int(second < len(STAGES))
            second += 1
        else:
            name, p, behind = ("regroup", parts), 0, 0
            parts += 1
        ahead = 2 if name[0] == "regroup" else int(name in AHEAD)
        if (name, p) != ("x", 1):
            order.append((name, p, behind, ahead - behind))
    assert (first, second - B_FIRST, parts) == (len(STAGES), len(STAGES), REGROUPS)
    return order


ORDER = merged_order()
TURN_BANK = {1: 3, 2: 3, 3: 0, 4: 1}
HIDDEN_BANK = [[1, 2, 0], [0, 1, 2]]


def vit_kernel(nc, x, tok_w, tok_b, cls_tok, pos, attn_w, wg, w1, b1, w2, b2, w_qkv, w_proj, b_proj,
               fc1_w, fc1_b, fc2_w, fc2_b, gate_pair, atom_in_w, atom_in_b, atom_out_w, atom_out_b,
               balance, out, scratch):
    with ExitStack() as ctx:
        def sb(name, shape, dt=F32, stack=ctx):
            return stack.enter_context(nc.sbuf_tensor(name, shape, dt))

        def sem(name):
            return ctx.enter_context(nc.semaphore(name))

        def both(name):
            return [sem(f"{name}_{p}") for p in range(2)]

        ident = sb("ident", [128, 128])
        ones = sb("ones", [2, 128])
        ones_pair = sb("ones_pair", [2, R], F32R)
        pair_factor = sb("pair_factor", [2, 1])
        not_cls = sb("not_cls", [R, 1])
        ones32 = sb("ones32", [R, 32])
        group_row = sb("group_row", [128, GROUPS])
        rest_factor = sb("rest_factor", [128, 1])
        upper_factor = sb("upper_factor", [128, 1])
        select = sb("select", [128, GROUPS, R], F32R)
        minus_half = sb("minus_half", [128, T])
        eps = sb("eps", [128, T])
        pos_b = sb("pos_b", [R, T, D])
        tok_wT = sb("tok_wT", [128, TOKK, D])
        qk_fold = sb("qk_fold", [128, 2, 2, DD], F32R)
        attn_wv = sb("attn_wv", [128, 2, 2, D], F32R)
        qk_wT = sb("qk_wT", [128, 2, 2, 2 * HEADS * 32], F32R)
        v_wT = sb("v_wT", [128, 2, 2, D], F32R)
        fc1_wT = sb("fc1_wT", [128, 2, 2, HC * 128], F32R)
        wgT = sb("wgT", [128, 2, EXPERTS])
        proj_wT = sb("proj_wT", [128, GROUPS, D])
        bias_pair = sb("bias_pair", [2, 2, D], F32R)
        fc1_bc = sb("fc1_bc", [128, HC])
        fc2_wT = sb("fc2_wT", [128, HC, D])
        atom_brow = sb("atom_brow", [1, ATOMS, D])
        atom_bc = sb("atom_bc", [128, ATOMS, HC])


        with ExitStack() as early:
            tok_n = sb("tok_n", [KC, NK, F], stack=early)
            attn_n = sb("attn_n", [KC, 2, NK, D], stack=early)
            attn_v = sb("attn_v", [128, 2, D], stack=early)
            qkT = sb("qkT", [KC, 2, NK, D], stack=early)
            qkv_n = sb("qkv_n", [KC, 6, D], stack=early)
            proj_n = sb("proj_n", [KC, NK, HEADS, 32], stack=early)
            fc1_n = sb("fc1_n", [128, HC, D], stack=early)
            fc2_n = sb("fc2_n", [KC, NK, F], stack=early)
            wg_n = sb("wg_n", [EXPERTS, D], stack=early)
            row_add = sb("row_add", [R, T, D], stack=early)
            bias_rows = sb("bias_rows", [2, 2, D], stack=early)
            bias_high = sb("bias_high", [2, 2, D], F32R, early)

        with ExitStack() as loop:
            def two(name, shape, dt=F32, stack=loop):
                return [sb(f"{name}{p}", shape, dt, stack) for p in range(2)]

            w1_sb = two("w1_sb", [128, 2, 2, F], F32R)
            w2_sb = two("w2_sb", [128, HC, D])
            xnT = two("xnT", [128, 2, 2, SP_], F32R)
            tokT = two("tokT", [128, 2, 2, SP_], F32R)
            xin = sb("xin", [XROWS, PS, SIDE], stack=loop)
            xg = sb("xg", [XROWS, GRID, PS * PS], stack=loop)
            xT = sb("xT", [128, 2 * XROWS * GRID + 4], stack=loop)
            hx = two("hx", [R, T * D + T * DD])
            h = [hx[p][:, 0:T * D] for p in range(2)]
            h_tok = two("h_tok", [R, T, D])
            h_tiles = [h[p].rearrange("p (t d) -> p t d", t=T) for p in range(2)]
            xn = [hx[p][:, T * D:].rearrange("p (t d) -> p t d", t=T) for p in range(2)]
            stats = two("stats", [R, T, 6])
            moments = two("moments", [R, T, 2])
            var_eps = two("var_eps", [R, T])
            rstd = two("rstd", [R, T])
            vals = two("vals", [R, T, D + 16])
            nmax0 = two("nmax0", [R, T])
            sum0 = two("sum0", [R, T])
            inv0 = two("inv0", [R, T])
            xsum = two("xsum", [128, 2])
            logit = two("logit", [R, EXPERTS])
            nlmax = two("nlmax", [R, 1])
            lexp = two("lexp", [R, EXPERTS])
            lsum = two("lsum", [R, 1])
            linv = two("linv", [R, 1])
            ltop = two("ltop", [R, 1])
            weight = two("weight", [R, 1])
            below = two("below", [R, 2])
            expert = two("expert", [1, 1], I32)
            b1_sb = two("b1_sb", [128, HC])
            b2_rows = two("b2_rows", [2, D])
            b2_high = two("b2_high", [2, D], F32R)
            b2_pair = two("b2_pair", [2, D], F32R)
            with ExitStack() as hid:
                hidT = two("hidT", [128, HC, SP_], stack=hid)
            hi = two("hi", [128, 2 * GROUPS, SP_], F32R)
            rest = two("rest", [128, 2 * GROUPS, SP_], F32R)
            nmax1 = two("nmax1", [R, T, 4, 32])
            nmaxT = two("nmaxT", [128, SP_], F32R)
            inv1 = two("inv1", [128, SP_])
            probs, w1_raw = [], []
            for p in range(2):
                first = sb(f"probs_first{p}", [R, 2, T, SP_], stack=loop)
                with ExitStack() as raw:
                    w1_raw.append(sb(f"w1_raw{p}", [128, 2, F], stack=raw))
                rest_of_ring = sb(f"probs_rest{p}", [R, RING - 2, T, SP_], stack=loop)
                probs.append((first, rest_of_ring))
            probs0 = [probs[p][0][:, 0, :, :] for p in range(2)]
            turned = [probs[p][0][:, 1, :, :] for p in range(2)]
            headT = two("headT", [128, GROUPS, SP_])
            y = two("y", [R, T, D])
        atom_in_n = [sb(f"atom_in_n{a}", [128, HC, D]) for a in range(ATOMS)]
        atom_out_n = [sb(f"atom_out_n{a}", [KC, NK, F]) for a in range(ATOMS)]

        def ring(p, s):
            first, others = probs[p]
            return first[:, s % RING, :, :] if s % RING < 2 else others[:, s % RING - 2, :, :]
        cls = sb("cls", [IMAGES, NCLS, 2, D])
        clsT = sb("clsT", [KC, NK, NCLS, IMAGES])
        gate = sb("gate", [IMAGES, 2 * NCLS, D])
        gbias = sb("gbias", [IMAGES, 2 * NCLS])
        prod = sb("prod", [IMAGES, 2 * NCLS, D])
        sumsq = sb("sumsq", [IMAGES, 3 * NCLS])
        norms = sb("norms", [IMAGES, 3 * NCLS])
        dots = sb("dots", [IMAGES, NCLS, 2])
        small = sb("small", [IMAGES, 8, 2 * NCLS])
        coef = sb("coef", [IMAGES, NCLS, 2])
        atom_inT = [sb(f"atom_inT{a}", [KC, NK, HC, 128]) for a in range(2)]
        atom_outT = [sb(f"atom_outT{a}", [128, HC, D]) for a in range(ATOMS)]
        atom_hid = [sb(f"atom_hid{a}", [128, HC, 2 if a < 3 else 3, IMAGES]) for a in range(ATOMS)]
        half = sb("half", [IMAGES, 3 * NCLS])

        banks = [ctx.enter_context(nc.psum_tensor(f"banks{p}", [128, 4, 512], F32)) for p in range(2)]
        bank = [[banks[p][:, k, :] for k in range(4)] for p in range(2)]
        all_banks = bank[0] + bank[1]

        ld_tok, ld_attn, ld_late, ld_cls = sem("ld_tok"), sem("ld_attn"), sem("ld_late"), sem("ld_cls")
        ld_atoms = sem("ld_atoms")
        consts, zeros = sem("consts"), sem("zeros")
        w_turned, w_high, w_placed = sem("w_turned"), sem("w_high"), sem("w_placed")
        x_loaded, x_regrouped, x_turned = sem("x_loaded"), sem("x_regrouped"), sem("x_turned")
        x_placed_v, x_placed_a = sem("x_placed_v"), sem("x_placed_a")
        tok_done, h_ready = both("tok_done"), both("h_ready")
        stats_ready, moments_ready = both("stats_ready"), both("moments_ready")
        eps_added, rstd_ready = both("eps_added"), both("rstd_ready")
        xn_ready, xn_turned, xnT_ready = both("xn_ready"), both("xn_turned"), both("xnT_ready")
        xn_high, g_high, w1_high, b2_rounded = both("xn_high"), both("g_high"), both("w1_high"), both("b2_rounded")
        g_done, g_ready, v_done, v_ready = both("g_done"), both("g_ready"), both("v_done"), both("v_ready")
        s0_done, nmax0_ready, p0_ready = both("s0_done"), both("nmax0_ready"), both("p0_ready")
        p0_turned, p0T_ready, inv0_ready, o0_done = (both("p0_turned"), both("p0T_ready"),
                                                     both("inv0_ready"), both("o0_done"))
        xsum_ready, logit_done, logit_ready = both("xsum_ready"), both("logit_done"), both("logit_ready")
        nlmax_ready, lexp_ready, below_ready = both("nlmax_ready"), both("lexp_ready"), both("below_ready")
        expert_ready, experts_loaded = both("expert_ready"), both("experts_loaded")
        w1_loaded, w1_ready = both("w1_loaded"), both("w1_ready")
        lparts_ready, weight_ready = both("lparts_ready"), both("weight_ready")
        hid_done, hid_ready, y_done = both("hid_done"), both("hid_ready"), both("y_done")
        qk_done, hi_ready, rest_ready = both("qk_done"), both("hi_ready"), both("rest_ready")
        s1_done, nmax1_ready = both("s1_done"), both("nmax1_ready")
        nmax_turned, nmaxT_ready = both("nmax_turned"), both("nmaxT_ready")
        st_done, p1_ready, inv1_ready = both("st_done"), both("p1_ready"), both("inv1_ready")
        heads_done, heads_ready, proj_done = both("heads_done"), both("heads_ready"), both("proj_done")
        out_ready = both("out_ready")
        cls_stored, stored = both("cls_stored"), both("stored")
        c_turned, c_placed, a_hid, a_gelu = sem("c_turned"), sem("c_placed"), sem("a_hid"), sem("a_gelu")
        cand_done, cls_step, cls_pool, cls_exp = (sem("cand_done"), sem("cls_step"), sem("cls_pool"),
                                                  sem("cls_exp"))
        cls_out_stored, cls_ready, combined = sem("cls_out_stored"), sem("cls_ready"), sem("combined")

        x_rows = x.rearrange("b c (y i) w -> (b c y) i w", i=PS)
        tok_v = tok_w.rearrange("(k p) d -> p k d", k=NK)

        def folded(src, width):
            jobs = []
            for c in range(0, HC, 2):
                jobs.append([src[:, k, cc::width] if width > 1 else src[:, k, cc * 128:(cc + 1) * 128]
                             for cc in (c, c + 1) for k in range(NK)])
            return jobs

        def feature_blocks(ws):
            return [[w[:, 0:128] for w in ws], [[w[:, 128:D], w[:, 128:D]] for w in ws]]

        turns = []
        for c, ins in zip(range(0, TOKK, 2), folded(tok_n, 1)):
            turns.append((ins, tok_wT[:, c:c + 2, :].rearrange("p a d -> p (a d)"), None, None))
        for w in range(2):
            for k in range(NK):
                turns.append(([attn_n[:, w, j, k * KC:(k + 1) * KC] for j in range(NK)], qkT[:, w, k, :], None, None))
        ATTN_TURNS = len(turns)
        for k, ins in enumerate(feature_blocks([wg_n])):
            turns.append((ins, wgT[:, k, :], None, None))
        for e in range(4):
            for k, ins in enumerate(feature_blocks([qkv_n[:, e, :]])):
                dst = [qk_wT[:, part, k, e * 6 * 32:(e + 1) * 6 * 32].rearrange("p (h r d) -> p h r d", d=HD, r=2)
                       for part in range(2)]
                turns.append((ins, dst[0], HD ** -0.5 if e < 2 else 1.0, dst[1]))
        for k, ins in enumerate(feature_blocks([qkv_n[:, e, :] for e in (4, 5)])):
            turns.append((ins, v_wT[:, 0, k, :], 1.0, v_wT[:, 1, k, :]))
        for g in range(GROUPS):
            turns.append(([proj_n[:, k, 4 * g:4 * g + 4, :].rearrange("p h d -> p (h d)") for k in range(NK)],
                          proj_wT[:, g, :], None, None))
        for c in range(0, HC, 3):
            for k, ins in enumerate(feature_blocks([fc1_n[:, c + j, :] for j in range(3)])):
                dst = [fc1_wT[:, part, k, c * 128:(c + 3) * 128] for part in range(2)]
                turns.append((ins, dst[0], 1.0, dst[1]))
        for c, ins in zip(range(0, HC, 2), folded(fc2_n, HC)):
            turns.append((ins, fc2_wT[:, c:c + 2, :].rearrange("p a d -> p (a d)"), None, None))

        def route(c, r):
            left, right = c // 2, 3 + c % 2
            return (left, c % 2, right) if r == 0 else (right, c // 2, left)

        def clsT_v(k, a):
            if a < 3:
                return clsT[:, k, 2 * a:2 * a + 2, :]
            return clsT[:, k, a - 3::2, :]

        cls_turns = [([cls[:, c, 1, k * KC:(k + 1) * KC] for c in range(NCLS)],
                      clsT[:, k, :, :].rearrange("p n b -> p (n b)")) for k in range(NK)]
        atom_turns = []
        for a in range(ATOMS):
            jobs = []
            for k in range(NK):
                for c in range(0, HC, 3):
                    jobs.append(([atom_in_n[a][:, c + j, k * KC:(k + 1) * KC] for j in range(3)],
                                 atom_inT[a % 2][:, k, c:c + 3, :].rearrange("p c f -> p (c f)")))
            for c, ins in zip(range(0, HC, 2), folded(atom_out_n[a], HC)):
                jobs.append((ins, atom_outT[a][:, c:c + 2, :].rearrange("p a d -> p (a d)")))
            atom_turns.append(jobs)
        SUMS_STEP, SHIFT_STEP = 4, 13

        def x_tile(u):
            hh, q = divmod(u, 3)
            lo, hi = PX[q]
            dst = xT[:, hh * XROWS * GRID:(hh + 1) * XROWS * GRID].rearrange("p (r x) -> p x r", x=GRID)
            return dst[:, lo:hi, :], bank[0][u % 3][:, 0:(hi - lo) * XROWS].rearrange("p (x r) -> p x r", r=XROWS)

        def rows_of(a):
            return sum(b.shape[1] for b in a) if isinstance(a, list) else a.shape[1]

        def width(aps):
            return sum((a[0] if isinstance(a, list) else a).shape[0] for a in aps)

        def placings(j):
            ins, dst, _, low = turns[j]
            src = all_banks[j % 8][0:rows_of(ins[0]), 0:width(ins)]
            if len(dst.shape) < 4:
                return [(src, dst, low)]
            src = src.rearrange("p (h d) -> p h d", d=HD)
            return [(src, dst[:, :, r, :], low[:, :, r, :]) for r in range(2)]

        def norm_count(n, it):
            if n == 1:
                return 1 if isinstance(it, int) and it == 0 else 4 * it - 1
            last = isinstance(it, int) and it == PAIRS - 1
            return 4 * it + {2: 2, 3: 4 - last, 4: 5 - last}[n]

        def run_stages(eng, stages):
            for name in AHEAD:
                stages(name, 0, 0)
            for name in AHEAD[1:]:
                stages(name, 1, 0)
            for k in range(REGROUPS):
                stages(("regroup", k), 0, 1)
            for name, p, behind, shift in ORDER:
                if not behind:
                    stages(name, p, shift)
            with eng.Fori(1, PAIRS - 2) as i:
                for name, p, _, shift in ORDER:
                    stages(name, p, i + shift if shift else i)
            for it in (PAIRS - 2, PAIRS - 1):
                for name, p, _, shift in ORDER:
                    if it + shift < PAIRS:
                        stages(name, p, it + shift)
            for name, p, behind, shift in ORDER:
                if behind and PAIRS + shift < PAIRS:
                    stages(name, p, PAIRS + shift)

        block = ctx.enter_context(nc.Block())

        @block.sync
        def _(sp):
            sp.dma_start(tok_n[:], tok_v).then_inc(ld_tok, 16)
            sp.dma_start(xin[:], x_rows[0:XROWS]).then_inc(x_loaded, 16)
            sp.dma_start(attn_n[:], attn_w[0:2].rearrange("w (k p) o -> p w k o", k=NK)).then_inc(ld_attn, 16)
            sp.dma_start(attn_v[:, 0, :], attn_w[2, 0:128]).then_inc(ld_attn, 16)
            for r in (0, 64):
                sp.dma_start(attn_v[r:r + 64, 1, :], attn_w[2, 128:D]).then_inc(ld_attn, 16)
            sp.wait_ge(zeros, 1)
            sp.dma_start(pos_b[0:R - 1, 0, :], pos[1:R, :]).then_inc(ld_tok, 16)
            sp.dma_start(pos_b[0:R - 1, 1, :], pos[R:SEQ, :]).then_inc(ld_tok, 16)
            sp.dma_start(pos_b[R - 1:R, 0, :], pos[0:1, :]).then_inc(ld_tok, 16)
            sp.dma_start(row_add[0:R - 1, 0, :], tok_b.unsqueeze(0).broadcast_to([R - 1, D])).then_inc(ld_tok, 16)
            sp.dma_start(row_add[0:R - 1, 1, :], tok_b.unsqueeze(0).broadcast_to([R - 1, D])).then_inc(ld_tok, 16)
            sp.dma_start(row_add[R - 1:R, 0, :], cls_tok).then_inc(ld_tok, 16)
            sp.dma_start(wg_n[:], wg).then_inc(ld_late, 16)
            sp.dma_start(qkv_n[:], w_qkv.rearrange("(e p) c -> p e c", e=6)).then_inc(ld_late, 16)
            for k in range(NK):
                sp.dma_start(proj_n[:, k, :, 0:HD],
                             w_proj[k * KC:(k + 1) * KC, :].rearrange("p (h d) -> p h d", d=HD)).then_inc(ld_late, 16)
            sp.dma_start(bias_rows[:, 0, :], b_proj.unsqueeze(0).broadcast_to([2, D])).then_inc(ld_late, 16)
            sp.dma_start(fc1_n[:], fc1_w.rearrange("(p c) d -> p c d", c=HC)).then_inc(ld_late, 16)
            sp.dma_start(fc1_bc[:], fc1_b.rearrange("(p c) -> p c", c=HC)).then_inc(ld_late, 16)
            sp.dma_start(fc2_n[:], fc2_w.rearrange("(k p) f -> p k f", k=NK)).then_inc(ld_late, 16)
            sp.dma_start(bias_rows[:, 1, :], fc2_b.unsqueeze(0).broadcast_to([2, D])).then_inc(ld_late, 16)
            sp.dma_start(atom_brow[:], atom_out_b.unsqueeze(0)).then_inc(ld_atoms, 16)
            sp.dma_start(atom_bc[:], atom_in_b.rearrange("a (p c) -> p a c", c=HC)).then_inc(ld_atoms, 16)

            def stages(name, p, it):
                if name == "x" and not (isinstance(it, int) and it == PAIRS - 1):
                    sp.wait_ge(x_regrouped, REGROUPS * (it + 1))
                    sp.dma_start(xin[:], x_rows[bass.ds((it + 1) * XROWS, XROWS)]).then_inc(x_loaded, 16)
                if name == "route":
                    sp.wait_ge(expert_ready[p], it + 1)
                    sp.nop(nofuse=True)
                    e = sp.value_load(expert[p][0:1, 0:1], min_val=0, max_val=EXPERTS - 1)
                    w = w1[bass.ds(e, 1)].rearrange("o p f -> (o p) f")
                    sp.dma_start(w1_raw[p][:, 0, :], w[0:128]).then_inc(w1_loaded[p], 16)
                    for r in (0, 64):
                        sp.dma_start(w1_raw[p][r:r + 64, 1, :], w[128:D]).then_inc(w1_loaded[p], 16)
                    sp.dma_start(b1_sb[p][:], b1[bass.ds(e, 1)].rearrange("o (p c) -> (o p) c", c=HC)
                                 ).then_inc(w1_loaded[p], 16)
                    for r in range(2):
                        sp.dma_start(b2_rows[p][r:r + 1, :], b2[bass.ds(e, 1)]).then_inc(w1_loaded[p], 16)
                    sp.dma_start(w2_sb[p][:], w2[bass.ds(e, 1)].rearrange("o (p c) d -> (o p) c d", c=HC)
                                 ).then_inc(experts_loaded[p], 16)
                if name == "norm4":
                    sp.wait_ge(xn_ready[p], norm_count(4, it))
                    img = 2 * it + p
                    first_tile = hx[p][:, 0:2 * T * D].rearrange("p (k c) -> p k c", k=2)[:, :, 0:D]
                    sp.dma_start(scratch[bass.ds(img, 1), 1:NCLS].rearrange("o n k d -> (o n) k d"),
                                 first_tile[0:NCLS - 1]).then_inc(cls_stored[p], 16)
                    sp.dma_start(scratch[bass.ds(img, 1), 0:1].rearrange("o n k d -> (o n) k d"),
                                 first_tile[R - 1:R]).then_inc(cls_stored[p], 16)
                if name == "out1_1":
                    sp.wait_ge(out_ready[p], it + 1)
                    img = 2 * it + p
                    sp.dma_start(out[bass.ds(img, 1), NCLS:R].rearrange("o s d -> (o s) d"),
                                 y[p][NCLS - 1:R - 1, 0, :]).then_inc(stored[p], 16)
                    sp.dma_start(out[bass.ds(img, 1), R:SEQ].rearrange("o s d -> (o s) d"),
                                 y[p][0:R - 1, 1, :]).then_inc(stored[p], 16)

            run_stages(sp, stages)
            for p in range(2):
                sp.wait_ge(cls_stored[p], 32 * PAIRS + 32)
                sp.wait_ge(stored[p], 32 * PAIRS + 32)
            sp.wait_ge(cls_ready, 1)
            sp.dma_start(cls[:], scratch).then_inc(ld_cls, 16)
            for a in range(ATOMS):
                sp.dma_start(atom_in_n[a][:], atom_in_w[a].rearrange("(p c) d -> p c d", c=HC)).then_inc(ld_atoms, 16)
                sp.dma_start(atom_out_n[a][:], atom_out_w[a].rearrange("(k p) f -> p k f", k=NK)).then_inc(ld_atoms, 16)
            sp.dma_start(gate[:], gate_pair.rearrange("n r d -> (n r) d").unsqueeze(0)
                         .broadcast_to([IMAGES, 2 * NCLS, D])).then_inc(ld_cls, 16)
            sp.dma_start(gbias[:], balance.rearrange("n r -> (n r)").unsqueeze(0)
                         .broadcast_to([IMAGES, 2 * NCLS])).then_inc(ld_cls, 16)
            sp.wait_ge(cls_ready, 2)
            sp.dma_start(out[:, 0:NCLS, :], cls[:, :, 0, :]).then_inc(cls_out_stored, 16)
            sp.wait_ge(cls_out_stored, 16)

        @block.gpsimd
        def _(pool):
            g = nc.gpsimd
            g.memset(ident[:], 0.0).then_inc(consts, 1)
            pool.wait_ge(consts, 1)
            g.affine_select(out=ident[:], in_=ident[:], compare_op=ALU.not_equal, fill=1.0, base=0,
                            pattern=[[-1, 128]], channel_multiplier=1).then_inc(consts, 1)
            g.memset(eps[:], EPS)
            g.memset(minus_half[:], -0.5).then_inc(consts, 1)
            pool.wait_ge(consts, 2)
            g.tensor_scalar(not_cls[:], ident[0:R, R - 1:R], -1.0, 1.0, ALU.mult, ALU.add).then_inc(consts, 1)
            pool.wait_ge(consts, 4)

            def regroup(it, k):
                if k == 0:
                    pool.wait_ge(x_loaded, 16 * it + 16)
                    if not isinstance(it, int) or it:
                        pool.wait_ge(x_turned, 6 * it)
                    pool.nop(nofuse=True)
                lo, hi = k * REGROUPED, (k + 1) * REGROUPED
                dst = xg[:, lo:hi, :].rearrange("p x (i j) -> p i x j", j=PS)
                src = xin[:, :, lo * PS:hi * PS].rearrange("p i (x j) -> p i x j", j=PS)
                g.tensor_copy(dst, src).then_inc(x_regrouped, 1)

            for k in range(REGROUPS):
                regroup(0, k)

            def stages(name, p, it):
                if name[0] == "regroup":
                    regroup(it, name[1])
                if name[:4] == "stat":
                    n = norm_count(int(name[4]), it)
                    pool.wait_ge(moments_ready[p], n)
                    g.tensor_tensor(var_eps[p][:], moments[p][:, :, 1], eps[0:R, 0:T], ALU.add).then_inc(eps_added[p], 1)
                    pool.wait_ge(eps_added[p], n)
                    g.tensor_tensor(rstd[p][:], var_eps[p][:], minus_half[0:R, 0:T], ALU.pow).then_inc(rstd_ready[p], 1)

            run_stages(pool, stages)
            pool.wait_ge(cls_step, 4)
            g.tensor_tensor(norms[:], sumsq[:], half[:], ALU.pow).then_inc(cls_pool, 1)

        @block.tensor
        def _(pe):
            t_ = nc.tensor

            def turn(ins, dst, sem_):
                at = 0
                for parts in ins:
                    row = 0
                    for a in parts if isinstance(parts, list) else [parts]:
                        n, m = a.shape[0], a.shape[1]
                        if row == 0:
                            last = t_.transpose(dst[row:row + m, at:at + n], a, ident[0:n, 0:n])
                        else:
                            last = t_.matmul(dst[row:row + m, at:at + n], a, ident[0:n, 0:n], start=True, stop=True)
                        row += m
                    at += n
                last.then_inc(sem_, 1)

            pe.wait_ge(consts, 4)
            pe.wait_ge(ld_tok, 16 * 7)
            for j, (ins, _, _, _) in enumerate(turns):
                if j == TOKK // 2:
                    pe.wait_ge(ld_attn, 16 * 4)
                if j == ATTN_TURNS:
                    pe.wait_ge(ld_late, 16 * 9)
                if j >= 8:
                    pe.wait_ge(w_placed, j - 7)
                turn(ins, all_banks[j % 8], w_turned)
            pe.wait_ge(w_placed, len(turns))
            for m, blocks in enumerate([[(0, 0, 128)], [(0, 128, D), (64, 128, D)]]):
                for row, lo, end in blocks:
                    for at, n, src in ((0, D, 0), (D, DD - D, 128)):
                        for k in range(NK):
                            last = t_.matmul(all_banks[m][row:row + end - lo, at:at + n], qkT[:, 0, k, lo:end],
                                             qkT[:, 1, k, src:src + n], start=(k == 0), stop=(k == NK - 1))
                last.then_inc(w_turned, 1)
            pe.wait_ge(w_placed, len(turns) + 2 + 3)

            def patches(p, t):
                for k in range(TOKK):
                    c, hh = k // 2, k % 2
                    at = (hh * XROWS + (p * CHANNELS + c) * GRID) * GRID + t * (R - 1)
                    yield xT[:, at:at + R], tok_wT[:, k, :]

            def accumulate(dst, pairs):
                pairs = list(pairs)
                for j, (a, b) in enumerate(pairs):
                    last = t_.matmul(dst, a, b, start=(j == 0), stop=(j == len(pairs) - 1))
                return last

            def products(x, w):
                return [(x(0, 0), w(0, 0)), (x(0, 0), w(1, 0)), (x(1, 0), w(0, 0)), (x(1, 1), w(0, 1)),
                        (x(1, 1), w(1, 1))]

            def tokens(p, t=None, xT=xnT):
                lo, end = (0, SP_) if t is None else (t * R, (t + 1) * R)
                return lambda part, k: xT[p][:, part, k, lo:end]

            def columns(w, cols=slice(None)):
                return lambda part, k: w[:, part, k, cols]

            def swapped(pairs):
                return [(b, a) for a, b in pairs]

            def turn_tokens(p, it, n, b):
                pe.wait_ge(xn_ready[p], norm_count(n, it))
                for t in range(T):
                    for k in range(2):
                        last = t_.transpose(b[:, k * SP_ + t * R:k * SP_ + (t + 1) * R],
                                            xn[p][:, t, k * 128:(k + 1) * 128], ident[0:R, 0:R])
                last.then_inc(xn_turned[p], 1)

            def values(p, it, b, w, xT):
                for t in range(T):
                    last = accumulate(b[0:R, t * D:(t + 1) * D], products(tokens(p, t, xT), columns(w)))
                last.then_inc(v_done[p], 1)

            def hidden(p, n, j, w, cols):
                for c in (2 * j, 2 * j + 1):
                    last = accumulate(bank[p][HIDDEN_BANK[n][j]][:, (c % 2) * SP_:(c % 2 + 1) * SP_],
                                      swapped(products(tokens(p), columns(w, cols(c)))))
                last.then_inc(hid_done[p], 1)

            def hid_out(p, it, n, t, w, pair):
                b = bank[p][3]
                for c in range(HC):
                    if t == 0 and c % 2 == 0:
                        pe.wait_ge(hid_ready[p], 6 * it + 3 * n + c // 2 + 1)
                    t_.matmul(b[0:R, t * D:(t + 1) * D], hidT[p][:, c, t * R:(t + 1) * R], w[:, c, :],
                              start=(c == 0), stop=False)
                last = t_.matmul(b[0:R, t * D:(t + 1) * D], ones_pair[:], pair, start=False, stop=True)
                if t == T - 1:
                    last.then_inc(y_done[p], 1)

            def stages(name, p, it):
                b = bank[p]
                if name == "x":
                    if not isinstance(it, int) or it:
                        pe.wait_ge(logit_ready[0], it)
                    for u in range(6):
                        hh, q = divmod(u, 3)
                        if u >= 3:
                            pe.wait_ge(x_placed_v if u % 2 else x_placed_a, 3 * it + (u - 3) // 2 + 1)
                        if hh == 0:
                            pe.wait_ge(x_regrouped, REGROUPS * it + (PX[q][1] + REGROUPED - 1) // REGROUPED)
                        for j, px in enumerate(range(*PX[q])):
                            src = xg[:, px, hh * 128:(hh + 1) * 128]
                            last = t_.transpose(bank[0][u % 3][:, j * XROWS:(j + 1) * XROWS], src,
                                                ident[0:XROWS, 0:XROWS])
                        last.then_inc(x_turned, 1)
                elif name in ("tok0", "tok1"):
                    if name == "tok0":
                        pe.wait_ge(x_placed_v, 3 * it + 3)
                        pe.wait_ge(x_placed_a, 3 * it + 3)
                    t = int(name[3])
                    last = accumulate(b[0][0:R, t * D:(t + 1) * D], patches(p, t))
                    if t == T - 1:
                        last.then_inc(tok_done[p], 1)
                elif name[:4] == "turn":
                    n = int(name[4])
                    turn_tokens(p, it, n, b[TURN_BANK[n]])
                elif name == "q0":
                    pe.wait_ge(xnT_ready[p], norm_count(1, it))
                    for m in range(2):
                        last = accumulate(b[2][:, m * SP_:(m + 1) * SP_], swapped(products(
                            tokens(p, None, tokT), columns(qk_fold, slice(m * 128, (m + 1) * 128)))))
                    last.then_inc(g_done[p], 1)
                elif name == "v0":
                    if not isinstance(it, int) or it:
                        pe.wait_ge(out_ready[p], it)
                    values(p, it, b[3], attn_wv, tokT)
                elif name == "s0":
                    pe.wait_ge(g_ready[p], it + 1)
                    for t in range(T):
                        last = accumulate(b[0][0:R, t * SP_:(t + 1) * SP_], swapped(products(
                            tokens(p, None, tokT), columns(xnT[p], slice(t * R, (t + 1) * R)))))
                    last.then_inc(s0_done[p], 1)
                elif name == "p0":
                    pe.wait_ge(p0_ready[p], it + 1)
                    for kt in range(T):
                        for t in range(T):
                            last = t_.transpose(b[1][0:R, kt * SP_ + t * R:kt * SP_ + (t + 1) * R],
                                                probs0[p][:, t, kt * R:(kt + 1) * R], ident[0:R, 0:R])
                    last.then_inc(p0_turned[p], 1)
                elif name == "o0":
                    pe.wait_ge(p0T_ready[p], it + 1)
                    pe.wait_ge(v_ready[p], 2 * it + 1)
                    for t in range(T):
                        last = accumulate(b[2][0:R, t * D:(t + 1) * D],
                                          [(turned[p][:, kt, t * R:(t + 1) * R], vals[p][:, kt, 0:D])
                                           for kt in range(T)])
                    last.then_inc(o0_done[p], 1)
                elif name == "route":
                    pe.wait_ge(xsum_ready[p], it + 1)
                    accumulate(b[1][0:R, 0:EXPERTS],
                               [(xsum[p][0:n, k:k + 1].broadcast_to([n, R]), wgT[0:n, k, :])
                                for k, n in enumerate((128, D - 128))]
                               ).then_inc(logit_done[p], 1)
                elif name[:4] == "hid0":
                    if name == "hid0_0":
                        pe.wait_ge(w1_ready[p], 2 * it + 2)
                    hidden(p, 0, int(name[5]), w1_sb[p], lambda c: slice(c, None, HC))
                elif name[:4] == "out0":
                    if name == "out0_0":
                        pe.wait_ge(experts_loaded[p], 16 * it + 16)
                        if not (isinstance(it, int) and it == PAIRS - 1):
                            pe.wait_ge(xnT_ready[p], norm_count(1, it + 1))
                    hid_out(p, it, 0, int(name[5]), w2_sb[p], b2_pair[p][:])
                elif name[:3] == "qk1":
                    pe.wait_ge(xnT_ready[p], norm_count(3, it))
                    j = int(name[4])
                    for m in (2 * j, 2 * j + 1):
                        last = accumulate(b[1 + j][:, (m % 2) * SP_:(m % 2 + 1) * SP_], swapped(products(
                            tokens(p), columns(qk_wT, slice(m * 128, (m + 1) * 128)))))
                    last.then_inc(qk_done[p], 1)
                elif name == "v1":
                    values(p, it, b[0], v_wT, xnT)
                elif name[0] == "max":
                    j = name[1]
                    if j == 0:
                        pe.wait_ge(hi_ready[p], GROUPS * it + GROUPS)
                        pe.wait_ge(rest_ready[p], GROUPS * it + GROUPS)
                        pe.wait_ge(v_ready[p], 2 * it + 2)
                    if j >= 2:
                        pe.wait_ge(nmax1_ready[p], 6 * it + j - 1)
                    for h in (2 * j, 2 * j + 1):
                        r, gr = (h % 4) * 32, h // 4
                        for t in range(T):
                            last = t_.matmul(b[h % 4][0:R, t * SP_:(t + 1) * SP_],
                                             rest[p][r:r + 32, gr, t * R:(t + 1) * R],
                                             hi[p][r:r + 32, GROUPS + gr, :], start=True, stop=True)
                    last.then_inc(s1_done[p], 1)
                elif name == "maxT":
                    pe.wait_ge(nmax1_ready[p], 6 * it + 6)
                    for t in range(T):
                        last = t_.transpose(b[0][:, t * R:(t + 1) * R], nmax1[p][:, t, :, :].rearrange("p s g -> p (s g)"),
                                            ident[0:R, 0:R])
                    last.then_inc(nmax_turned[p], 1)
                elif name[0] == "att":
                    s = name[1]
                    if s < HEADS:
                        if s == 0:
                            pe.wait_ge(nmaxT_ready[p], it + 1)
                        if s >= 2:
                            pe.wait_ge(p1_ready[p], HEADS * it + s - 1)
                        r, gr = (s % 4) * 32, s // 4
                        for kt in range(T):
                            last = accumulate(b[s % 2][0:R, kt * SP_:(kt + 1) * SP_],
                                              [(w[p][r:r + 32, GROUPS + gr, kt * R:(kt + 1) * R],
                                                rest[p][r:r + 32, gr, :]) for w in (hi, rest)]
                                              + [(select[r:r + 32, gr, :], nmaxT[p][r:r + 32, :])])
                        last.then_inc(st_done[p], 1)
                    if s % 4 == 1 and s > 4:
                        gr = s // 4 - 1
                        pe.wait_ge(p1_ready[p], HEADS * it + 4 * gr + 4)
                        if gr:
                            pe.wait_ge(heads_ready[p], GROUPS * it + gr)
                        for kt in range(T):
                            rows = R if kt == 0 else R - 1
                            for dst in (b[2], b[3]):
                                for h in range(4 * gr, 4 * gr + 4):
                                    r = (h % 4) * 32
                                    w = vals[p][0:rows, kt, h * HD:h * HD + 32] if dst is b[2] else ones32[0:rows, :]
                                    last = t_.matmul(dst[r:r + 32, 0:SP_], w, ring(p, h)[0:rows, kt, :],
                                                     start=(kt == 0), stop=(kt == T - 1))
                        last.then_inc(heads_done[p], 1)
                elif name == "proj":
                    pe.wait_ge(heads_ready[p], GROUPS * it + GROUPS)
                    for t in range(T):
                        last = accumulate(b[0][0:R, t * D:(t + 1) * D],
                                          [(headT[p][:, gr, t * R:(t + 1) * R], proj_wT[:, gr, :])
                                           for gr in range(GROUPS)] + [(ones_pair[:], bias_pair[:, 0, :])])
                    last.then_inc(proj_done[p], 1)
                elif name[:4] == "hid1":
                    pe.wait_ge(xnT_ready[p], norm_count(4, it))
                    hidden(p, 1, int(name[5]), fc1_wT, lambda c: slice(c * 128, (c + 1) * 128))
                elif name[:4] == "out1":
                    hid_out(p, it, 1, int(name[5]), fc2_wT, bias_pair[:, 1, :])

            run_stages(pe, stages)

            n = 0
            pe.wait_ge(ld_cls, 48)
            pe.wait_ge(ld_atoms, 16 * (2 + 2 * ATOMS))
            pe.wait_ge(cls_ready, 1)
            for ins, dst in cls_turns:
                if n >= 2:
                    pe.wait_ge(c_placed, n - 1)
                turn(ins, all_banks[n % 2], c_turned)
                n += 1
            for a in range(ATOMS):
                for ins, dst in atom_turns[a]:
                    pe.wait_ge(c_placed, n - 1)
                    turn(ins, all_banks[n % 2], c_turned)
                    n += 1
                pe.wait_ge(c_placed, n)
                w = clsT_v(0, a).shape[1] * IMAGES
                for c in range(HC):
                    u = a * HC + c
                    if u >= 2:
                        pe.wait_ge(a_gelu, u - 1)
                    dst = all_banks[2 + u % 2][:, 0:w].rearrange("p (n b) -> p n b", b=IMAGES)
                    accumulate(dst, [(atom_inT[a % 2][:, k, c, :], clsT_v(k, a)) for k in range(NK)]
                               ).then_inc(a_hid, 1)
            pe.wait_ge(a_gelu, ATOMS * HC)
            for c in range(NCLS):
                if c >= 2:
                    pe.wait_ge(combined, 2 * c - 2)
                for r in range(2):
                    src, col, dst = route(c, r)
                    last = accumulate(all_banks[4 + c % 2][0:IMAGES, r * D:(r + 1) * D],
                                      [(atom_hid[src][:, j, col, :], atom_outT[dst][:, j, :]) for j in range(HC)]
                                      + [(ones[0:1, 0:IMAGES], atom_brow[0:1, dst, :])])
                last.then_inc(cand_done, 1)

        @block.vector
        def _(dve):
            v = nc.vector
            v.memset(pos_b[:], 0.0)
            v.memset(row_add[:], 0.0)
            v.memset(proj_n[:], 0.0).then_inc(zeros, 1)
            v.memset(xT[:, 2 * XROWS * GRID:], 0.0)
            v.memset(ones[:], 1.0)
            v.memset(ones32[:], 1.0)
            for p in range(2):
                v.memset(probs0[p][:, :, SEQ:SP_], 0.0)
                last = v.memset(vals[p][:, :, D:D + 16], 0.0)
            last.then_inc(zeros, 1)
            for p in range(2):
                dve.sem_inc(cls_stored[p], 32)
                dve.sem_inc(stored[p], 32)
            dve.wait_ge(zeros, 2)
            dve.wait_ge(ld_tok, 16 * 7)
            dve.wait_ge(consts, 4)
            for gr in range(GROUPS):
                v.tensor_reduce(group_row[:, gr:gr + 1], ident[:, gr::32], AX, ALU.add)
            v.memset(nmax1[0][:], 0.0)
            v.memset(nmax1[1][:], 0.0).then_inc(zeros, 1)
            dve.wait_ge(zeros, 3)
            v.tensor_copy(select[:], group_row[:].unsqueeze(2).broadcast_to([128, GROUPS, R]))
            v.tensor_reduce(rest_factor[:], ident[:].rearrange("p (h r d) -> p h r d", d=HD, r=2)[:, :, 1, :],
                            mybir.AxisListType.XY, ALU.add, negate=True)
            v.tensor_reduce(upper_factor[:], ident[:, 64:128], AX, ALU.add, negate=True)
            v.tensor_copy(ones_pair[:], ones[:, 0:R])
            v.tensor_scalar(pair_factor[:], ident[0:2, 1:2], -1.0, None, ALU.mult).then_inc(zeros, 1)
            highs = 0
            for j, (_, dst, f, low) in enumerate(turns):
                if low is None:
                    dve.wait_ge(w_turned, j + 1)
                    v.tensor_copy(dst, placings(j)[0][0]).then_inc(w_placed, 1)
                else:
                    highs += 1
                    dve.wait_ge(w_high, highs)
                    for src, high, lo in placings(j):
                        last = v.scalar_tensor_tensor(out=lo, in0=src, scalar=f, in1=high.bitcast(F32),
                                                      op0=ALU.mult, op1=ALU.subtract)
                    last.then_inc(w_placed, 1)
            for m in range(2):
                dve.wait_ge(w_high, highs + m + 1)
                v.scalar_tensor_tensor(out=qk_fold[:, 1, m, :], in0=all_banks[m][:, 0:DD], scalar=D ** -0.5,
                                       in1=qk_fold[:, 0, m, :].bitcast(F32), op0=ALU.mult,
                                       op1=ALU.subtract).then_inc(w_placed, 1)
            dve.wait_ge(w_high, highs + 3)
            v.tensor_tensor(attn_wv[:, 1, :, :], attn_v[:], attn_wv[:, 0, :, :].bitcast(F32),
                            ALU.subtract).then_inc(w_placed, 1)
            dve.wait_ge(w_high, highs + 4)
            dve.wait_ge(zeros, 4)
            v.scalar_tensor_tensor(out=bias_pair[:], in0=bias_high[:].bitcast(F32), scalar=pair_factor[:, 0:1],
                                   in1=bias_rows[:], op0=ALU.mult, op1=ALU.add).then_inc(w_placed, 1)
            v.tensor_tensor(pos_b[:], pos_b[:], row_add[:], ALU.add).then_inc(w_placed, 1)
            dve.wait_ge(w_placed, len(turns) + 2 + 3)

            def token_moments(p, it, n):
                dve.wait_ge(h_ready[p], norm_count(n, it))
                for t in range(T):
                    last = v.bn_stats(stats[p][:, t, :], (h_tok[p] if n == 1 else h_tiles[p])[:, t, :])
                last.then_inc(stats_ready[p], 1)
                dve.wait_ge(stats_ready[p], norm_count(n, it))
                dve.nop(nofuse=True)
                for t in range(T):
                    last = v.bn_aggr(moments[p][:, t, :], stats[p][:, t, :])
                last.then_inc(moments_ready[p], 1)

            def apply_norm(p, it, n):
                dve.wait_ge(rstd_ready[p], norm_count(n, it))
                for t in range(T):
                    for at, lo in ((0, 0), (D, 128)):
                        last = v.tensor_scalar(xn[p][:, t, at:at + D - lo], (h_tok[p] if n == 1 else h_tiles[p])[:, t, lo:D],
                                               moments[p][:, t, 0:1], rstd[p][:, t:t + 1], ALU.subtract, ALU.mult)
                last.then_inc(xn_ready[p], 1)

            def stages(name, p, it):
                b = bank[p]
                if name == "x":
                    for u in range(0, 6, 2):
                        dve.wait_ge(x_turned, 6 * it + u + 1)
                        dst, src = x_tile(u)
                        v.tensor_copy(dst, src).then_inc(x_placed_v, 1)
                elif name == "tok1":
                    dve.wait_ge(tok_done[p], it + 1)
                    v.scalar_tensor_tensor(out=h_tok[p][:].rearrange("p t d -> p (t d)"), in0=b[0][0:R, 0:T * D], scalar=not_cls[:, 0:1],
                                           in1=pos_b[:].rearrange("p t d -> p (t d)"),
                                           op0=ALU.mult, op1=ALU.add).then_inc(h_ready[p], 1)
                elif name[:4] == "stat":
                    token_moments(p, it, int(name[4]))
                elif name[:4] == "norm":
                    apply_norm(p, it, int(name[4]))
                elif name[:4] == "turn":
                    n = int(name[4])
                    dst = (tokT if n == 1 else xnT)[p]
                    dve.wait_ge(xn_high[p], norm_count(n, it))
                    for k, f in enumerate((-1.0, upper_factor[:, 0:1])):
                        last = v.scalar_tensor_tensor(
                            out=dst[:, 1, k, :], in0=dst[:, 0, k, :].bitcast(F32), scalar=f,
                            in1=b[TURN_BANK[n]][:, k * SP_:(k + 1) * SP_], op0=ALU.mult, op1=ALU.add)
                    last.then_inc(xnT_ready[p], 1)
                elif name == "q0":
                    dve.wait_ge(g_high[p], it + 1)
                    v.scalar_tensor_tensor(
                        out=xnT[p][:, 1, :, :].rearrange("p k s -> p (k s)"),
                        in0=xnT[p][:, 0, :, :].bitcast(F32).rearrange("p k s -> p (k s)"), scalar=-1.0,
                        in1=b[2][:, 0:2 * SP_], op0=ALU.mult, op1=ALU.add).then_inc(g_ready[p], 1)
                elif name == "split":
                    dve.wait_ge(b2_rounded[p], it + 1)
                    v.scalar_tensor_tensor(out=b2_pair[p][:], in0=b2_high[p][:].bitcast(F32), scalar=pair_factor[:, 0:1],
                                           in1=b2_rows[p][:], op0=ALU.mult, op1=ALU.add)
                    for k in range(2):
                        dve.wait_ge(w1_high[p], 2 * it + k + 1)
                        v.tensor_tensor(w1_sb[p][:, 1, k, :], w1_raw[p][:, k, :],
                                        w1_sb[p][:, 0, k, :].bitcast(F32), ALU.subtract).then_inc(w1_ready[p], 1)
                elif name == "s0":
                    dve.wait_ge(s0_done[p], it + 1)
                    v.tensor_reduce(nmax0[p][:], b[0][0:R, 0:T * SP_].rearrange("p (t s) -> p t s", s=SP_)[:, :, 0:SEQ],
                                    AX, ALU.max, negate=True).then_inc(nmax0_ready[p], 1)
                elif name == "p0":
                    dve.wait_ge(p0_turned[p], it + 1)
                    v.tensor_copy(turned[p].rearrange("p k s -> p (k s)"),
                                  b[1][0:R, 0:T * SP_]).then_inc(p0T_ready[p], 1)
                    v.reciprocal(inv0[p][:], sum0[p][:]).then_inc(inv0_ready[p], 1)
                elif name == "o0":
                    dve.wait_ge(o0_done[p], it + 1)
                    dve.wait_ge(inv0_ready[p], it + 1)
                    if not (isinstance(it, int) and it == 0):
                        dve.wait_ge(out_ready[p], it)
                    dve.wait_ge(cls_stored[p], 32 * it + 32)
                    for t in range(T):
                        last = v.scalar_tensor_tensor(out=h_tiles[p][:, t, :], in0=b[2][0:R, t * D:(t + 1) * D],
                                                      scalar=inv0[p][:, t:t + 1], in1=h_tok[p][:, t, :],
                                                      op0=ALU.mult, op1=ALU.add)
                    last.then_inc(h_ready[p], 1)
                elif name == "route":
                    dve.wait_ge(xnT_ready[p], norm_count(2, it))
                    v.tensor_reduce(xsum[p][:], b[TURN_BANK[2]][:, 0:2 * SP_].rearrange("p (k s) -> p k s", k=2)
                                    [:, :, 0:SEQ], AX, ALU.add).then_inc(xsum_ready[p], 1)
                    dve.wait_ge(logit_done[p], it + 1)
                    v.tensor_scalar(logit[p][:], b[1][0:R, 0:EXPERTS], 1.0 / SEQ, None, ALU.mult).then_inc(logit_ready[p], 1)
                    dve.wait_ge(logit_ready[p], it + 1)
                    v.tensor_reduce(nlmax[p][:], logit[p][:], AX, ALU.max, negate=True).then_inc(nlmax_ready[p], 1)
                    dve.wait_ge(nlmax_ready[p], it + 1)
                    v.tensor_scalar(below[p][:], logit[p][:, 0:2], nlmax[p][:, 0:1], 0.0, ALU.add,
                                    ALU.is_lt).then_inc(below_ready[p], 1)
                    dve.wait_ge(below_ready[p], it + 1)
                    v.scalar_tensor_tensor(out=expert[p][:], in0=below[p][0:1, 1:2], scalar=1.0,
                                           in1=below[p][0:1, 0:1], op0=ALU.add, op1=ALU.mult).then_inc(expert_ready[p], 1)
                    dve.wait_ge(lexp_ready[p], it + 1)
                    v.tensor_reduce(ltop[p][:], lexp[p][:], AX, ALU.max)
                    v.reciprocal(linv[p][:], lsum[p][:]).then_inc(lparts_ready[p], 1)
                    dve.wait_ge(lparts_ready[p], it + 1)
                    v.tensor_tensor(weight[p][:], ltop[p][:], linv[p][:], ALU.mult).then_inc(weight_ready[p], 1)
                elif name == "out0_1":
                    dve.wait_ge(y_done[p], 2 * it + 1)
                    dve.wait_ge(weight_ready[p], it + 1)
                    v.scalar_tensor_tensor(out=h[p], in0=b[3][0:R, 0:T * D], scalar=weight[p][:, 0:1], in1=h[p],
                                           op0=ALU.mult, op1=ALU.add).then_inc(h_ready[p], 1)
                elif name[:3] == "qk1":
                    j = int(name[4])
                    dve.wait_ge(hi_ready[p], GROUPS * it + j + 1)
                    for lo, end, f in {0: [(0, 2, rest_factor[:, 0:1])],
                                       1: [(2, 3, rest_factor[:, 0:1]), (3, 4, -1.0)],
                                       2: [(4, 6, -1.0)]}[j]:
                        last = v.scalar_tensor_tensor(
                            out=rest[p][:, lo:end, :].rearrange("p m s -> p (m s)"),
                            in0=hi[p][:, lo:end, :].bitcast(F32).rearrange("p m s -> p (m s)"), scalar=f,
                            in1=b[1 + j][:, (lo - 2 * j) * SP_:(end - 2 * j) * SP_], op0=ALU.mult, op1=ALU.add)
                    last.then_inc(rest_ready[p], 1)
                elif name[0] == "max":
                    j = name[1]
                    dve.wait_ge(s1_done[p], 6 * it + j + 1)
                    k = 2 * (j % 2)
                    src = banks[p][0:R, k:k + 2, 0:T * SP_].rearrange("p h (t s) -> p h t s", s=SP_)[:, :, :, 0:SEQ]
                    v.tensor_reduce(nmax1[p][:, :, k:k + 2, j // 2].rearrange("p t h -> p h t"), src, AX, ALU.max,
                                    negate=True).then_inc(nmax1_ready[p], 1)
                elif name == "maxT":
                    dve.wait_ge(nmax_turned[p], it + 1)
                    v.tensor_copy(nmaxT[p][:], b[0][:, 0:SP_]).then_inc(nmaxT_ready[p], 1)
                elif name[0] == "att" and name[1] % 4 == 1 and name[1] > 4:
                    gr = name[1] // 4 - 1
                    dve.wait_ge(heads_done[p], GROUPS * it + gr + 1)
                    v.reciprocal(inv1[p][:], b[3][:, 0:SP_]).then_inc(inv1_ready[p], 1)
                    dve.wait_ge(inv1_ready[p], GROUPS * it + gr + 1)
                    v.tensor_tensor(headT[p][:, gr, :], b[2][:, 0:SP_], inv1[p][:], ALU.mult).then_inc(heads_ready[p], 1)
                elif name == "proj":
                    dve.wait_ge(proj_done[p], it + 1)
                    v.tensor_tensor(h[p], b[0][0:R, 0:T * D], h[p], ALU.add).then_inc(h_ready[p], 1)
                elif name == "out1_1":
                    dve.wait_ge(y_done[p], 2 * it + 2)
                    dve.wait_ge(stored[p], 32 * it + 32)
                    v.tensor_tensor(y[p][:].rearrange("p t d -> p (t d)"), b[3][0:R, 0:T * D], h[p],
                                    ALU.add).then_inc(out_ready[p], 1)

            run_stages(dve, stages)

            for p in range(2):
                dve.wait_ge(out_ready[p], PAIRS)
                dve.wait_ge(stored[p], 32 * PAIRS + 32)
                dve.wait_ge(cls_stored[p], 32 * PAIRS + 32)
            v.memset(half[:], 0.5).then_inc(cls_ready, 1)
            for n, (ins, dst) in enumerate(cls_turns + [job for jobs in atom_turns for job in jobs]):
                dve.wait_ge(c_turned, n + 1)
                a, job = divmod(n - len(cls_turns), len(atom_turns[0]))
                if a >= 2 and job == 0:
                    dve.wait_ge(a_hid, (a - 1) * HC)
                v.tensor_copy(dst, all_banks[n % 2][0:ins[0].shape[1], 0:width(ins)]).then_inc(c_placed, 1)

            dve.wait_ge(ld_cls, 48)
            dve.wait_ge(cls_ready, 1)
            step = [0]

            def link(ins):
                step[0] += 1
                ins.then_inc(cls_step, 1)
                dve.wait_ge(cls_step, step[0])

            xc = cls[:, :, 1, :]
            pv = prod[:].rearrange("b (n r) d -> b n r d", r=2)
            gv = gate[:].rearrange("b (n r) d -> b n r d", r=2)
            sv = small[:].rearrange("b k (n r) -> b k n r", r=2)

            def over_routes(a):
                return a.unsqueeze(2).broadcast_to([IMAGES, NCLS, 2])

            link(v.tensor_tensor(prod[:, 0:NCLS, :], xc, xc, ALU.mult))
            link(v.tensor_reduce(sumsq[:, 0:NCLS], prod[:, 0:NCLS, :], AX, ALU.add))
            link(v.tensor_tensor(prod[:], gate[:], gate[:], ALU.mult))
            link(v.tensor_reduce(sumsq[:, NCLS:], prod[:], AX, ALU.add))
            assert step[0] == SUMS_STEP
            for r in range(2):
                last = v.tensor_tensor(pv[:, :, r, :], xc, gv[:, :, r, :], ALU.mult)
            link(last)
            link(v.tensor_reduce(dots[:].rearrange("b n r -> b (n r)"), prod[:], AX, ALU.add))
            dve.wait_ge(cls_pool, 1)
            link(v.tensor_scalar(norms[:], norms[:], 1e-12, None, ALU.max))
            link(v.reciprocal(sumsq[:], norms[:]))
            link(v.tensor_tensor(dots[:], dots[:], over_routes(sumsq[:, 0:NCLS]), ALU.mult))
            link(v.tensor_tensor(dots[:], dots[:], sumsq[:, NCLS:].rearrange("b (n r) -> b n r", r=2), ALU.mult))
            link(v.tensor_tensor(dots[:], dots[:], gbias[:].rearrange("b (n r) -> b n r", r=2), ALU.add))
            link(v.tensor_reduce(small[:, 0, 0:NCLS], dots[:], AX, ALU.max))
            link(v.tensor_tensor(sv[:, 1, :, :], dots[:], over_routes(small[:, 0, 0:NCLS]), ALU.subtract))
            assert step[0] == SHIFT_STEP
            dve.wait_ge(cls_exp, 1)
            link(v.tensor_reduce(small[:, 3, 0:NCLS], sv[:, 2, :, :], AX, ALU.add))
            link(v.reciprocal(small[:, 4, 0:NCLS], small[:, 3, 0:NCLS]))
            link(v.tensor_tensor(sv[:, 5, :, :], sv[:, 2, :, :], over_routes(small[:, 4, 0:NCLS]), ALU.mult))
            link(v.tensor_tensor(small[:, 6, 0:NCLS], dots[:, :, 0], dots[:, :, 1], ALU.is_ge))
            link(v.tensor_scalar(small[:, 7, 0:NCLS], small[:, 6, 0:NCLS], -1.0, 1.0, ALU.mult, ALU.add))
            link(v.tensor_tensor(coef[:, :, 0], sv[:, 5, :, 0], small[:, 6, 0:NCLS], ALU.mult))
            link(v.tensor_tensor(coef[:, :, 1], sv[:, 5, :, 1], small[:, 7, 0:NCLS], ALU.mult))
            for c in range(NCLS):
                dve.wait_ge(cand_done, c + 1)
                for r in range(2):
                    v.scalar_tensor_tensor(out=cls[:, c, 0, :], in0=all_banks[4 + c % 2][0:IMAGES, r * D:(r + 1) * D],
                                           scalar=coef[:, c, r:r + 1], in1=cls[:, c, 0, :],
                                           op0=ALU.mult, op1=ALU.add).then_inc(combined, 1)
                    dve.wait_ge(combined, 2 * c + r + 1)
            v.memset(half[:], 0.0).then_inc(cls_ready, 1)

        @block.scalar
        def _(act):
            s_ = nc.scalar

            def softmax_weights(dst, src, nmax, total):
                for t in range(T):
                    last = s_.activation(dst[:, t, 0:SEQ], src[0:R, t * SP_:t * SP_ + SEQ], ACT.Exp,
                                         bias=nmax[:, t:t + 1], scale=1.0, accum_out=total[:, t:t + 1])
                return last

            for j, (_, dst, f, low) in enumerate(turns):
                if low is not None:
                    act.wait_ge(w_turned, j + 1)
                    for src, high, _ in placings(j):
                        last = s_.activation(high, src, ACT.Copy, scale=f)
                    last.then_inc(w_high, 1)
            for m in range(2):
                act.wait_ge(w_turned, len(turns) + m + 1)
                s_.activation(qk_fold[:, 0, m, :], all_banks[m][:, 0:DD], ACT.Copy, scale=D ** -0.5).then_inc(w_high, 1)
            act.wait_ge(ld_attn, 16 * 4)
            s_.activation(attn_wv[:, 0, :, :], attn_v[:], ACT.Copy).then_inc(w_high, 1)
            act.wait_ge(ld_late, 16 * 9)
            s_.activation(bias_high[:], bias_rows[:], ACT.Copy).then_inc(w_high, 1)

            def stages(name, p, it):
                b = bank[p]
                if name == "x":
                    for u in range(1, 6, 2):
                        act.wait_ge(x_turned, 6 * it + u + 1)
                        dst, src = x_tile(u)
                        s_.activation(dst, src, ACT.Copy).then_inc(x_placed_a, 1)
                elif name == "q0":
                    act.wait_ge(g_done[p], it + 1)
                    s_.activation(xnT[p][:, 0, :, :].rearrange("p k s -> p (k s)"), b[2][:, 0:2 * SP_],
                                  ACT.Copy).then_inc(g_high[p], 1)
                elif name[:4] == "turn":
                    n = int(name[4])
                    act.wait_ge(xn_turned[p], norm_count(n, it))
                    dst = (tokT if n == 1 else xnT)[p]
                    s_.activation(dst[:, 0, :, :].rearrange("p k s -> p (k s)"),
                                  b[TURN_BANK[n]][:, 0:2 * SP_], ACT.Copy).then_inc(xn_high[p], 1)
                elif name == "split":
                    act.wait_ge(w1_loaded[p], 96 * it + 96)
                    s_.activation(b2_high[p][:], b2_rows[p][:], ACT.Copy).then_inc(b2_rounded[p], 1)
                    for k in range(2):
                        s_.activation(w1_sb[p][:, 0, k, :], w1_raw[p][:, k, :], ACT.Copy).then_inc(w1_high[p], 1)
                elif name == "v0":
                    act.wait_ge(v_done[p], 2 * it + 1)
                    s_.activation(vals[p][:, :, 0:D], b[3][0:R, 0:T * D].rearrange("p (t d) -> p t d", t=T),
                                  ACT.Copy).then_inc(v_ready[p], 1)
                elif name == "s0":
                    act.wait_ge(nmax0_ready[p], it + 1)
                    softmax_weights(probs0[p], b[0], nmax0[p], sum0[p]).then_inc(p0_ready[p], 1)
                elif name == "route":
                    act.wait_ge(nlmax_ready[p], it + 1)
                    s_.activation(lexp[p][:], logit[p][:], ACT.Exp, bias=nlmax[p][:, 0:1], scale=1.0,
                                  accum_out=lsum[p][:]).then_inc(lexp_ready[p], 1)
                elif name[:3] == "hid":
                    layer, j = int(name[3]), int(name[5])
                    bias = fc1_bc if layer else b1_sb[p]
                    act.wait_ge(hid_done[p], 6 * it + 3 * layer + j + 1)
                    for c in (2 * j, 2 * j + 1):
                        last = s_.activation(hidT[p][:, c, :], b[HIDDEN_BANK[layer][j]][:, (c % 2) * SP_:(c % 2 + 1) * SP_], ACT.Gelu,
                                             bias=bias[:, c:c + 1], scale=1.0)
                    last.then_inc(hid_ready[p], 1)
                elif name[:3] == "qk1":
                    j = int(name[4])
                    act.wait_ge(qk_done[p], GROUPS * it + j + 1)
                    s_.activation(hi[p][:, 2 * j:2 * j + 2, :].rearrange("p m s -> p (m s)"),
                                  b[1 + j][:, 0:2 * SP_], ACT.Copy).then_inc(hi_ready[p], 1)
                elif name == "v1":
                    act.wait_ge(v_done[p], 2 * it + 2)
                    s_.activation(vals[p][:, :, 0:D], b[0][0:R, 0:T * D].rearrange("p (t d) -> p t d", t=T),
                                  ACT.Copy).then_inc(v_ready[p], 1)
                elif name[0] == "att" and name[1] < HEADS:
                    s = name[1]
                    if s >= RING:
                        act.wait_ge(heads_done[p], GROUPS * it + (s - RING) // 4 + 1)
                    act.wait_ge(st_done[p], HEADS * it + s + 1)
                    s_.activation(ring(p, s).rearrange("p k s -> p (k s)"),
                                  b[s % 2][0:R, 0:T * SP_], ACT.Exp).then_inc(p1_ready[p], 1)

            run_stages(act, stages)
            for u in range(ATOMS * HC):
                a, c = divmod(u, HC)
                act.wait_ge(a_hid, u + 1)
                n = atom_hid[a].shape[2]
                s_.activation(atom_hid[a][:, c, :, :], all_banks[2 + u % 2][:, 0:n * IMAGES]
                              .rearrange("p (n b) -> p n b", b=IMAGES), ACT.Gelu,
                              bias=atom_bc[:, a, c:c + 1], scale=1.0).then_inc(a_gelu, 1)
            act.wait_ge(cls_step, SHIFT_STEP)
            s_.activation(small[:, 2, :], small[:, 1, :], ACT.Exp).then_inc(cls_exp, 1)


_INS = ["x", "L0_tok_W", "L0_tok_b", "L0_tok_class_token", "L0_tok_pos_embed", "L0_attn_W", "L0_ffn_Wg",
        "L0_ffn_W1", "L0_ffn_b1", "L0_ffn_W2", "L0_ffn_b2", "L1_attn_w_qkv", "L1_attn_w_proj",
        "L1_attn_b_proj", "L1_ffn_fc1_w", "L1_ffn_fc1_b", "L1_ffn_fc2_w", "L1_ffn_fc2_b",
        "L1_ffn_gate_pair", "L1_ffn_atom_in_w", "L1_ffn_atom_in_b", "L1_ffn_atom_out_w",
        "L1_ffn_atom_out_b", "L1_ffn_balance_bias"]


def kernel(**inputs):
    import numpy as _np
    import concourse.bacc as _bacc
    from concourse import mybir as _mybir
    from concourse.bass_utils import run_bass_kernel_spmd as _run

    nc = _bacc.Bacc("TRN2", target_bir_lowering=False, num_devices=1)
    arrays, args = {}, []
    for name in _INS:
        a = _np.ascontiguousarray(inputs[name])
        arrays[f"in_{name}_dram"] = a
        args.append(nc.dram_tensor(f"in_{name}_dram", a.shape, _mybir.dt.from_np(a.dtype), kind="ExternalInput").ap())
    out = nc.dram_tensor("out_0_dram", (IMAGES, SEQ, D), _mybir.dt.float32, kind="ExternalOutput").ap()
    scratch = nc.dram_tensor("cls_scratch", (IMAGES, NCLS, 2, D), _mybir.dt.float32, kind="Internal").ap()
    vit_kernel(nc, *args, out, scratch)
    r = _run(nc, [arrays], core_ids=[0])
    return r.results[0]["out_0_dram"]
```
